# Optimizing a Trainium2 kernel written in Bass

```python
import numpy as np
import jax
import jax.numpy as jnp

def _softmax(x, axis=-1):
    return jax.nn.softmax(x, axis=axis)

def _gelu(x):
    return jax.nn.gelu(x, approximate=True)

def _silu(x):
    return jax.nn.silu(x)

def _sigmoid(x):
    return jax.nn.sigmoid(x)

def _layernorm(x, axis=-1, eps=1e-05):
    m = jnp.mean(x, axis=axis, keepdims=True)
    v = jnp.var(x, axis=axis, keepdims=True)
    return (x - m) / jnp.sqrt(v + eps)

def _scatter_add(tgt, idx, src, axis=0):
    return tgt.at[idx].add(src)

def _segment_sum(src, seg, n):
    return jax.ops.segment_sum(src, seg, n)
kernel_name = 'mk_perceiver_d4_seqx_r8_d02030'

def setup_inputs(seed: int=0):
    np.random.seed(seed)
    _w = jnp.asarray

    def _rec_inputs():
        import jax
        import jax.numpy as jnp
        _rk = jax.random.key(seed)
        x = -0.0002928 + 1 * jax.random.normal(jax.random.fold_in(_rk, 1), (128, 32, 128), jnp.float32)
        _lenS = 32 - jax.random.randint(jax.random.fold_in(_rk, 7), (128,), 0, max(1, 32 // 4) + 1, jnp.int32)
        _lenS2 = 257 - jax.random.randint(jax.random.fold_in(_rk, 8), (128,), 0, max(1, 257 // 4) + 1, jnp.int32)
        _ctx_1024P = jax.random.normal(jax.random.fold_in(_rk, 11), (128, 16, 128), jnp.float32)
        _ctx_1024c = jax.random.dirichlet(jax.random.fold_in(_rk, 511), 0.3 * jnp.ones((16,), jnp.float32), (128, 257))
        _ctx_1024t = jnp.einsum('bsk,bkd->bsd', _ctx_1024c, _ctx_1024P)
        _ctx_1024t = _ctx_1024t * jax.lax.rsqrt(jnp.mean(jnp.square(_ctx_1024t)) + 1e-12) * 0.953939
        ctx_1024 = -1.39393e-06 + 0.999914 * (_ctx_1024t + 0.3 * jax.random.normal(jax.random.fold_in(_rk, 611), (128, 257, 128), jnp.float32))
        fside_BxS2_0 = jax.random.uniform(jax.random.fold_in(_rk, 13), (128, 257), jnp.float32, 0.0, 0.999833)
        itok_BxS2_0_99 = jax.random.randint(jax.random.fold_in(_rk, 14), (128, 257), 0, 100, jnp.int32)
        _validS = jnp.arange(32)[None, :] < _lenS[:, None]
        _validS2 = jnp.arange(257)[None, :] < _lenS2[:, None]
        _causal = jnp.tril(jnp.ones((32, 32), dtype=bool))
        mask_1x1xSxS2_fk1 = jnp.where(jnp.broadcast_to(_validS2[0:1, None, None, :], (1, 1, 32, 257)), 1.0, 0.0).astype(jnp.float32)
        return (x, ctx_1024, fside_BxS2_0, itok_BxS2_0_99, mask_1x1xSxS2_fk1)
    x, ctx_1024, fside_BxS2_0, itok_BxS2_0_99, mask_1x1xSxS2_fk1 = _rec_inputs()

    def _L0_xattn_setup():
        import jax, jax.numpy as jnp
        import numpy as np
        import math
        D_MODEL = 128
        N_HEADS = 16
        key = jax.random.key(seed)
        ks = jax.random.split(key, 11)
        N, L, S = (2, 256, 256)
        d = D_MODEL
        s = 1.0 / math.sqrt(d)
        return {'queries': jax.random.normal(ks[0], (N, L, d), dtype=jnp.float32), 'keys': jax.random.normal(ks[1], (N, S, d), dtype=jnp.float32), 'values': jax.random.normal(ks[2], (N, S, d), dtype=jnp.float32), 'Wq': jax.random.normal(ks[3], (d, d), dtype=jnp.float32) * s, 'bq': jax.random.normal(ks[4], (d,), dtype=jnp.float32) * s, 'Wk': jax.random.normal(ks[5], (d, d), dtype=jnp.float32) * s, 'bk': jax.random.normal(ks[6], (d,), dtype=jnp.float32) * s, 'Wv': jax.random.normal(ks[7], (d, d), dtype=jnp.float32) * s, 'bv': jax.random.normal(ks[8], (d,), dtype=jnp.float32) * s, 'Wo': jax.random.normal(ks[9], (d, d), dtype=jnp.float32) * s, 'bo': jax.random.normal(ks[10], (d,), dtype=jnp.float32) * s}
    _L0_xattn_all = _L0_xattn_setup()
    _L0_xattn_in = {k: v for k, v in _L0_xattn_all.items() if k in ('Wq', 'bq', 'Wk', 'bk', 'Wv', 'bv', 'Wo', 'bo')}
    del _L0_xattn_all

    def _L0_attn_setup():
        import jax, jax.numpy as jnp
        import numpy as np
        N_EMBD = 128
        B, T = (8, 256)

        def _wkv_scan(time_decay, time_first, k, v):
            Bn, Tn, Cn = k.shape
            kT = jnp.swapaxes(k, 0, 1)
            vT = jnp.swapaxes(v, 0, 1)
            aa0 = jnp.zeros((Bn, Cn), k.dtype)
            bb0 = jnp.zeros((Bn, Cn), k.dtype)
            pp0 = jnp.full((Bn, Cn), -10000.0, k.dtype)

            def step(carry, kv):
                aa, bb, pp = carry
                kt, vt = kv
                ww = time_first + pp
                p = jnp.maximum(pp, ww)
                e1 = jnp.exp(pp - p)
                e2 = jnp.exp(ww - p)
                wkv_t = (e1 * aa + e2 * vt) / (e1 * bb + e2 + 1e-06)
                ww2 = time_decay + pp
                p2 = jnp.maximum(pp, ww2)
                e1b = jnp.exp(pp - p2)
                e2b = jnp.exp(ww2 - p2)
                aa = e1b * aa + e2b * vt
                bb = e1b * bb + e2b
                return ((aa, bb, p2), wkv_t)
            _, wkvT = jax.lax.scan(step, (aa0, bb0, pp0), (kT, vT))
            return jnp.swapaxes(wkvT, 0, 1)
        key = jax.random.key(seed)
        ks = jax.random.split(key, 7)
        C = N_EMBD
        x = jax.random.normal(ks[0], (B, T, C), dtype=jnp.float32)
        time_decay = jnp.full((C,), -1.0, dtype=jnp.float32)
        time_first = jnp.full((C,), 0.5, dtype=jnp.float32)
        s = 1.0 / np.sqrt(C)
        key_w = jax.random.uniform(ks[1], (C, C), jnp.float32, -s, s)
        value_w = jax.random.uniform(ks[2], (C, C), jnp.float32, -s, s)
        recep_w = jax.random.uniform(ks[3], (C, C), jnp.float32, -s, s)
        out_w = jax.random.uniform(ks[4], (C, C), jnp.float32, -s, s)
        return {'x': x, 'time_decay': time_decay, 'time_first': time_first, 'key_w': key_w, 'value_w': value_w, 'recep_w': recep_w, 'out_w': out_w}
    _L0_attn_all = _L0_attn_setup()
    _L0_attn_in = {k: v for k, v in _L0_attn_all.items() if k in ('time_decay', 'time_first', 'key_w', 'value_w', 'recep_w', 'out_w')}
    del _L0_attn_all

    def _L0_ffn_setup():
        import jax, jax.numpy as jnp
        import numpy as np
        from jax import lax
        D_MODEL = 128
        D_FF = 512
        NUM_EXPERTS = 24
        TOP_K = 2
        key = jax.random.key(seed)
        ks = jax.random.split(key, 7)
        s1 = 1.0 / np.sqrt(D_MODEL)
        s2 = 1.0 / np.sqrt(D_FF)
        x = jax.random.normal(ks[0], (2, 128, D_MODEL), dtype=jnp.float32)
        gate_w = jax.random.uniform(ks[1], (D_MODEL, NUM_EXPERTS), jnp.float32, -s1, s1)
        gate_b = jax.random.uniform(ks[2], (NUM_EXPERTS,), jnp.float32, -s1, s1)
        w1 = jax.random.uniform(ks[3], (NUM_EXPERTS, D_MODEL, D_FF), jnp.float32, -s1, s1)
        b1 = jax.random.uniform(ks[4], (NUM_EXPERTS, D_FF), jnp.float32, -s1, s1)
        w2 = jax.random.uniform(ks[5], (NUM_EXPERTS, D_FF, D_MODEL), jnp.float32, -s2, s2)
        b2 = jax.random.uniform(ks[6], (NUM_EXPERTS, D_MODEL), jnp.float32, -s2, s2)
        return {'x': x, 'gate_w': gate_w, 'gate_b': gate_b, 'w1': w1, 'b1': b1, 'w2': w2, 'b2': b2}
    _L0_ffn_all = _L0_ffn_setup()
    _L0_ffn_in = {k: v for k, v in _L0_ffn_all.items() if k in ('gate_w', 'gate_b', 'w1', 'b1', 'w2', 'b2')}
    del _L0_ffn_all

    def _L1_xattn_setup():
        import jax, jax.numpy as jnp
        import numpy as np
        D_MODEL = 128
        NUM_HEADS = 16
        DEPTH = D_MODEL // NUM_HEADS
        B, S = (2, 256)

        def _split_heads(x):
            b, s, _ = x.shape
            return x.reshape(b, s, NUM_HEADS, DEPTH).transpose(0, 2, 1, 3)
        key = jax.random.key(seed)
        ks = jax.random.split(key, 12)
        s = 0.02
        inp = {'v': jax.random.normal(ks[0], (B, S, D_MODEL), jnp.float32), 'k': jax.random.normal(ks[1], (B, S, D_MODEL), jnp.float32), 'q': jax.random.normal(ks[2], (B, S, D_MODEL), jnp.float32), 'mask': jnp.triu(jnp.ones((S, S), jnp.float32), k=1)[None, None, :, :], 'wq_w': jax.random.normal(ks[3], (D_MODEL, D_MODEL), jnp.float32) * s, 'wq_b': jnp.zeros((D_MODEL,), jnp.float32), 'wk_w': jax.random.normal(ks[4], (D_MODEL, D_MODEL), jnp.float32) * s, 'wk_b': jnp.zeros((D_MODEL,), jnp.float32), 'wv_w': jax.random.normal(ks[5], (D_MODEL, D_MODEL), jnp.float32) * s, 'wv_b': jnp.zeros((D_MODEL,), jnp.float32), 'dense_w': jax.random.normal(ks[6], (D_MODEL, D_MODEL), jnp.float32) * s, 'dense_b': jnp.zeros((D_MODEL,), jnp.float32)}
        return inp
    _L1_xattn_all = _L1_xattn_setup()
    _L1_xattn_in = {k: v for k, v in _L1_xattn_all.items() if k in ('wq_w', 'wq_b', 'wk_w', 'wk_b', 'wv_w', 'wv_b', 'dense_w', 'dense_b')}
    del _L1_xattn_all

    def _L1_attn_setup():
        import math
        import jax, jax.numpy as jnp
        import numpy as np
        NUM_BUCKETS = 32
        MAX_DISTANCE = 128
        HEADS = 8
        DIM_HEAD = 64

        def _relative_position_bucket(rel_pos, num_buckets=NUM_BUCKETS, max_distance=MAX_DISTANCE):
            n = jnp.maximum(-rel_pos, 0)
            max_exact = num_buckets // 2
            is_small = n < max_exact
            val_if_large = max_exact + (jnp.log(jnp.maximum(n, 1).astype(jnp.float32) / max_exact) / math.log(max_distance / max_exact) * (num_buckets - max_exact)).astype(jnp.int32)
            val_if_large = jnp.minimum(val_if_large, num_buckets - 1)
            return jnp.where(is_small, n, val_if_large)
        key = jax.random.key(seed)
        ks = jax.random.split(key, 5)
        b, n, dim = (2, 256, 128)
        inner = HEADS * DIM_HEAD
        return {'x': jax.random.normal(ks[0], (b, n, dim), dtype=jnp.float32), 'Wq': jax.random.normal(ks[1], (dim, inner), dtype=jnp.float32) * dim ** (-0.5), 'Wkv': jax.random.normal(ks[2], (dim, 2 * inner), dtype=jnp.float32) * dim ** (-0.5), 'Wo': jax.random.normal(ks[3], (inner, dim), dtype=jnp.float32) * inner ** (-0.5), 'bo': jnp.zeros((dim,), dtype=jnp.float32), 'rel_emb': jax.random.normal(ks[4], (NUM_BUCKETS, HEADS), dtype=jnp.float32) * 0.02}
    _L1_attn_all = _L1_attn_setup()
    _L1_attn_in = {k: v for k, v in _L1_attn_all.items() if k in ('Wq', 'Wkv', 'Wo', 'bo', 'rel_emb')}
    del _L1_attn_all

    def _L1_ffn_setup():
        import jax, jax.numpy as jnp
        import numpy as np
        D_MODEL = 128
        EXPANSION = 4
        D_HIDDEN = D_MODEL * EXPANSION
        NUM_STAGES = int(np.log2(D_HIDDEN))

        def butterfly(y, weights, dim):
            lead = y.shape[:-1]
            for stage in range(weights.shape[0]):
                s = 2 ** stage
                nb = dim // (2 * s)
                yr = y.reshape(*lead, nb, 2, s)
                a = yr[..., 0, :]
                b = yr[..., 1, :]
                w = weights[stage].reshape(nb, s, 2, 2)
                na = w[..., 0, 0] * a + w[..., 0, 1] * b
                nb2 = w[..., 1, 0] * a + w[..., 1, 1] * b
                y = jnp.stack([na, nb2], axis=-2).reshape(*lead, dim)
            return y
        key = jax.random.key(seed)
        ks = jax.random.split(key, 6)
        B, S = (4, 256)
        x = jax.random.normal(ks[0], (B, S, D_MODEL), jnp.float32)
        W_exp = jax.random.normal(ks[1], (D_MODEL, D_HIDDEN), jnp.float32) * 0.02
        b_exp = jnp.zeros((D_HIDDEN,), jnp.float32)
        up_weights = jax.random.normal(ks[2], (NUM_STAGES, D_HIDDEN // 2, 2, 2), jnp.float32) * 0.02
        up_bias = jnp.zeros((D_HIDDEN,), jnp.float32)
        down_weights = jax.random.normal(ks[3], (NUM_STAGES, D_HIDDEN // 2, 2, 2), jnp.float32) * 0.02
        W_con = jax.random.normal(ks[4], (D_HIDDEN, D_MODEL), jnp.float32) * 0.02
        b_con = jnp.zeros((D_MODEL,), jnp.float32)
        down_bias = jnp.zeros((D_MODEL,), jnp.float32)
        return dict(x=x, W_exp=W_exp, b_exp=b_exp, up_weights=up_weights, up_bias=up_bias, down_weights=down_weights, W_con=W_con, b_con=b_con, down_bias=down_bias)
    _L1_ffn_all = _L1_ffn_setup()
    _L1_ffn_in = {k: v for k, v in _L1_ffn_all.items() if k in ('W_exp', 'b_exp', 'up_weights', 'up_bias', 'down_weights', 'W_con', 'b_con', 'down_bias')}
    del _L1_ffn_all

    def _L2_xattn_setup():
        import jax, jax.numpy as jnp
        import numpy as np
        D_MODEL = 128
        N_HEADS = 16
        D_K = D_MODEL // N_HEADS

        def _split_heads(x):
            B, S, _ = x.shape
            return x.reshape(B, S, N_HEADS, D_K).transpose(0, 2, 1, 3)
        key = jax.random.key(seed)
        ks = jax.random.split(key, 12)
        B, S = (2, 256)
        scale = 1.0 / np.sqrt(D_MODEL)
        inp = {'query': jax.random.normal(ks[0], (B, S, D_MODEL), jnp.float32), 'key': jax.random.normal(ks[1], (B, S, D_MODEL), jnp.float32), 'value': jax.random.normal(ks[2], (B, S, D_MODEL), jnp.float32), 'weights': jax.random.uniform(ks[3], (B, S), jnp.float32), 'wq': jax.random.normal(ks[4], (D_MODEL, D_MODEL), jnp.float32) * scale, 'bq': jnp.zeros((D_MODEL,), jnp.float32), 'wk': jax.random.normal(ks[5], (D_MODEL, D_MODEL), jnp.float32) * scale, 'bk': jnp.zeros((D_MODEL,), jnp.float32), 'wv': jax.random.normal(ks[6], (D_MODEL, D_MODEL), jnp.float32) * scale, 'bv': jnp.zeros((D_MODEL,), jnp.float32), 'wo': jax.random.normal(ks[7], (D_MODEL, D_MODEL), jnp.float32) * scale, 'bo': jnp.zeros((D_MODEL,), jnp.float32)}
        return inp
    _L2_xattn_all = _L2_xattn_setup()
    _L2_xattn_in = {k: v for k, v in _L2_xattn_all.items() if k in ('wq', 'bq', 'wk', 'bk', 'wv', 'bv', 'wo', 'bo')}
    del _L2_xattn_all

    def _L2_attn_setup():
        import jax, jax.numpy as jnp
        import numpy as np
        B, T, D, H = (8, 512, 128, 8)

        def _block_linear(x, w, b):
            Bx, Tx, Dx = x.shape
            h, bw = (w.shape[0], w.shape[1])
            xb = x.reshape(Bx, Tx, h, bw)
            y = jnp.einsum('bthi,hij->bthj', xb, w) + b
            return y.reshape(Bx, Tx, Dx)

        def _rglru(x, a_param, ig_w, ig_b, ag_w, ag_b, sqrt_fn):
            gate_x = jax.nn.sigmoid(_block_linear(x, ig_w, ig_b))
            gate_a = jax.nn.sigmoid(_block_linear(x, ag_w, ag_b))
            log_a = -8.0 * gate_a * jax.nn.softplus(a_param)
            a = jnp.exp(log_a)
            a2 = jnp.exp(2.0 * log_a)
            multiplier = sqrt_fn(jnp.maximum(1.0 - a2, 1e-07))
            normed_x = x * gate_x * multiplier
            p = jnp.cumprod(a, axis=1)
            p_prefix = jnp.concatenate([jnp.ones_like(p[:, :1]), p[:, :-1]], axis=1)
            p_prefix = jnp.maximum(p_prefix, 1e-07)
            S = jnp.cumsum(normed_x / p_prefix, axis=1)
            h = p_prefix * S
            return (h, h[:, -1, :])

        def _reference_tuple_inner(x, segment_pos, a_param, ig_w, ig_b, ag_w, ag_b):
            y, last_h = _rglru(x, a_param, ig_w, ig_b, ag_w, ag_b, jnp.sqrt)
            return (y, last_h)
        key = jax.random.key(seed)
        k0, k1, k2, k3 = jax.random.split(key, 4)
        bw = D // H
        std = (1.0 / bw) ** 0.5
        x = jax.random.normal(k0, (B, T, D), dtype=jnp.float32)
        segment_pos = jnp.tile(jnp.arange(T, dtype=jnp.int32)[None, :], (B, 1))
        ig_w = jax.random.normal(k1, (H, bw, bw), dtype=jnp.float32) * std
        ig_b = jnp.zeros((H, bw), dtype=jnp.float32)
        ag_w = jax.random.normal(k2, (H, bw, bw), dtype=jnp.float32) * std
        ag_b = jnp.zeros((H, bw), dtype=jnp.float32)
        eps = 1e-08
        u = jax.random.uniform(k3, (D,), minval=0.9 ** 2 + eps, maxval=0.999 ** 2 + eps)
        a_param = jnp.log(jnp.exp(-0.5 * jnp.log(u)) - 1.0).astype(jnp.float32)
        return dict(x=x, segment_pos=segment_pos, a_param=a_param, ig_w=ig_w, ig_b=ig_b, ag_w=ag_w, ag_b=ag_b)
    _L2_attn_all = _L2_attn_setup()
    _L2_attn_in = {k: v for k, v in _L2_attn_all.items() if k in ('segment_pos', 'a_param', 'ig_w', 'ig_b', 'ag_w', 'ag_b')}
    del _L2_attn_all

    def _L2_ffn_setup():
        import jax, jax.numpy as jnp
        import numpy as np
        B, S = (4, 256)
        D_MODEL, D_FF, N_EXPERTS, TOP_K = (128, 512, 8, 2)
        T = B * S
        CAPACITY_FACTOR, MIN_CAP = (1.25, 4)
        CAP = max(int(CAPACITY_FACTOR * (T * TOP_K / N_EXPERTS)), MIN_CAP)
        key = jax.random.key(seed)
        ks = jax.random.split(key, 6)

        def w(k, shape, fan):
            return jax.random.normal(k, shape, jnp.float32) * fan ** (-0.5)
        return {'x': jax.random.normal(ks[0], (B, S, D_MODEL), jnp.float32), 'Wr': w(ks[1], (D_MODEL, N_EXPERTS), D_MODEL), 'W1': w(ks[2], (N_EXPERTS, D_MODEL, D_FF), D_MODEL), 'b1': jnp.zeros((N_EXPERTS, D_FF), jnp.float32), 'W2': w(ks[3], (N_EXPERTS, D_FF, D_MODEL), D_FF), 'b2': jnp.zeros((N_EXPERTS, D_MODEL), jnp.float32), 'fw1': w(ks[4], (D_MODEL, D_FF), D_MODEL), 'fb1': jnp.zeros((D_FF,), jnp.float32), 'fw2': w(ks[5], (D_FF, D_MODEL), D_FF), 'fb2': jnp.zeros((D_MODEL,), jnp.float32)}
    _L2_ffn_all = _L2_ffn_setup()
    _L2_ffn_in = {k: v for k, v in _L2_ffn_all.items() if k in ('Wr', 'W1', 'b1', 'W2', 'b2', 'fw1', 'fb1', 'fw2', 'fb2')}
    del _L2_ffn_all

    def _L3_xattn_setup():
        import jax, jax.numpy as jnp
        import numpy as np
        B, S, D = (4, 256, 128)
        H = 16
        HD = D // H
        NEG = -1000000000.0
        key = jax.random.key(seed)
        ks = jax.random.split(key, 8)
        x = jax.random.normal(ks[0], (B, S, D), dtype=jnp.float32)
        y = jax.random.normal(ks[1], (B, S, D), dtype=jnp.float32)
        log_seqs = jax.random.randint(ks[2], (B, S), 0, 100, dtype=jnp.int64)
        sc = 1.0 / np.sqrt(D)
        Wq = jax.random.normal(ks[3], (D, D), dtype=jnp.float32) * sc
        Wk = jax.random.normal(ks[4], (D, D), dtype=jnp.float32) * sc
        Wv = jax.random.normal(ks[5], (D, D), dtype=jnp.float32) * sc
        Wo = jax.random.normal(ks[6], (D, D), dtype=jnp.float32) * sc
        bo = jnp.zeros((D,), dtype=jnp.float32)
        return {'x': x, 'y': y, 'log_seqs': log_seqs, 'pad_id': 0, 'Wq': Wq, 'Wk': Wk, 'Wv': Wv, 'Wo': Wo, 'bo': bo}
    _L3_xattn_all = _L3_xattn_setup()
    _L3_xattn_in = {k: v for k, v in _L3_xattn_all.items() if k in ('Wq', 'Wk', 'Wv', 'Wo', 'bo')}
    del _L3_xattn_all

    def _L3_attn_setup():
        import jax, jax.numpy as jnp
        import numpy as np
        B, S, D, H = (2, 256, 128, 16)
        HEAD_DIM = D // H
        WINDOW = 32
        DILATION = 1
        NEG = jnp.float32(-1000000000.0)

        def _build_attn_mask(seq_len):
            idx = jnp.arange(seq_len)
            diff = idx[None, :] - idx[:, None]
            mask = jnp.where(diff > 0, -jnp.inf, 0.0).astype(jnp.float32)
            cond = (jnp.abs(diff) <= WINDOW) & (jnp.abs(diff) % DILATION == 0)
            allowed = jnp.where(cond, 0.0, -jnp.inf).astype(jnp.float32)
            mask = jnp.maximum(mask, allowed)
            return jnp.maximum(mask, NEG)
        key = jax.random.key(seed)
        k = jax.random.split(key, 5)
        return {'x': jax.random.normal(k[0], (B, S, D), dtype=jnp.float32), 'in_proj_w': jax.random.normal(k[1], (3 * D, D), dtype=jnp.float32) * D ** (-0.5), 'in_proj_b': jax.random.normal(k[2], (3 * D,), dtype=jnp.float32) * 0.02, 'out_proj_w': jax.random.normal(k[3], (D, D), dtype=jnp.float32) * D ** (-0.5), 'out_proj_b': jax.random.normal(k[4], (D,), dtype=jnp.float32) * 0.02}
    _L3_attn_all = _L3_attn_setup()
    _L3_attn_in = {k: v for k, v in _L3_attn_all.items() if k in ('in_proj_w', 'in_proj_b', 'out_proj_w', 'out_proj_b')}
    del _L3_attn_all

    def _L3_ffn_setup():
        import jax, jax.numpy as jnp
        import numpy as np
        D = 128
        H = 256
        E = 8
        B, T = (4, 256)
        LN_EPS = 1e-05
        key = jax.random.key(seed)
        k = jax.random.split(key, 6)
        std = 0.02
        return {'x': jax.random.normal(k[0], (B, T, D), dtype=jnp.float32), 'gate_w': jax.random.normal(k[1], (E, D), dtype=jnp.float32) * std, 'expert_w1': jax.random.normal(k[2], (E, D, H), dtype=jnp.float32) * std, 'expert_w2': jax.random.normal(k[3], (E, H, D), dtype=jnp.float32) * std, 'ln_gamma': jnp.ones((D,), dtype=jnp.float32), 'ln_beta': jnp.zeros((D,), dtype=jnp.float32)}
    _L3_ffn_all = _L3_ffn_setup()
    _L3_ffn_in = {k: v for k, v in _L3_ffn_all.items() if k in ('gate_w', 'expert_w1', 'expert_w2', 'ln_gamma', 'ln_beta')}
    del _L3_ffn_all
    return {'x': x, 'ctx_1024': ctx_1024, 'fside_BxS2_0': fside_BxS2_0, 'itok_BxS2_0_99': itok_BxS2_0_99, 'mask_1x1xSxS2_fk1': mask_1x1xSxS2_fk1, 'L0_xattn_Wq': _L0_xattn_in['Wq'], 'L0_xattn_bq': _L0_xattn_in['bq'], 'L0_xattn_Wk': _L0_xattn_in['Wk'], 'L0_xattn_bk': _L0_xattn_in['bk'], 'L0_xattn_Wv': _L0_xattn_in['Wv'], 'L0_xattn_bv': _L0_xattn_in['bv'], 'L0_xattn_Wo': _L0_xattn_in['Wo'], 'L0_xattn_bo': _L0_xattn_in['bo'], 'L0_attn_time_decay': _L0_attn_in['time_decay'], 'L0_attn_time_first': _L0_attn_in['time_first'], 'L0_attn_key_w': _L0_attn_in['key_w'], 'L0_attn_value_w': _L0_attn_in['value_w'], 'L0_attn_recep_w': _L0_attn_in['recep_w'], 'L0_attn_out_w': _L0_attn_in['out_w'], 'L0_ffn_gate_w': _L0_ffn_in['gate_w'], 'L0_ffn_gate_b': _L0_ffn_in['gate_b'], 'L0_ffn_w1': _L0_ffn_in['w1'], 'L0_ffn_b1': _L0_ffn_in['b1'], 'L0_ffn_w2': _L0_ffn_in['w2'], 'L0_ffn_b2': _L0_ffn_in['b2'], 'L1_xattn_wq_w': _L1_xattn_in['wq_w'], 'L1_xattn_wq_b': _L1_xattn_in['wq_b'], 'L1_xattn_wk_w': _L1_xattn_in['wk_w'], 'L1_xattn_wk_b': _L1_xattn_in['wk_b'], 'L1_xattn_wv_w': _L1_xattn_in['wv_w'], 'L1_xattn_wv_b': _L1_xattn_in['wv_b'], 'L1_xattn_dense_w': _L1_xattn_in['dense_w'], 'L1_xattn_dense_b': _L1_xattn_in['dense_b'], 'L1_attn_Wq': _L1_attn_in['Wq'], 'L1_attn_Wkv': _L1_attn_in['Wkv'], 'L1_attn_Wo': _L1_attn_in['Wo'], 'L1_attn_bo': _L1_attn_in['bo'], 'L1_attn_rel_emb': _L1_attn_in['rel_emb'], 'L1_ffn_W_exp': _L1_ffn_in['W_exp'], 'L1_ffn_b_exp': _L1_ffn_in['b_exp'], 'L1_ffn_up_weights': _L1_ffn_in['up_weights'], 'L1_ffn_up_bias': _L1_ffn_in['up_bias'], 'L1_ffn_down_weights': _L1_ffn_in['down_weights'], 'L1_ffn_W_con': _L1_ffn_in['W_con'], 'L1_ffn_b_con': _L1_ffn_in['b_con'], 'L1_ffn_down_bias': _L1_ffn_in['down_bias'], 'L2_xattn_wq': _L2_xattn_in['wq'], 'L2_xattn_bq': _L2_xattn_in['bq'], 'L2_xattn_wk': _L2_xattn_in['wk'], 'L2_xattn_bk': _L2_xattn_in['bk'], 'L2_xattn_wv': _L2_xattn_in['wv'], 'L2_xattn_bv': _L2_xattn_in['bv'], 'L2_xattn_wo': _L2_xattn_in['wo'], 'L2_xattn_bo': _L2_xattn_in['bo'], 'L2_attn_segment_pos': _L2_attn_in['segment_pos'], 'L2_attn_a_param': _L2_attn_in['a_param'], 'L2_attn_ig_w': _L2_attn_in['ig_w'], 'L2_attn_ig_b': _L2_attn_in['ig_b'], 'L2_attn_ag_w': _L2_attn_in['ag_w'], 'L2_attn_ag_b': _L2_attn_in['ag_b'], 'L2_ffn_Wr': _L2_ffn_in['Wr'], 'L2_ffn_W1': _L2_ffn_in['W1'], 'L2_ffn_b1': _L2_ffn_in['b1'], 'L2_ffn_W2': _L2_ffn_in['W2'], 'L2_ffn_b2': _L2_ffn_in['b2'], 'L2_ffn_fw1': _L2_ffn_in['fw1'], 'L2_ffn_fb1': _L2_ffn_in['fb1'], 'L2_ffn_fw2': _L2_ffn_in['fw2'], 'L2_ffn_fb2': _L2_ffn_in['fb2'], 'L3_xattn_Wq': _L3_xattn_in['Wq'], 'L3_xattn_Wk': _L3_xattn_in['Wk'], 'L3_xattn_Wv': _L3_xattn_in['Wv'], 'L3_xattn_Wo': _L3_xattn_in['Wo'], 'L3_xattn_bo': _L3_xattn_in['bo'], 'L3_attn_in_proj_w': _L3_attn_in['in_proj_w'], 'L3_attn_in_proj_b': _L3_attn_in['in_proj_b'], 'L3_attn_out_proj_w': _L3_attn_in['out_proj_w'], 'L3_attn_out_proj_b': _L3_attn_in['out_proj_b'], 'L3_ffn_gate_w': _L3_ffn_in['gate_w'], 'L3_ffn_expert_w1': _L3_ffn_in['expert_w1'], 'L3_ffn_expert_w2': _L3_ffn_in['expert_w2'], 'L3_ffn_ln_gamma': _L3_ffn_in['ln_gamma'], 'L3_ffn_ln_beta': _L3_ffn_in['ln_beta']}

def reference(x, ctx_1024, fside_BxS2_0, itok_BxS2_0_99, mask_1x1xSxS2_fk1, L0_xattn_Wq, L0_xattn_bq, L0_xattn_Wk, L0_xattn_bk, L0_xattn_Wv, L0_xattn_bv, L0_xattn_Wo, L0_xattn_bo, L0_attn_time_decay, L0_attn_time_first, L0_attn_key_w, L0_attn_value_w, L0_attn_recep_w, L0_attn_out_w, L0_ffn_gate_w, L0_ffn_gate_b, L0_ffn_w1, L0_ffn_b1, L0_ffn_w2, L0_ffn_b2, L1_xattn_wq_w, L1_xattn_wq_b, L1_xattn_wk_w, L1_xattn_wk_b, L1_xattn_wv_w, L1_xattn_wv_b, L1_xattn_dense_w, L1_xattn_dense_b, L1_attn_Wq, L1_attn_Wkv, L1_attn_Wo, L1_attn_bo, L1_attn_rel_emb, L1_ffn_W_exp, L1_ffn_b_exp, L1_ffn_up_weights, L1_ffn_up_bias, L1_ffn_down_weights, L1_ffn_W_con, L1_ffn_b_con, L1_ffn_down_bias, L2_xattn_wq, L2_xattn_bq, L2_xattn_wk, L2_xattn_bk, L2_xattn_wv, L2_xattn_bv, L2_xattn_wo, L2_xattn_bo, L2_attn_segment_pos, L2_attn_a_param, L2_attn_ig_w, L2_attn_ig_b, L2_attn_ag_w, L2_attn_ag_b, L2_ffn_Wr, L2_ffn_W1, L2_ffn_b1, L2_ffn_W2, L2_ffn_b2, L2_ffn_fw1, L2_ffn_fb1, L2_ffn_fw2, L2_ffn_fb2, L3_xattn_Wq, L3_xattn_Wk, L3_xattn_Wv, L3_xattn_Wo, L3_xattn_bo, L3_attn_in_proj_w, L3_attn_in_proj_b, L3_attn_out_proj_w, L3_attn_out_proj_b, L3_ffn_gate_w, L3_ffn_expert_w1, L3_ffn_expert_w2, L3_ffn_ln_gamma, L3_ffn_ln_beta):
    import jax
    import jax.numpy as jnp

    def _L0_xattn_ref(queries, keys, values, Wq, bq, Wk, bk, Wv, bv, Wo, bo):
        import jax, jax.numpy as jnp
        import numpy as np
        import math
        D_MODEL = 128
        N_HEADS = 16
        N, L, _ = queries.shape
        S = keys.shape[1]
        H = N_HEADS
        q = (queries @ Wq.T + bq).reshape(N, L, H, -1)
        k = (keys @ Wk.T + bk).reshape(N, S, H, -1)
        v = (values @ Wv.T + bv).reshape(N, S, H, -1)
        D = k.shape[-1]
        sm = jnp.einsum('nlhd,nshd->nlhs', q, k) / math.sqrt(D)
        causal_mask = jnp.triu(jnp.ones((L, S), dtype=bool), k=1)
        sm = jnp.where(causal_mask[None, :, None, :], -jnp.inf, sm)
        sm = jax.nn.softmax(sm, axis=-1)
        attn = jnp.einsum('nlhs,nshd->nlhd', sm, v)
        new_values = attn.reshape(N, L, H * D)
        return new_values @ Wo.T + bo

    def _L0_attn_ref(x, time_decay, time_first, key_w, value_w, recep_w, out_w):
        import jax, jax.numpy as jnp
        import numpy as np
        N_EMBD = 128
        B, T = (8, 256)

        def _wkv_scan(time_decay, time_first, k, v):
            Bn, Tn, Cn = k.shape
            kT = jnp.swapaxes(k, 0, 1)
            vT = jnp.swapaxes(v, 0, 1)
            aa0 = jnp.zeros((Bn, Cn), k.dtype)
            bb0 = jnp.zeros((Bn, Cn), k.dtype)
            pp0 = jnp.full((Bn, Cn), -10000.0, k.dtype)

            def step(carry, kv):
                aa, bb, pp = carry
                kt, vt = kv
                ww = time_first + pp
                p = jnp.maximum(pp, ww)
                e1 = jnp.exp(pp - p)
                e2 = jnp.exp(ww - p)
                wkv_t = (e1 * aa + e2 * vt) / (e1 * bb + e2 + 1e-06)
                ww2 = time_decay + pp
                p2 = jnp.maximum(pp, ww2)
                e1b = jnp.exp(pp - p2)
                e2b = jnp.exp(ww2 - p2)
                aa = e1b * aa + e2b * vt
                bb = e1b * bb + e2b
                return ((aa, bb, p2), wkv_t)
            _, wkvT = jax.lax.scan(step, (aa0, bb0, pp0), (kT, vT))
            return jnp.swapaxes(wkvT, 0, 1)
        k = jnp.einsum('btc,dc->btd', x, key_w)
        v = jnp.einsum('btc,dc->btd', x, value_w)
        r = jax.nn.sigmoid(jnp.einsum('btc,dc->btd', x, recep_w))
        wkv = _wkv_scan(time_decay, time_first, k, v)
        return jnp.einsum('btc,dc->btd', r * wkv, out_w)

    def _L0_ffn_ref(x, gate_w, gate_b, w1, b1, w2, b2):
        import jax, jax.numpy as jnp
        import numpy as np
        from jax import lax
        D_MODEL = 128
        D_FF = 512
        NUM_EXPERTS = 24
        TOP_K = 2
        gate_scores = jnp.einsum('bsd,de->bse', x, gate_w) + gate_b
        topk_val, topk_idx = lax.top_k(gate_scores, TOP_K)
        sparse_gates = jax.nn.softmax(topk_val, axis=-1)
        combine = jnp.sum(jax.nn.one_hot(topk_idx, NUM_EXPERTS, dtype=x.dtype) * sparse_gates[..., None], axis=-2)
        h = jax.nn.gelu(jnp.einsum('bsd,edf->besf', x, w1) + b1[None, :, None, :], approximate=False)
        y = jnp.einsum('besf,efd->besd', h, w2) + b2[None, :, None, :]
        out = jnp.einsum('bse,besd->bsd', combine, y)
        return out + x

    def _L1_xattn_ref(v, k, q, mask, wq_w, wq_b, wk_w, wk_b, wv_w, wv_b, dense_w, dense_b):
        import jax, jax.numpy as jnp
        import numpy as np
        D_MODEL = 128
        NUM_HEADS = 16
        DEPTH = D_MODEL // NUM_HEADS
        B, S = (2, 256)

        def _split_heads(x):
            b, s, _ = x.shape
            return x.reshape(b, s, NUM_HEADS, DEPTH).transpose(0, 2, 1, 3)
        qh = _split_heads(q @ wq_w.T + wq_b)
        kh = _split_heads(k @ wk_w.T + wk_b)
        vh = _split_heads(v @ wv_w.T + wv_b)
        scores = jnp.einsum('bhqd,bhkd->bhqk', qh, kh) / np.sqrt(DEPTH).astype(np.float32)
        scores = scores + mask * -1000000000.0
        attn = jax.nn.softmax(scores, axis=-1)
        av = jnp.einsum('bhqk,bhkd->bhqd', attn, vh)
        concat = av.transpose(0, 2, 1, 3).reshape(q.shape[0], -1, D_MODEL)
        return concat @ dense_w.T + dense_b

    def _L1_attn_ref(x, Wq, Wkv, Wo, bo, rel_emb):
        import math
        import jax, jax.numpy as jnp
        import numpy as np
        NUM_BUCKETS = 32
        MAX_DISTANCE = 128
        HEADS = 8
        DIM_HEAD = 64

        def _relative_position_bucket(rel_pos, num_buckets=NUM_BUCKETS, max_distance=MAX_DISTANCE):
            n = jnp.maximum(-rel_pos, 0)
            max_exact = num_buckets // 2
            is_small = n < max_exact
            val_if_large = max_exact + (jnp.log(jnp.maximum(n, 1).astype(jnp.float32) / max_exact) / math.log(max_distance / max_exact) * (num_buckets - max_exact)).astype(jnp.int32)
            val_if_large = jnp.minimum(val_if_large, num_buckets - 1)
            return jnp.where(is_small, n, val_if_large)
        b, n, dim = x.shape
        h, d = (HEADS, DIM_HEAD)
        scale = d ** (-0.5)
        bias_scale = d ** 0.5
        q = x @ Wq
        kv = x @ Wkv
        k, v = jnp.split(kv, 2, axis=-1)

        def to_heads(t):
            return t.reshape(b, n, h, d).transpose(0, 2, 1, 3)
        q, k, v = (to_heads(q) * scale, to_heads(k), to_heads(v))
        sim = jnp.einsum('bhid,bhjd->bhij', q, k)
        pos = jnp.arange(n)
        rel_pos = pos[None, :] - pos[:, None]
        buckets = _relative_position_bucket(rel_pos)
        bias = rel_emb[buckets]
        bias = bias.transpose(2, 0, 1)[None] * bias_scale
        sim = sim + bias
        causal_mask = jnp.triu(jnp.ones((n, n), dtype=bool), k=1)
        sim = jnp.where(causal_mask, -jnp.finfo(sim.dtype).max, sim)
        attn = jax.nn.softmax(sim, axis=-1)
        out = jnp.einsum('bhij,bhjd->bhid', attn, v)
        out = out.transpose(0, 2, 1, 3).reshape(b, n, h * d)
        return out @ Wo + bo

    def _L1_ffn_ref(x, W_exp, b_exp, up_weights, up_bias, down_weights, W_con, b_con, down_bias):
        import jax, jax.numpy as jnp
        import numpy as np
        D_MODEL = 128
        EXPANSION = 4
        D_HIDDEN = D_MODEL * EXPANSION
        NUM_STAGES = int(np.log2(D_HIDDEN))

        def butterfly(y, weights, dim):
            lead = y.shape[:-1]
            for stage in range(weights.shape[0]):
                s = 2 ** stage
                nb = dim // (2 * s)
                yr = y.reshape(*lead, nb, 2, s)
                a = yr[..., 0, :]
                b = yr[..., 1, :]
                w = weights[stage].reshape(nb, s, 2, 2)
                na = w[..., 0, 0] * a + w[..., 0, 1] * b
                nb2 = w[..., 1, 0] * a + w[..., 1, 1] * b
                y = jnp.stack([na, nb2], axis=-2).reshape(*lead, dim)
            return y
        h = jnp.einsum('bsd,dh->bsh', x, W_exp) + b_exp
        h = butterfly(h, up_weights, D_HIDDEN)
        h = jax.nn.gelu(h + up_bias, approximate=False)
        h = butterfly(h, down_weights, D_HIDDEN)
        y = jnp.einsum('bsh,hd->bsd', h, W_con) + b_con
        return y + down_bias

    def _L2_xattn_ref(query, key, value, weights, wq, bq, wk, bk, wv, bv, wo, bo):
        import jax, jax.numpy as jnp
        import numpy as np
        D_MODEL = 128
        N_HEADS = 16
        D_K = D_MODEL // N_HEADS

        def _split_heads(x):
            B, S, _ = x.shape
            return x.reshape(B, S, N_HEADS, D_K).transpose(0, 2, 1, 3)
        Q = _split_heads(query @ wq + bq)
        K = _split_heads(key @ wk + bk)
        V = _split_heads(value @ wv + bv)
        scores = jnp.einsum('bhqd,bhkd->bhqk', Q, K) / np.sqrt(D_K)
        log_w = jnp.log(weights + 1e-20)[:, None, None, :]
        attn = jax.nn.softmax(scores + log_w, axis=-1)
        out = jnp.einsum('bhqk,bhkd->bhqd', attn, V)
        B, H, S, Dk = out.shape
        out = out.transpose(0, 2, 1, 3).reshape(B, S, D_MODEL)
        return out @ wo + bo

    def _L2_attn_ref(x, segment_pos, a_param, ig_w, ig_b, ag_w, ag_b):
        import jax, jax.numpy as jnp
        import numpy as np
        B, T, D, H = (8, 512, 128, 8)

        def _block_linear(x, w, b):
            Bx, Tx, Dx = x.shape
            h, bw = (w.shape[0], w.shape[1])
            xb = x.reshape(Bx, Tx, h, bw)
            y = jnp.einsum('bthi,hij->bthj', xb, w) + b
            return y.reshape(Bx, Tx, Dx)

        def _rglru(x, a_param, ig_w, ig_b, ag_w, ag_b, sqrt_fn):
            gate_x = jax.nn.sigmoid(_block_linear(x, ig_w, ig_b))
            gate_a = jax.nn.sigmoid(_block_linear(x, ag_w, ag_b))
            log_a = -8.0 * gate_a * jax.nn.softplus(a_param)
            a = jnp.exp(log_a)
            a2 = jnp.exp(2.0 * log_a)
            multiplier = sqrt_fn(jnp.maximum(1.0 - a2, 1e-07))
            normed_x = x * gate_x * multiplier
            p = jnp.cumprod(a, axis=1)
            p_prefix = jnp.concatenate([jnp.ones_like(p[:, :1]), p[:, :-1]], axis=1)
            p_prefix = jnp.maximum(p_prefix, 1e-07)
            S = jnp.cumsum(normed_x / p_prefix, axis=1)
            h = p_prefix * S
            return (h, h[:, -1, :])

        def _reference_tuple_inner(x, segment_pos, a_param, ig_w, ig_b, ag_w, ag_b):
            y, last_h = _rglru(x, a_param, ig_w, ig_b, ag_w, ag_b, jnp.sqrt)
            return (y, last_h)
        return _reference_tuple_inner(x, segment_pos, a_param, ig_w, ig_b, ag_w, ag_b)[0]

    def _L2_ffn_ref(x, Wr, W1, b1, W2, b2, fw1, fb1, fw2, fb2):
        import jax, jax.numpy as jnp
        import numpy as np
        B, S = (4, 256)
        D_MODEL, D_FF, N_EXPERTS, TOP_K = (128, 512, 8, 2)
        T = B * S
        CAPACITY_FACTOR, MIN_CAP = (1.25, 4)
        CAP = max(int(CAPACITY_FACTOR * (T * TOP_K / N_EXPERTS)), MIN_CAP)
        Bx, Sx, D = x.shape
        Tn = Bx * Sx
        xf = x.reshape(Tn, D)
        logits = xf @ Wr
        probs = jax.nn.softmax(logits, axis=-1)
        scores, experts = jax.lax.top_k(probs, TOP_K)
        scores = scores / jnp.maximum(scores.sum(-1, keepdims=True), 1e-09)
        y_fb = jax.nn.gelu(xf @ fw1 + fb1, approximate=False) @ fw2 + fb2
        y = jnp.zeros_like(xf)
        fb_mask = jnp.zeros((Tn,), bool)
        for e in range(N_EXPERTS):
            assign = experts == e
            w_e = jnp.where(assign, scores, 0.0).sum(-1)
            eligible = assign.any(-1) & ~fb_mask
            rank = jnp.cumsum(eligible.astype(jnp.int32)) - 1
            keep = eligible & (rank < CAP)
            overflow = eligible & ~keep
            fb_mask = fb_mask | overflow
            y = jnp.where(overflow[:, None], y_fb, y)
            idx = jnp.nonzero(keep, size=CAP, fill_value=0)[0]
            valid = jnp.arange(CAP) < keep.sum()
            h = jax.nn.gelu(xf[idx] @ W1[e] + b1[e], approximate=False)
            y_e = h @ W2[e] + b2[e]
            y = y.at[idx].add(y_e * (w_e[idx] * valid)[:, None])
        return y.reshape(Bx, Sx, D)

    def _L3_xattn_ref(x, y, log_seqs, pad_id, Wq, Wk, Wv, Wo, bo):
        import jax, jax.numpy as jnp
        import numpy as np
        B, S, D = (4, 256, 128)
        H = 16
        HD = D // H
        NEG = -1000000000.0
        b = x.shape[0]
        q = (x @ Wq).reshape(b, -1, H, HD).transpose(0, 2, 1, 3)
        k = (y @ Wk).reshape(b, -1, H, HD).transpose(0, 2, 1, 3)
        v = (y @ Wv).reshape(b, -1, H, HD).transpose(0, 2, 1, 3)
        mask = (log_seqs == pad_id)[:, None, None, :]
        scores = jnp.einsum('bhqd,bhkd->bhqk', q, k)
        scores = jnp.where(mask, NEG, scores)
        probs = jax.nn.softmax(scores / np.sqrt(HD), axis=-1)
        attn = jnp.einsum('bhqk,bhkd->bhqd', probs, v)
        attn = attn.transpose(0, 2, 1, 3).reshape(b, -1, H * HD)
        return attn @ Wo + bo

    def _L3_attn_ref(x, in_proj_w, in_proj_b, out_proj_w, out_proj_b):
        import jax, jax.numpy as jnp
        import numpy as np
        B, S, D, H = (2, 256, 128, 16)
        HEAD_DIM = D // H
        WINDOW = 32
        DILATION = 1
        NEG = jnp.float32(-1000000000.0)

        def _build_attn_mask(seq_len):
            idx = jnp.arange(seq_len)
            diff = idx[None, :] - idx[:, None]
            mask = jnp.where(diff > 0, -jnp.inf, 0.0).astype(jnp.float32)
            cond = (jnp.abs(diff) <= WINDOW) & (jnp.abs(diff) % DILATION == 0)
            allowed = jnp.where(cond, 0.0, -jnp.inf).astype(jnp.float32)
            mask = jnp.maximum(mask, allowed)
            return jnp.maximum(mask, NEG)
        b, s, d = x.shape
        qkv = x @ in_proj_w.T + in_proj_b
        q, k, v = jnp.split(qkv, 3, axis=-1)

        def to_heads(t):
            return t.reshape(b, s, H, HEAD_DIM).transpose(0, 2, 1, 3)
        q, k, v = (to_heads(q), to_heads(k), to_heads(v))
        scale = jnp.float32(HEAD_DIM) ** (-0.5)
        scores = jnp.einsum('bhqd,bhkd->bhqk', q * scale, k)
        mask = _build_attn_mask(s)
        scores = scores + mask[None, None, :, :]
        attn = jax.nn.softmax(scores, axis=-1)
        out = jnp.einsum('bhqk,bhkd->bhqd', attn, v)
        out = out.transpose(0, 2, 1, 3).reshape(b, s, d)
        return out @ out_proj_w.T + out_proj_b

    def _L3_ffn_ref(x, gate_w, expert_w1, expert_w2, ln_gamma, ln_beta):
        import jax, jax.numpy as jnp
        import numpy as np
        D = 128
        H = 256
        E = 8
        B, T = (4, 256)
        LN_EPS = 1e-05
        Bb, Tt, Dd = x.shape
        x_flat = x.reshape(Bb * Tt, Dd)
        gate_logits = x_flat @ gate_w.T
        gate_probs = jax.nn.softmax(gate_logits, axis=-1)
        top_val = jnp.max(gate_probs, axis=-1)
        top_idx = jnp.argmax(gate_probs, axis=-1)
        top_val = top_val / (top_val + 1e-08)
        onehot = jax.nn.one_hot(top_idx, expert_w1.shape[0], dtype=x.dtype)
        xe = jnp.einsum('ne,nd->end', onehot, x_flat)
        he = jax.nn.gelu(jnp.einsum('end,edh->enh', xe, expert_w1), approximate=False)
        ye = jnp.einsum('enh,ehd->end', he, expert_w2)
        out_flat = jnp.einsum('end,ne->nd', ye, onehot) * top_val[:, None]
        out = out_flat.reshape(Bb, Tt, Dd)
        mu = jnp.mean(out, axis=-1, keepdims=True)
        var = jnp.mean((out - mu) ** 2, axis=-1, keepdims=True)
        out = (out - mu) * jax.lax.rsqrt(var + LN_EPS) * ln_gamma + ln_beta
        return out
    x = x + _L0_xattn_ref(_layernorm(x, axis=-1), ctx_1024, ctx_1024, L0_xattn_Wq, L0_xattn_bq, L0_xattn_Wk, L0_xattn_bk, L0_xattn_Wv, L0_xattn_bv, L0_xattn_Wo, L0_xattn_bo)
    x = x + _L0_attn_ref(_layernorm(x, axis=-1), L0_attn_time_decay, L0_attn_time_first, L0_attn_key_w, L0_attn_value_w, L0_attn_recep_w, L0_attn_out_w)
    x = x + _L0_ffn_ref(_layernorm(x, axis=-1), L0_ffn_gate_w, L0_ffn_gate_b, L0_ffn_w1, L0_ffn_b1, L0_ffn_w2, L0_ffn_b2)
    x = x + _L1_xattn_ref(ctx_1024, ctx_1024, _layernorm(x, axis=-1), mask_1x1xSxS2_fk1, L1_xattn_wq_w, L1_xattn_wq_b, L1_xattn_wk_w, L1_xattn_wk_b, L1_xattn_wv_w, L1_xattn_wv_b, L1_xattn_dense_w, L1_xattn_dense_b)
    x = x + _L1_attn_ref(_layernorm(x, axis=-1), L1_attn_Wq, L1_attn_Wkv, L1_attn_Wo, L1_attn_bo, L1_attn_rel_emb)
    x = x + _L1_ffn_ref(_layernorm(x, axis=-1), L1_ffn_W_exp, L1_ffn_b_exp, L1_ffn_up_weights, L1_ffn_up_bias, L1_ffn_down_weights, L1_ffn_W_con, L1_ffn_b_con, L1_ffn_down_bias)
    x = x + _L2_xattn_ref(_layernorm(x, axis=-1), ctx_1024, ctx_1024, fside_BxS2_0, L2_xattn_wq, L2_xattn_bq, L2_xattn_wk, L2_xattn_bk, L2_xattn_wv, L2_xattn_bv, L2_xattn_wo, L2_xattn_bo)
    x = x + _L2_attn_ref(_layernorm(x, axis=-1), L2_attn_segment_pos, L2_attn_a_param, L2_attn_ig_w, L2_attn_ig_b, L2_attn_ag_w, L2_attn_ag_b)
    x = x + _L2_ffn_ref(_layernorm(x, axis=-1), L2_ffn_Wr, L2_ffn_W1, L2_ffn_b1, L2_ffn_W2, L2_ffn_b2, L2_ffn_fw1, L2_ffn_fb1, L2_ffn_fw2, L2_ffn_fb2)
    x = x + _L3_xattn_ref(_layernorm(x, axis=-1), ctx_1024, itok_BxS2_0_99, 0, L3_xattn_Wq, L3_xattn_Wk, L3_xattn_Wv, L3_xattn_Wo, L3_xattn_bo)
    x = x + _L3_attn_ref(_layernorm(x, axis=-1), L3_attn_in_proj_w, L3_attn_in_proj_b, L3_attn_out_proj_w, L3_attn_out_proj_b)
    x = x + _L3_ffn_ref(_layernorm(x, axis=-1), L3_ffn_gate_w, L3_ffn_expert_w1, L3_ffn_expert_w2, L3_ffn_ln_gamma, L3_ffn_ln_beta)
    return x

_drawn_inputs = setup_inputs


def setup_inputs(seed=0):
    import zlib

    import numpy as np

    out = dict(_drawn_inputs(seed))
    spreads = {'L0_attn_time_decay': (-1.0, 0.551),
     'L0_attn_time_first': (0.5, 0.6),
     'L1_xattn_wq_b': (0.0, 0.8),
     'L1_xattn_wk_b': (0.0, 2.0),
     'L1_xattn_wv_b': (0.0, 0.1),
     'L1_xattn_dense_b': (0.0, 0.1),
     'L1_attn_bo': (0.0, 0.1),
     'L1_ffn_b_exp': (0.0, 0.1),
     'L1_ffn_up_bias': (0.0, 0.1),
     'L1_ffn_b_con': (0.0, 0.1),
     'L1_ffn_down_bias': (0.0, 0.1),
     'L2_xattn_bq': (0.0, 0.1),
     'L2_xattn_bk': (0.0, 2.0),
     'L2_xattn_bv': (0.0, 0.1),
     'L2_xattn_bo': (0.0, 0.1),
     'L2_attn_ig_b': (0.0, 0.1),
     'L2_attn_ag_b': (0.0, 0.277),
     'L2_ffn_b1': (0.0, 0.288),
     'L2_ffn_b2': (0.0, 0.1),
     'L2_ffn_fb1': (0.0, 0.1),
     'L2_ffn_fb2': (0.0, 0.1),
     'L3_xattn_bo': (0.0, 0.1),
     'L3_ffn_ln_gamma': (1.0, 0.2),
     'L3_ffn_ln_beta': (0.0, 0.1)}
    factors = {'L0_xattn_bk': 64.0, 'L1_xattn_wq_w': 8.0, 'L1_xattn_wk_w': 7.694}
    for name, (base, spread) in spreads.items():
        noise = np.random.default_rng([zlib.crc32(name.encode()), seed]).standard_normal(out[name].shape)
        drawn = base * np.exp(spread * noise) if base else spread * noise
        out[name] = jnp.asarray(drawn.astype(out[name].dtype))
    for name, factor in factors.items():
        out[name] = (out[name] * factor).astype(out[name].dtype)
    return out
```

```python
from contextlib import ExitStack

import concourse.bass as bass
from concourse import mybir

F32 = mybir.dt.float32
I32 = mybir.dt.int32
ACT = mybir.ActivationFunctionType
ALU = mybir.AluOpType
AX = mybir.AxisListType

P = 128
NB = 128
S = 32
KEYS = 257
TILES = NB * S // P
BPT = P // S
GT = 4
GW = GT * P
GROUPS = TILES // GT
HEADS = 16
EPS = 1e-5
CAP = 320
MASKED = -1.0e30

SLOTS = ["x0_q", "x0_k", "x0_v", "x0_o", "a0_v", "a0_r", "a0_o", "x1_q", "x1_k", "x1_v", "x1_o",
         "x2_q", "x2_k", "x2_v", "x2_o", "a2_i", "a2_a", "x3_q", "x3_k", "x3_v", "x3_o",
         "a3_q", "a3_k", "a3_v", "a3_o"] + [f"a1_{n}{c}" for n in "qkvo" for c in range(4)]
WAT = {n: i for i, n in enumerate(SLOTS)}
VECS = ["x0_bq", "x0_bk", "x0_bv", "x1_bq", "x1_bk", "x1_bv", "x2_bq", "x2_bk", "x2_bv",
        "a3_bq", "a3_bk", "a3_bv", "zero", "time_decay", "time_first", "a_param", "ig_b", "ag_b",
        "up_b0", "up_b1", "up_b2", "up_b3"]
VAT = {n: i for i, n in enumerate(VECS)}
ROWS = ["x0_bo", "x1_bo", "a1_bo", "x2_bo", "x3_bo", "a3_bo", "b_con", "down_bias", "gamma", "beta", "zero"]
RAT = {n: i for i, n in enumerate(ROWS)}
CONSTS = {"ident": 128, "group": 4, "head": 4, "quarter": 4, "sel": 32, "later": 32, "rev": 24, "upto": 128,
          "ones": 128, "mask4": 128, "diag512": 512}
CAT = {}
_at = 0
for _n, _w in CONSTS.items():
    CAT[_n] = (_at, _at + _w)
    _at += _w
NCONST = _at

DMA_SIGNALS = ["loaded", "ctx_loaded", "row_loaded", "w_loaded", "w_loaded0", "w_loaded1", "ct_loaded0", "ct_loaded1", "ct_loaded2",
               "ct_loaded3", "stored"]
SIGNALS = ["dve_passed", "pe_passed", "act_passed", "dve_step", "act_step", "pool_step",
           "var_ready", "rstd_ready", "xn_ready", "xnT_psum", "xnT_ready",
           "proj_psum0", "proj_psum1", "proj_psum2", "proj_done0", "proj_done1", "proj_done2",
           "q_built", "v_turned", "v_built", "scores", "centred", "exp_ready", "sums_ready", "probs_ready", "pT_ready",
           "av_psum", "heads_ready", "y_psum", "x_added",
           "kv_psum", "k_psum", "k_ready", "v_ready", "s_summed", "exp_done", "pT_psum", "a_ready",
           "o_psum", "o_ready", "pl_psum", "pl_ready", "pT2_psum", "pT2_ready",
           "up_psum", "gelu_ready", "down_psum", "copied", "logits", "stage_ready",
           "c_turned", "c_ready", "scan_ready", "a_done", "b_done", "c_done", "d_done", "e_done"]


class Signal:

    def __init__(self, sem, base, unit):
        self.sem, self.base, self.unit = sem, base, unit

    def __call__(self, k):
        return self.sem, self.base + k * self.unit


class Signals:

    CREDIT = 16

    def __init__(self, ctx, nc):
        self.sems = {n: ctx.enter_context(nc.semaphore(n)) for n in SIGNALS + DMA_SIGNALS}
        self.unit = {n: 16 if n in DMA_SIGNALS else 1 for n in self.sems}
        self.total = {n: self.CREDIT * self.unit[n] for n in self.sems}

    def __call__(self, name, times):
        s = Signal(self.sems[name], self.total[name], self.unit[name])
        self.total[name] += times * self.unit[name]
        return s


class Steps:

    def __init__(self, eng, signals, name):
        self.eng, self.signals, self.name = eng, signals, name
        self.base, self.k = signals.total[name], 0

    def link(self, ins):
        self.k += 1
        ins.then_inc(self.signals.sems[self.name], 1)
        self.eng.wait_ge(self.signals.sems[self.name], self.base + self.k)

    def count(self, ins):
        self.k += 1
        ins.then_inc(self.signals.sems[self.name], 1)

    def wait(self):
        self.eng.wait_ge(self.signals.sems[self.name], self.base + self.k)

    def loop(self, start, stop, per):
        return _StepLoop(self, start, stop, per)

    def close(self):
        self.signals.total[self.name] = self.base + self.k


class _StepLoop:
    def __init__(self, steps, start, stop, per):
        self.s, self.start, self.stop, self.per = steps, start, stop, per

    def __enter__(self):
        self.fori = self.s.eng.Fori(self.start, self.stop)
        i = self.fori.__enter__()
        self.b0, self.k0 = self.s.base, self.s.k
        self.s.base, self.s.k = (i - self.start) * self.per + (self.b0 + self.k0), 0
        return i

    def __exit__(self, *a):
        r = self.fori.__exit__(*a)
        assert a[0] is not None or self.s.k == self.per, f"the body links {self.s.k}, not {self.per}"
        self.s.base, self.s.k = self.b0, self.k0 + (self.stop - self.start) * self.per
        return r


def program(nc, T, out):
    with ExitStack() as ctx:
        def sb(name, shape, dt=F32):
            return ctx.enter_context(nc.sbuf_tensor(name, shape, dt))

        sig = Signals(ctx, nc)
        B = [ctx.enter_context(nc.psum_tensor(f"bank{i}", [P, 512], F32)) for i in range(8)]
        X = sb("X", [P, TILES, P])
        XNT = sb("XNT", [P, TILES * P])
        W = sb("W", [P, len(SLOTS), P])
        V = sb("V", [P, len(VECS)])
        R = sb("R", [1, len(ROWS), P])
        C = sb("C", [P, NCONST])
        GW0, GW2, GW3 = sb("GW0", [P, 24]), sb("GW2", [P, 8]), sb("GW3", [P, 8])
        GB = sb("GB", [1, 24])
        mean = sb("mean", [P, TILES])
        rstd = sb("rstd", [P, TILES])

        names = {}

        def hold(scope, name, shape):
            names[name] = names.get(name, 0) + 1
            return scope.enter_context(nc.sbuf_tensor(f"{name}_{names[name]}", shape, F32))

        def const(name):
            return C[:, CAT[name][0]:CAT[name][1]]

        def w(name):
            return W[:, WAT[name], :]

        def v(name):
            return V[:, VAT[name]:VAT[name] + 1]

        def r(name):
            return R[0:1, RAT[name], :]

        ident = const("ident")
        ones_row = C[0:1, CAT["ones"][0]:CAT["ones"][0] + P]
        xt = T["x"].rearrange("(t b) s d -> (b s) t d", b=BPT)
        ot = out.rearrange("(t b) s d -> (b s) t d", b=BPT)

        loaded = sig("loaded", 9)
        with nc.Block() as block:
            @block.sync
            def _(sp):
                for n, s in sig.sems.items():
                    sp.sem_inc(s, sig.CREDIT * sig.unit[n])
                for dst, src in ((X, xt), (C, T["consts"]), (W, T["weights"]), (V, T["vecs"]),
                                 (R, T["rows"]), (GW0, T["gate0"]), (GB, T["gate0_b"]), (GW2, T["gate2"]), (GW3, T["gate3"])):
                    sp.dma_start(dst[:], src).then_inc(loaded.sem, 16)
                sp.wait_ge(*loaded(9))

        def norm(add_back=False):
            with ExitStack() as c2:
                st = hold(c2, "stats", [P, TILES, 6])
                var = hold(c2, "var", [P, TILES])
                dif = hold(c2, "dif", [P, TILES])
                xn = hold(c2, "xn", [P, 2, GT, P])
                var_ready, rstd_ready = sig("var_ready", 1), sig("rstd_ready", 1)
                xn_ready, xnT_psum, xnT_ready = sig("xn_ready", 8), sig("xnT_psum", 8), sig("xnT_ready", 8)
                block = c2.enter_context(nc.Block())

                @block.vector
                def _(dve):
                    st_ = Steps(dve, sig, "dve_step")
                    with st_.loop(0, GROUPS, GT) as g:
                        for j in range(GT):
                            st_.count(dve.bn_stats(st[:, bass.ds(g * GT + j, 1), :], X[:, bass.ds(g * GT + j, 1), :]))
                    st_.wait()
                    st_.count(dve.tensor_tensor(mean[:], st[:, :, 1], st[:, :, 4], ALU.add))
                    st_.count(dve.tensor_tensor(dif[:], st[:, :, 1], st[:, :, 4], ALU.subtract))
                    st_.link(dve.tensor_tensor(var[:], st[:, :, 2], st[:, :, 5], ALU.add))
                    st_.count(dve.tensor_scalar(mean[:], mean[:], 0.5, None, ALU.mult))
                    st_.count(dve.tensor_scalar(var[:], var[:], 1.0 / P, EPS, ALU.mult, ALU.add))
                    st_.link(dve.tensor_tensor(dif[:], dif[:], dif[:], ALU.mult))
                    st_.close()
                    dve.scalar_tensor_tensor(out=var[:], in0=dif[:], scalar=0.25, in1=var[:],
                                             op0=ALU.mult, op1=ALU.add).then_inc(var_ready.sem, 1)
                    dve.wait_ge(*rstd_ready(1))
                    with st_.loop(0, GROUPS // 2, 8 if add_back else 0) as i:
                        for q in range(2):
                            g = i * 2 + q
                            dve.wait_ge(*xnT_psum(g - 1))
                            for j in range(GT):
                                t = g * GT + j
                                ins = dve.tensor_scalar(xn[:, q, j, :], X[:, bass.ds(t, 1), :], mean[:, bass.ds(t, 1)],
                                                        rstd[:, bass.ds(t, 1)], ALU.subtract, ALU.mult)
                                if j == GT - 1:
                                    ins.then_inc(xn_ready.sem, 1)
                                if add_back and j < GT - 1:
                                    st_.count(ins)
                            if add_back:
                                dve.wait_ge(*xn_ready(g + 1))
                                xg = X[:, bass.ds(g * GT, GT), :]
                                st_.count(dve.tensor_tensor(xg, xg, xn[:, q], ALU.add))
                    st_.close()

                @block.scalar
                def _(act):
                    st_ = Steps(act, sig, "act_step")
                    act.wait_ge(*var_ready(1))
                    st_.link(act.activation(var[:], var[:], ACT.Ln))
                    act.activation(rstd[:], var[:], ACT.Exp, scale=-0.5).then_inc(rstd_ready.sem, 1)
                    st_.close()
                    with act.Fori(0, GROUPS // 2) as i:
                        for q in range(2):
                            g = i * 2 + q
                            act.wait_ge(*xnT_psum(g + 1))
                            act.copy(XNT[:, bass.ds(g * GW, GW)], B[q][:]).then_inc(xnT_ready.sem, 1)

                @block.tensor
                def _(pe):
                    with pe.Fori(0, GROUPS // 2) as i:
                        for q in range(2):
                            g = i * 2 + q
                            pe.wait_ge(*xn_ready(g + 1))
                            pe.wait_ge(*xnT_ready(g - 1))
                            for j in range(GT):
                                ins = pe.transpose(B[q][:, j * P:(j + 1) * P], xn[:, q, j, :], ident)
                            ins.then_inc(xnT_psum.sem, 1)

        def project(jobs):
            psum = [sig(f"proj_psum{j}", 8) for j in range(len(jobs))]
            done = [sig(f"proj_done{j}", 8) for j in range(len(jobs))]
            with nc.Block() as block:
                @block.tensor
                def _(pe):
                    with pe.Fori(0, GROUPS // 2) as i:
                        for q in range(2):
                            g = i * 2 + q
                            for j, (dst, wt, src, bias, scale) in enumerate(jobs):
                                pe.wait_ge(*done[j](g - 1))
                                pe.matmul(B[2 * j + q][:], wt, src[:, bass.ds(g * GW, GW)],
                                          start=True, stop=True).then_inc(psum[j].sem, 1)

                @block.vector
                def _(dve):
                    with dve.Fori(0, GROUPS // 2) as i:
                        for q in range(2):
                            g = i * 2 + q
                            for j in (0, 2):
                                if j < len(jobs):
                                    dst, wt, src, bias, scale = jobs[j]
                                    dve.wait_ge(*psum[j](g + 1))
                                    dve.tensor_scalar(dst[:, bass.ds(g * GW, GW)], B[2 * j + q][:], bias, scale,
                                                      ALU.add, ALU.mult).then_inc(done[j].sem, 1)

                if len(jobs) > 1:
                    assert jobs[1][4] == 1.0

                    @block.scalar
                    def _(act):
                        with act.Fori(0, GROUPS // 2) as i:
                            for q in range(2):
                                g = i * 2 + q
                                act.wait_ge(*psum[1](g + 1))
                                act.activation(jobs[1][0][:, bass.ds(g * GW, GW)], B[2 + q][:], ACT.Identity,
                                               bias=jobs[1][3]).then_inc(done[1].sem, 1)

        def attn16(name, src, bv, bo, causal):
            with ExitStack() as c2:
                def sb2(n, shape):
                    return hold(c2, n, shape)
                QT, KT, VT = sb2("QT", [P, TILES * P]), sb2("KT", [P, TILES * P]), sb2("VT", [P, TILES * P])
                project([(QT, w(name + "_q"), XNT, v(name + "_bq"), 8 ** -0.5),
                         (KT, w(name + "_k"), src, v(name + "_bk"), 1.0),
                         (VT, w(name + "_v"), src, v("zero"), 1.0)])
                mask4x = sb2("mask4x", [P, BPT, 4, S])
                qb, kb, vb = (sb2(n, [P, 2, BPT, 4, S]) for n in ("qb", "kb", "vb"))
                vt = sb2("vt", [P, 2, P])
                e = sb2("e", [P, 2, GW])
                pt = sb2("pt", [P, 2, GW])
                m = sb2("m", [P, 2, 4, P])
                mx, sm = sb2("mx", [P, 2, 16]), sb2("sm", [P, 2, 16])
                q_built, v_turned, v_built = sig("q_built", 32), sig("v_turned", 32), sig("v_built", 32)
                scores, centred, exp_ready = sig("scores", 32), sig("centred", 32), sig("exp_ready", 32)
                pT_ready, av_psum = sig("pT_ready", 32), sig("av_psum", 32)
                heads_ready, y_psum, x_added = sig("heads_ready", 32), sig("y_psum", 32), sig("x_added", 32)
                copied = sig("copied", 1)
                N = TILES

                def masked(eng, dst, srcap, mask, over_src):
                    return eng.tensor_tensor(dst, srcap.unsqueeze(2).to_broadcast([P, BPT, 4, S]),
                                             mask.unsqueeze(1).unsqueeze(3).to_broadcast([P, BPT, 4, S]), ALU.mult)

                block = c2.enter_context(nc.Block())

                def run(eng, stages, depth, steps=None, per=0):
                    for t in range(2):
                        stages(t, t % 2, lambda x: 0 <= x < N)
                    lp = steps.loop(1, N // 2, per) if steps else eng.Fori(1, N // 2)
                    with lp as i:
                        for q in range(2):
                            stages(i * 2 + q, q, lambda x: True)
                    for t in range(N, N + depth):
                        stages(t, t % 2, lambda x: 0 <= x < N)

                @block.gpsimd
                def _(pool):
                    def stages(t, q, ok):
                        pool.wait_ge(*scores(t - 1))
                        tok = bass.ds(t * P, P)
                        masked(pool, qb[:, q], QT[:, tok].rearrange("p (b s) -> p b s", b=BPT), const("group"), 1)
                        masked(pool, kb[:, q], KT[:, tok].rearrange("p (b s) -> p b s", b=BPT), const("head"), 1)\
                            .then_inc(q_built.sem, 1)
                        pool.wait_ge(*v_turned(t + 1))
                        pool.wait_ge(*av_psum(t - 1))
                        masked(pool, vb[:, q], vt[:, q, :].rearrange("p (b s) -> p b s", b=BPT), const("group"), 1)\
                            .then_inc(v_built.sem, 1)
                    run(pool, stages, 0)

                @block.tensor
                def _(pe):
                    def stages(t, q, ok):
                        if ok(t):
                            pe.wait_ge(*q_built(t + 1))
                            pe.wait_ge(*centred(t - 1))
                            if isinstance(t, int) and t == 0:
                                pe.wait_ge(*copied(1))
                            if causal:
                                pe.matmul(B[q][:], ident, mask4x[:].rearrange("p b j k -> p (b j k)"), start=True,
                                          stop=False, skip_group_check=True)
                            for b in range(BPT):
                                ins = pe.matmul(B[q][:, b * P:(b + 1) * P], qb[:, q, b].rearrange("p j s -> p (j s)"),
                                                kb[:, q, b].rearrange("p j s -> p (j s)"), start=not causal, stop=True,
                                                skip_group_check=True)
                            ins.then_inc(scores.sem, 1)
                        u, z = t - 1, 1 - q
                        if ok(u):
                            pe.wait_ge(*pT_ready(u + 1))
                            pe.wait_ge(*v_built(u + 1))
                            pe.wait_ge(*heads_ready(u - 1))
                            for b in range(BPT):
                                out_b = B[2 + z][:].rearrange("p (j b s) -> p j b s", j=4, b=BPT)[:, :, b, :]
                                ins = pe.matmul(out_b, vb[:, z, b].rearrange("p j s -> p (j s)"),
                                                pt[:, z, b * P:(b + 1) * P], start=True, stop=True)
                            ins.then_inc(av_psum.sem, 1)
                        u, z = t - 2, q
                        if ok(u):
                            pe.wait_ge(*heads_ready(u + 1))
                            pe.wait_ge(*x_added(u - 1))
                            pe.matmul(B[4 + z][:, 0:P], ones_row, r(bo), start=True, stop=False)
                            for j in range(4):
                                ins = pe.matmul(B[4 + z][:, 0:P], m[:, z, j, :], w(name + "_o"),
                                                start=False, stop=(j == 3))
                            ins.then_inc(y_psum.sem, 1)
                    run(pe, stages, 2)

                @block.scalar
                def _(act):
                    def stages(t, q, ok):
                        act.wait_ge(*centred(t + 1))
                        act.activation(e[:, q, :], e[:, q, :], ACT.Exp).then_inc(exp_ready.sem, 1)
                    run(act, stages, 0)

                @block.vector
                def _(dve):
                    st_ = Steps(dve, sig, "dve_step")
                    for b in range(BPT):
                        for j in range(4):
                            ins = dve.tensor_scalar(mask4x[:, b, j, :], const("later"),
                                                    MASKED, None, ALU.mult)
                    ins.then_inc(copied.sem, 1)

                    def stages(t, q, ok):
                        if ok(t):
                            dve.wait_ge(*v_built(t - 1))
                            tok = bass.ds(t * P, P)
                            st_.link(dve.tensor_copy(vt[:, q, :], VT[:, tok]))
                            dve.transpose(vt[:, q, :], vt[:, q, :]).then_inc(v_turned.sem, 1)
                            dve.wait_ge(*scores(t + 1))
                            st_.link(dve.tensor_reduce(mx[:, q, :], B[q][:].rearrange("p (g k) -> p g k", k=S), AX.X, ALU.max))
                            dve.tensor_tensor(e[:, q, :].rearrange("p (g k) -> p g k", k=S),
                                              B[q][:].rearrange("p (g k) -> p g k", k=S),
                                              mx[:, q, :].unsqueeze(2).to_broadcast([P, 16, S]),
                                              ALU.subtract).then_inc(centred.sem, 1)
                        u, z = t - 1, 1 - q
                        if ok(u):
                            dve.wait_ge(*av_psum(u + 1))
                            dve.wait_ge(*y_psum(u - 1))
                            dve.scalar_tensor_tensor(out=m[:, z].rearrange("p j t -> p (j t)"), in0=B[2 + z][:],
                                                     scalar=v(bv), in1=const("diag512"), op0=ALU.add,
                                                     op1=ALU.mult).then_inc(heads_ready.sem, 1)
                        if ok(t):
                            dve.wait_ge(*exp_ready(t + 1))
                            ev = e[:, q, :].rearrange("p (g k) -> p g k", k=S)
                            st_.link(dve.tensor_reduce(sm[:, q, :], ev, AX.X, ALU.add))
                            st_.link(dve.reciprocal(sm[:, q, :], sm[:, q, :]))
                            st_.link(dve.tensor_tensor(ev, ev, sm[:, q, :].unsqueeze(2).to_broadcast([P, 16, S]), ALU.mult))
                            dve.wait_ge(*av_psum(t - 1))
                            dve.transpose(pt[:, q, :], e[:, q, :]).then_inc(pT_ready.sem, 1)
                        u, z = t - 2, q
                        if ok(u):
                            dve.wait_ge(*y_psum(u + 1))
                            xt_ = X[:, bass.ds(u, 1), :]
                            dve.tensor_tensor(xt_, xt_, B[4 + z][:, 0:P].unsqueeze(1), ALU.add).then_inc(x_added.sem, 1)
                    run(dve, stages, 2, st_, 10)
                    st_.close()

        def rwkv():
            with ExitStack() as c2:
                def sb2(n, shape):
                    return hold(c2, n, shape)
                VT, RT = sb2("VT", [P, TILES * P]), sb2("RT", [P, TILES * P])
                project([(VT, w("a0_v"), XNT, v("zero"), 1.0), (RT, w("a0_r"), XNT, v("zero"), 1.0)])
                pp = sb2("pp", [P, S + 1])
                relu_td = sb2("relu_td", [P, S])
                low = sb2("low", [P, S])
                ex = sb2("ex", [P, 4, S])
                bb = sb2("bb", [P, S + 1])
                den = sb2("den", [P, S])
                decay = sb2("decay", [P, 16, S])
                ub = sb2("ub", [P, 16, S])
                aa = sb2("aa", [P, 16, S])
                y = sb2("y", [P, 2, 16, S])
                a_done, b_done = sig("a_done", 1), sig("b_done", 1)
                exp_ready, scan_ready = sig("exp_ready", 8), sig("scan_ready", 8)
                y_psum, x_added = sig("y_psum", 8), sig("x_added", 8)
                block = c2.enter_context(nc.Block())
                td, tf = v("time_decay"), v("time_first")

                @block.vector
                def _(dve):
                    st_ = Steps(dve, sig, "dve_step")
                    p0 = pp[:, 0:S]
                    st_.count(dve.memset(pp[:, 0:1], -10000.0))
                    st_.count(dve.memset(low[:], -3.0e38))
                    st_.count(dve.memset(bb[:, 0:1], 0.0))
                    st_.count(dve.memset(ub[:], 0.0))
                    st_.count(dve.memset(decay[:], 0.0))
                    st_.count(dve.memset(relu_td[:], 0.0))
                    st_.wait()
                    st_.link(dve.tensor_scalar(relu_td[:], relu_td[:], td, None, ALU.max))
                    st_.link(dve.tensor_tensor_scan(pp[:, 1:S + 1], relu_td[:], low[:], pp[:, 0:1], ALU.add, ALU.max))
                    for k, x in ((0, tf), (2, td)):
                        st_.link(dve.tensor_scalar(ex[:, k + 1, :], p0, x, None, ALU.add))
                        st_.link(dve.tensor_tensor(den[:], p0, ex[:, k + 1, :], ALU.max))
                        st_.count(dve.tensor_tensor(ex[:, k, :], p0, den[:], ALU.subtract))
                        ins = dve.tensor_tensor(ex[:, k + 1, :], ex[:, k + 1, :], den[:], ALU.subtract)
                        st_.link(ins) if k == 0 else ins.then_inc(a_done.sem, 1)
                    dve.wait_ge(*b_done(1))
                    st_.link(dve.tensor_tensor_scan(bb[:, 1:S + 1], ex[:, 2, :], ex[:, 3, :], bb[:, 0:1], ALU.mult, ALU.add))
                    st_.link(dve.tensor_tensor(den[:], ex[:, 0, :], bb[:, 0:S], ALU.mult))
                    st_.link(dve.tensor_tensor(den[:], den[:], ex[:, 1, :], ALU.add))
                    st_.link(dve.tensor_scalar(den[:], den[:], 1e-6, None, ALU.add))
                    st_.link(dve.reciprocal(den[:], den[:]))
                    st_.count(dve.tensor_tensor(ex[:, 0, :], ex[:, 0, :], den[:], ALU.mult))
                    st_.count(dve.tensor_tensor(ex[:, 1, :], ex[:, 1, :], den[:], ALU.mult))
                    st_.link(dve.tensor_copy(decay[:, :, 1:S], ex[:, 2, 0:S - 1].unsqueeze(1).to_broadcast([P, 16, S - 1])))

                    def add(g, q):
                        dve.wait_ge(*y_psum(g + 1))
                        xg = X[:, bass.ds(g * GT, GT), :]
                        dve.tensor_tensor(xg, xg, B[q][:].rearrange("p (t d) -> p t d", t=GT), ALU.add)\
                            .then_inc(x_added.sem, 1)

                    def body(g, q):
                        vg = VT[:, bass.ds(g * GW, GW)].rearrange("p (b s) -> p b s", s=S)
                        st_.link(dve.tensor_tensor(ub[:, :, 1:S], vg[:, :, 0:S - 1],
                                                   ex[:, 3, 0:S - 1].unsqueeze(1).to_broadcast([P, 16, S - 1]), ALU.mult))
                        st_.link(dve.tensor_tensor_scan(aa[:].rearrange("p b s -> p (b s)"), decay[:].rearrange("p b s -> p (b s)"),
                                                        ub[:].rearrange("p b s -> p (b s)"), 0.0, ALU.mult, ALU.add))
                        st_.link(dve.tensor_tensor(aa[:], aa[:], ex[:, 0, :].unsqueeze(1).to_broadcast([P, 16, S]), ALU.mult))
                        dve.wait_ge(*y_psum(g - 1))
                        st_.link(dve.tensor_tensor(y[:, q], vg, ex[:, 1, :].unsqueeze(1).to_broadcast([P, 16, S]), ALU.mult))
                        st_.link(dve.tensor_tensor(y[:, q], y[:, q], aa[:], ALU.add))
                        dve.wait_ge(*exp_ready(g + 1))
                        st_.link(dve.tensor_scalar(aa[:].rearrange("p b s -> p (b s)"), RT[:, bass.ds(g * GW, GW)], 1.0, None, ALU.add))
                        st_.link(dve.reciprocal(aa[:], aa[:]))
                        dve.tensor_tensor(y[:, q], y[:, q], aa[:], ALU.mult).then_inc(scan_ready.sem, 1)
                    with st_.loop(0, GROUPS // 2, 14) as i:
                        for q in range(2):
                            body(i * 2 + q, q)
                            add(i * 2 + q, q)
                    st_.close()

                @block.scalar
                def _(act):
                    act.wait_ge(*a_done(1))
                    act.activation(ex[:], ex[:], ACT.Exp).then_inc(b_done.sem, 1)
                    with act.Fori(0, GROUPS) as g:
                        rg = RT[:, bass.ds(g * GW, GW)]
                        act.activation(rg, rg, ACT.Exp, scale=-1.0).then_inc(exp_ready.sem, 1)

                @block.tensor
                def _(pe):
                    with pe.Fori(0, GROUPS // 2) as i:
                        for q in range(2):
                            g = i * 2 + q
                            pe.wait_ge(*scan_ready(g + 1))
                            pe.wait_ge(*x_added(g - 1))
                            for j in range(GT):
                                ins = pe.matmul(B[q][:, j * P:(j + 1) * P],
                                                y[:, q].rearrange("p b s -> p (b s)")[:, j * P:(j + 1) * P],
                                                w("a0_o"), start=True, stop=True)
                            ins.then_inc(y_psum.sem, 1)

        def rglru():
            with ExitStack() as c2:
                def sb2(n, shape):
                    return hold(c2, n, shape)
                GX, GA = sb2("GX", [P, TILES * P]), sb2("GA", [P, TILES * P])
                project([(GX, w("a2_i"), XNT, v("ig_b"), 1.0), (GA, w("a2_a"), XNT, v("ag_b"), 1.0)])
                cp = sb2("cp", [P, 4])
                inner, first = sb2("inner", [P, 16, S]), sb2("first", [P, 16, S])
                a, a2, ash, p, u = (sb2(n, [P, 2, 16, S]) for n in ("a", "a2", "ash", "p", "u"))
                gx = sb2("gx", [P, 2, 16, S])
                a_done, b_done = sig("a_done", 1), sig("b_done", 1)
                exp_ready, c_done, d_done, e_done = sig("exp_ready", 8), sig("c_done", 8), sig("d_done", 8), sig("e_done", 8)
                copied, y_done = sig("copied", 8), sig("sums_ready", 8)
                scan_ready, y_psum, x_added = sig("scan_ready", 8), sig("y_psum", 8), sig("x_added", 8)
                block = c2.enter_context(nc.Block())
                flat = "p b s -> p (b s)"

                @block.scalar
                def _(act):
                    st_ = Steps(act, sig, "act_step")
                    st_.link(act.activation(cp[:, 0:1], v("a_param"), ACT.Abs))
                    st_.link(act.activation(cp[:, 0:1], cp[:, 0:1], ACT.Exp, scale=-1.0))
                    act.activation(cp[:, 0:1], cp[:, 0:1], ACT.Ln, bias=1.0).then_inc(a_done.sem, 1)
                    st_.close()
                    with act.Fori(0, GROUPS) as g:
                        tok = bass.ds(g * GW, GW)
                        act.activation(GX[:, tok], GX[:, tok], ACT.Exp, scale=-1.0)
                        act.activation(GA[:, tok], GA[:, tok], ACT.Exp, scale=-1.0).then_inc(exp_ready.sem, 1)
                    act.wait_ge(*b_done(1))
                    with st_.loop(0, GROUPS // 2, 2) as i:
                        for q in range(2):
                            g = i * 2 + q
                            act.wait_ge(*c_done(g + 1))
                            act.activation(a2[:, q], a[:, q], ACT.Exp, scale=cp[:, 2:3]).then_inc(d_done.sem, 1)
                            act.wait_ge(*scan_ready(g - 1))
                            act.activation(ash[:, q], a[:, q], ACT.Exp, scale=cp[:, 1:2]).then_inc(copied.sem, 1)
                            act.wait_ge(*e_done(g + 1))
                            st_.link(act.activation(a2[:, q], a2[:, q], ACT.Ln))
                            act.activation(a2[:, q], a2[:, q], ACT.Exp, scale=0.5).then_inc(y_done.sem, 1)
                    st_.close()

                @block.vector
                def _(dve):
                    st_ = Steps(dve, sig, "dve_step")
                    st_.count(dve.memset(inner[:], 1.0))
                    st_.count(dve.memset(first[:], 0.0))
                    st_.wait()
                    st_.count(dve.memset(inner[:, :, 0:1], 0.0))
                    st_.count(dve.memset(first[:, :, 0:1], 1.0))
                    st_.link(dve.memset(cp[:, 3:4], 0.0))
                    dve.wait_ge(*a_done(1))
                    st_.link(dve.tensor_scalar(cp[:, 3:4], cp[:, 3:4], v("a_param"), None, ALU.max))
                    st_.link(dve.tensor_tensor(cp[:, 3:4], cp[:, 3:4], cp[:, 0:1], ALU.add))
                    st_.count(dve.tensor_scalar(cp[:, 1:2], cp[:, 3:4], -8.0, None, ALU.mult))
                    dve.tensor_scalar(cp[:, 2:3], cp[:, 3:4], -16.0, None, ALU.mult).then_inc(b_done.sem, 1)
                    with st_.loop(0, GROUPS // 2, 26) as i:
                        for q in range(2):
                            g = i * 2 + q
                            tok = bass.ds(g * GW, GW)
                            dve.wait_ge(*exp_ready(g + 1))
                            st_.link(dve.tensor_scalar(a[:, q].rearrange(flat), GA[:, tok], 1.0, None, ALU.add))
                            dve.reciprocal(a[:, q], a[:, q]).then_inc(c_done.sem, 1)
                            st_.link(dve.tensor_scalar(gx[:, q].rearrange(flat), GX[:, tok], 1.0, None, ALU.add))
                            st_.link(dve.reciprocal(gx[:, q], gx[:, q]))
                            st_.link(dve.tensor_tensor(gx[:, q].rearrange(flat), gx[:, q].rearrange(flat), XNT[:, tok], ALU.mult))
                            dve.wait_ge(*d_done(g + 1))
                            st_.link(dve.tensor_scalar(a2[:, q], a2[:, q], -1.0, 1.0, ALU.mult, ALU.add))
                            dve.tensor_scalar(a2[:, q], a2[:, q], 1e-7, None, ALU.max).then_inc(e_done.sem, 1)
                            dve.wait_ge(*copied(g + 1))
                            st_.count(dve.tensor_copy(u[:, q, :, 1:S], ash[:, q, :, 0:S - 1]))
                            st_.link(dve.memset(u[:, q, :, 0:1], 0.0))
                            st_.link(dve.tensor_tensor_scan(p[:, q].rearrange(flat), u[:, q].rearrange(flat),
                                                            first[:].rearrange(flat), 0.0, ALU.mult, ALU.add))
                            st_.link(dve.tensor_scalar(p[:, q], p[:, q], 1e-7, None, ALU.max))
                            st_.link(dve.reciprocal(u[:, q], p[:, q]))
                            dve.wait_ge(*y_done(g + 1))
                            st_.link(dve.tensor_tensor(gx[:, q], gx[:, q], a2[:, q], ALU.mult))
                            st_.link(dve.tensor_tensor(u[:, q], u[:, q], gx[:, q], ALU.mult))
                            dve.wait_ge(*y_psum(g - 1))
                            st_.link(dve.tensor_tensor_scan(gx[:, q].rearrange(flat), inner[:].rearrange(flat),
                                                            u[:, q].rearrange(flat), 0.0, ALU.mult, ALU.add))
                            dve.tensor_tensor(p[:, q], p[:, q], gx[:, q], ALU.mult).then_inc(scan_ready.sem, 1)
                            dve.wait_ge(*y_psum(g + 1))
                            xg = X[:, bass.ds(g * GT, GT), :]
                            dve.tensor_tensor(xg, xg, B[q][:].rearrange("p (t d) -> p t d", t=GT), ALU.add)\
                                .then_inc(x_added.sem, 1)
                    st_.close()

                @block.tensor
                def _(pe):
                    with pe.Fori(0, GROUPS // 2) as i:
                        for q in range(2):
                            g = i * 2 + q
                            pe.wait_ge(*scan_ready(g + 1))
                            pe.wait_ge(*x_added(g - 1))
                            for j in range(GT):
                                ins = pe.transpose(B[q][:, j * P:(j + 1) * P],
                                                   p[:, q].rearrange(flat)[:, j * P:(j + 1) * P], ident)
                            ins.then_inc(y_psum.sem, 1)

        def gate_logits(G, E, gw, bias_row):
            with ExitStack() as c2:
                stage = hold(c2, "stage", [P, 2, GW])
                stage_ready, logits, copied = sig("stage_ready", 8), sig("logits", 8), sig("copied", 8)
                block = c2.enter_context(nc.Block())

                @block.scalar
                def _(act):
                    with act.Fori(0, GROUPS // 2) as i:
                        for q in range(2):
                            g = i * 2 + q
                            act.wait_ge(*logits(g - 1))
                            act.copy(stage[:, q, :], XNT[:, bass.ds(g * GW, GW)]).then_inc(stage_ready.sem, 1)

                @block.tensor
                def _(pe):
                    with pe.Fori(0, GROUPS // 2) as i:
                        for q in range(2):
                            g = i * 2 + q
                            pe.wait_ge(*stage_ready(g + 1))
                            pe.wait_ge(*copied(g - 1))
                            for j in range(GT):
                                o = B[q][:, j * E:(j + 1) * E]
                                if bias_row is not None:
                                    pe.matmul(o, ones_row, bias_row, start=True, stop=False)
                                ins = pe.matmul(o, stage[:, q, j * P:(j + 1) * P], gw, start=bias_row is None, stop=True)
                            ins.then_inc(logits.sem, 1)

                @block.vector
                def _(dve):
                    with dve.Fori(0, GROUPS // 2) as i:
                        for q in range(2):
                            g = i * 2 + q
                            dve.wait_ge(*logits(g + 1))
                            dve.tensor_copy(G[:, bass.ds(g * GT, GT), 0:E],
                                            B[q][:, 0:GT * E].rearrange("p (t e) -> p t e", t=GT)).then_inc(copied.sem, 1)

        def bc(ap, E):
            return ap.unsqueeze(2).to_broadcast([P, TILES, E])

        def pick(st_, dve, G, m, hot, E, tmp):
            rev = const("rev")[:, 0:E].unsqueeze(1).to_broadcast([P, TILES, E])
            st_.link(dve.tensor_reduce(m[:], G, AX.X, ALU.max))
            st_.link(dve.tensor_tensor(hot, G, bc(m[:], E), ALU.is_equal))
            st_.link(dve.tensor_tensor(hot, hot, rev, ALU.mult))
            st_.link(dve.tensor_reduce(tmp[:], hot, AX.X, ALU.max))
            st_.link(dve.tensor_tensor(hot, hot, bc(tmp[:], E), ALU.is_equal))

        def route(kind, Cmb, E, gw, bias_row=None):
            with ExitStack() as c2:
                def sb2(n, shape):
                    return hold(c2, n, shape)
                G, h1, h2 = (sb2(n, [P, TILES, E]) for n in ("G", "h1", "h2"))
                m1, m2, tmp, tot, fb = (sb2(n, [P, TILES]) for n in ("m1", "m2", "tmp", "tot", "fb"))
                elig, keep, one = (sb2(n, [P, TILES]) for n in ("elig", "keep", "one"))
                gate_logits(G, E, gw, bias_row)
                a_done, b_done = sig("a_done", 1), sig("b_done", 1)
                c_done, d_done = (sig(n, E if kind == "capacity" else 0) for n in ("c_done", "d_done"))
                block = c2.enter_context(nc.Block())

                @block.scalar
                def _(act):
                    act.wait_ge(*a_done(1))
                    if kind == "pairs":
                        act.activation(m2[:], m2[:], ACT.Exp).then_inc(b_done.sem, 1)
                    else:
                        act.activation(G[:], G[:], ACT.Exp).then_inc(b_done.sem, 1)

                if kind == "capacity":
                    @block.tensor
                    def _(pe):
                        for e in range(E):
                            pe.wait_ge(*c_done(e + 1))
                            pe.matmul(B[0][:, 0:TILES], const("upto"), elig[:], start=True, stop=True)
                            pe.matmul(B[1][:, 0:TILES], const("ones"), elig[:], start=True, stop=True)\
                                .then_inc(d_done.sem, 1)

                @block.vector
                def _(dve):
                    st_ = Steps(dve, sig, "dve_step")
                    if kind == "pairs":
                        pick(st_, dve, G[:], m1, h1[:], E, tmp)
                        st_.link(dve.scalar_tensor_tensor(out=G[:], in0=h1[:], scalar=-3.0e38, in1=G[:],
                                                          op0=ALU.mult, op1=ALU.add))
                        pick(st_, dve, G[:], m2, h2[:], E, tmp)
                        dve.tensor_tensor(m2[:], m2[:], m1[:], ALU.subtract).then_inc(a_done.sem, 1)
                        dve.wait_ge(*b_done(1))
                        st_.link(dve.tensor_scalar(m1[:], m2[:], 1.0, None, ALU.add))
                        st_.link(dve.reciprocal(m1[:], m1[:]))
                        st_.link(dve.tensor_tensor(m2[:], m2[:], m1[:], ALU.mult))
                        st_.link(dve.tensor_tensor(h1[:], h1[:], bc(m1[:], E), ALU.mult))
                        st_.link(dve.tensor_tensor(h2[:], h2[:], bc(m2[:], E), ALU.mult))
                        st_.link(dve.tensor_tensor(Cmb[:], h1[:], h2[:], ALU.add))
                    else:
                        st_.link(dve.tensor_reduce(m1[:], G[:], AX.X, ALU.max))
                        dve.tensor_tensor(G[:], G[:], bc(m1[:], E), ALU.subtract).then_inc(a_done.sem, 1)
                        dve.wait_ge(*b_done(1))
                        st_.link(dve.tensor_reduce(m1[:], G[:], AX.X, ALU.add))
                        st_.link(dve.reciprocal(m1[:], m1[:]))
                        st_.link(dve.tensor_tensor(G[:], G[:], bc(m1[:], E), ALU.mult))
                        pick(st_, dve, G[:], m1, h1[:], E, tmp)
                    if kind == "first":
                        st_.link(dve.tensor_scalar(tmp[:], m1[:], 1e-8, None, ALU.add))
                        st_.link(dve.reciprocal(tmp[:], tmp[:]))
                        st_.link(dve.tensor_tensor(m1[:], m1[:], tmp[:], ALU.mult))
                        st_.link(dve.tensor_tensor(Cmb[:], h1[:], bc(m1[:], E), ALU.mult))
                    if kind == "capacity":
                        st_.link(dve.scalar_tensor_tensor(out=G[:], in0=h1[:], scalar=-3.0e38, in1=G[:],
                                                          op0=ALU.mult, op1=ALU.add))
                        pick(st_, dve, G[:], m2, h2[:], E, tmp)
                        st_.link(dve.tensor_tensor(tmp[:], m1[:], m2[:], ALU.add))
                        st_.link(dve.tensor_scalar(tmp[:], tmp[:], 1e-9, None, ALU.max))
                        st_.link(dve.reciprocal(tmp[:], tmp[:]))
                        st_.count(dve.tensor_tensor(m1[:], m1[:], tmp[:], ALU.mult))
                        st_.count(dve.tensor_tensor(m2[:], m2[:], tmp[:], ALU.mult))
                        st_.link(dve.tensor_tensor(G[:], h1[:], h2[:], ALU.add))
                        st_.count(dve.tensor_tensor(h1[:], h1[:], bc(m1[:], E), ALU.mult))
                        st_.link(dve.tensor_tensor(h2[:], h2[:], bc(m2[:], E), ALU.mult))
                        st_.count(dve.tensor_tensor(h1[:], h1[:], h2[:], ALU.add))
                        st_.count(dve.memset(one[:], 1.0))
                        st_.link(dve.memset(fb[:], 0.0))
                        for e in range(E):
                            st_.link(dve.tensor_tensor(keep[:], G[:, :, e], fb[:], ALU.mult))
                            dve.tensor_tensor(elig[:], G[:, :, e], keep[:], ALU.subtract).then_inc(c_done.sem, 1)
                            dve.wait_ge(*d_done(e + 1))
                            st_.link(dve.tensor_tensor_scan(tot[:], one[:], B[1][:, 0:TILES], 0.0, ALU.mult, ALU.add))
                            st_.link(dve.tensor_tensor(tot[:], tot[:], B[1][:, 0:TILES], ALU.subtract))
                            st_.link(dve.tensor_tensor(tot[:], tot[:], B[0][:, 0:TILES], ALU.add))
                            st_.link(dve.scalar_tensor_tensor(out=keep[:], in0=tot[:], scalar=float(CAP), in1=elig[:],
                                                              op0=ALU.is_le, op1=ALU.mult))
                            st_.link(dve.tensor_tensor(elig[:], elig[:], keep[:], ALU.subtract))
                            st_.count(dve.tensor_tensor(fb[:], fb[:], elig[:], ALU.add))
                            st_.link(dve.tensor_tensor(Cmb[:, :, e], h1[:, :, e], keep[:], ALU.mult))
                        st_.count(dve.tensor_copy(Cmb[:, :, E], fb[:]))
                        st_.link(dve.tensor_scalar(fb[:], fb[:], -1.0, 1.0, ALU.mult, ALU.add))
                        st_.link(dve.tensor_tensor(Cmb[:, :, 0:E], Cmb[:, :, 0:E], bc(fb[:], E), ALU.mult))
                    st_.close()

        def expert_bias(Cmb, E, b2):
            with ExitStack() as c2:
                def sb2(n, shape):
                    return hold(c2, n, shape)
                b2s = sb2("b2s", [E, P])
                cst, ct = sb2("cst", [P, 2, GT, E]), sb2("ct", [E, 2, GW])
                w_loaded = sig("w_loaded", 1)
                stage_ready, c_turned, c_ready = sig("stage_ready", 8), sig("c_turned", 8), sig("c_ready", 8)
                y_psum, x_added = sig("y_psum", 8), sig("x_added", 8)
                block = c2.enter_context(nc.Block())

                @block.sync
                def _(sp):
                    sp.dma_start(b2s[:], b2).then_inc(w_loaded.sem, 16)

                @block.vector
                def _(dve):
                    with dve.Fori(0, GROUPS // 2) as i:
                        for q in range(2):
                            g = i * 2 + q
                            dve.wait_ge(*c_turned(g - 1))
                            dve.tensor_copy(cst[:, q], Cmb[:, bass.ds(g * GT, GT), :]).then_inc(stage_ready.sem, 1)
                            dve.wait_ge(*y_psum(g + 1))
                            xg = X[:, bass.ds(g * GT, GT), :]
                            dve.tensor_tensor(xg, xg, B[2 + q][:].rearrange("p (t d) -> p t d", t=GT), ALU.add)\
                                .then_inc(x_added.sem, 1)

                @block.scalar
                def _(act):
                    with act.Fori(0, GROUPS // 2) as i:
                        for q in range(2):
                            g = i * 2 + q
                            act.wait_ge(*c_turned(g + 1))
                            act.wait_ge(*y_psum(g - 1))
                            act.copy(ct[:, q, :], B[q][0:E, :]).then_inc(c_ready.sem, 1)

                @block.tensor
                def _(pe):
                    pe.wait_ge(*w_loaded(1))
                    with pe.Fori(0, GROUPS // 2) as i:
                        for q in range(2):
                            g = i * 2 + q
                            pe.wait_ge(*stage_ready(g + 1))
                            pe.wait_ge(*c_ready(g - 1))
                            for j in range(GT):
                                ins = pe.transpose(B[q][0:E, j * P:(j + 1) * P], cst[:, q, j, :], ident)
                            ins.then_inc(c_turned.sem, 1)
                            pe.wait_ge(*c_ready(g + 1))
                            pe.wait_ge(*x_added(g - 1))
                            for j in range(GT):
                                ins = pe.matmul(B[2 + q][:, j * P:(j + 1) * P], ct[:, q, j * P:(j + 1) * P], b2s[:],
                                                start=True, stop=True)
                            ins.then_inc(y_psum.sem, 1)

        def experts(E, FC, Y, Cmb, w1, b1, w2, ready=None):
            with ExitStack() as c2:
                def sb2(n, shape):
                    return hold(c2, n, shape)
                F = FC * P
                if ready is None:
                    W1, W2, B1 = sb2("W1", [P, 2, F]), sb2("W2", [P, 2, FC, P]), sb2("B1", [P, 2, FC])
                else:
                    W1, W2, B1 = ready
                H = sb2("H", [P, 2, FC, GW])
                steps = E * GROUPS
                loads = [0, 0] if ready else [(E + 1) // 2, E // 2]
                w_loaded = [sig(f"w_loaded{s}", 3 * loads[s]) for s in range(2)]
                up_psum, gelu_ready = sig("up_psum", steps * FC), sig("gelu_ready", steps * FC)
                down_psum, x_added = sig("down_psum", steps), sig("x_added", steps)
                block = c2.enter_context(nc.Block())
                pairs = (E - 1) // 2

                def over_experts(eng, body):
                    if pairs:
                        with eng.Fori(0, pairs) as i:
                            for s in range(2):
                                body(i * 2 + s, i, s, False)
                    for e in range(2 * pairs, E):
                        body(e, e // 2, e % 2, e == E - 1)

                def over_groups(eng, e, fn, last=4):
                    with eng.Fori(0, last) as j:
                        for q in range(2):
                            fn(e, j * 2 + q, q)

                @block.sync
                def _(sp):
                    def body(e, h, s, last):
                        sp.wait_ge(*down_psum(8 * (e - 1)))
                        sp.dma_start(W1[:, s, :], w1[bass.ds(e, 1)].rearrange("e p f -> p (e f)")).then_inc(w_loaded[s].sem, 16)
                        sp.dma_start(B1[:, s, :], b1[bass.ds(e, 1)].rearrange("e p c -> p (e c)")).then_inc(w_loaded[s].sem, 16)
                        sp.dma_start(W2[:, s], w2[bass.ds(e, 1)].rearrange("e (c p) n -> p (e c) n", p=P)).then_inc(w_loaded[s].sem, 16)
                    if ready is None:
                        over_experts(sp, body)

                @block.tensor
                def _(pe):
                    def up(e, g, q, s):
                        for c in range(FC):
                            n = (e * GROUPS + g) * FC + c
                            bank = B[c if FC == 4 else 2 * q + c]
                            pe.wait_ge(*gelu_ready(n - 3))
                            pe.matmul(bank[:], W1[:, s, c * P:(c + 1) * P], XNT[:, bass.ds(g * GW, GW)],
                                      start=True, stop=True).then_inc(up_psum.sem, 1)

                    def down(e, g, q, s):
                        n = e * GROUPS + g
                        pe.wait_ge(*gelu_ready((n + 1) * FC))
                        pe.wait_ge(*x_added(n - 1))
                        for j in range(GT):
                            for c in range(FC):
                                ins = pe.matmul(B[4 + q][:, j * P:(j + 1) * P], H[:, q, c, j * P:(j + 1) * P],
                                                W2[:, s, c, :], start=(c == 0), stop=(c == FC - 1))
                        ins.then_inc(down_psum.sem, 1)

                    def body(e, h, s, last):
                        def fn(e, g, q):
                            up(e, g + 1, 1 - q, s)
                            down(e, g, q, s)
                        over_groups(pe, e, fn, 3)
                        up(e, 7, 1, s)
                        down(e, 6, 0, s)
                        if not last:
                            pe.wait_ge(*w_loaded[1 - s](3 * (h + s + 1)))
                            up(e + 1, 0, 0, 1 - s)
                        down(e, 7, 1, s)
                    if ready is None:
                        pe.wait_ge(*w_loaded[0](3))
                    up(0, 0, 0, 0)
                    over_experts(pe, body)

                @block.scalar
                def _(act):
                    def body(e, h, s, last):
                        if ready is None:
                            act.wait_ge(*w_loaded[s](3 * (h + 1)))

                        def fn(e, g, q):
                            n = e * GROUPS + g
                            act.wait_ge(*down_psum(n - 1))
                            for c in range(FC):
                                act.wait_ge(*up_psum(n * FC + c + 1))
                                bank = B[c if FC == 4 else 2 * q + c]
                                act.activation(H[:, q, c, :], bank[:], ACT.Gelu, bias=B1[:, s, c:c + 1])\
                                    .then_inc(gelu_ready.sem, 1)
                        over_groups(act, e, fn)
                    over_experts(act, body)

                @block.vector
                def _(dve):
                    def body(e, h, s, last):
                        def fn(e, g, q):
                            n = e * GROUPS + g
                            dve.wait_ge(*down_psum(n + 1))
                            dve.wait_ge(*x_added(n - 7))
                            for j in range(GT):
                                t = g * GT + j
                                yt = Y[:, bass.ds(t, 1), :]
                                bj = B[4 + q][:, j * P:(j + 1) * P]
                                if Cmb is None:
                                    ins = dve.tensor_tensor(yt, bj.unsqueeze(1), yt, ALU.add)
                                else:
                                    ins = dve.scalar_tensor_tensor(
                                        out=yt, in0=bj.unsqueeze(1), scalar=Cmb[:, bass.ds(t, 1), bass.ds(e, 1)].rearrange("p a b -> p (a b)"),
                                        in1=yt, op0=ALU.mult, op1=ALU.add)
                            ins.then_inc(x_added.sem, 1)
                        over_groups(dve, e, fn)
                    over_experts(dve, body)

        def attn8():
            with ExitStack() as c2:
                def sb2(n, shape):
                    return hold(c2, n, shape)
                BPS, N = BPT, TILES
                hot = sb2("hot", [32, S * P])
                emb = sb2("emb", [32, 8])
                bias = sb2("bias", [P, 2, S])
                laterM = sb2("laterM", [P, S])
                row_loaded, copied, a_done = sig("row_loaded", 2), sig("copied", 1), sig("a_done", 1)
                with nc.Block() as block:
                    @block.sync
                    def _(sp):
                        sp.dma_start(hot[:], T["buckets"]).then_inc(row_loaded.sem, 16)
                        sp.dma_start(emb[:], T["rel_emb"]).then_inc(row_loaded.sem, 16)

                    @block.tensor
                    def _(pe):
                        pe.wait_ge(*row_loaded(2))
                        for k in range(S):
                            ins = pe.matmul(B[0][:, 8 * k:8 * k + 8], hot[:, k * P:(k + 1) * P], emb[:], start=True, stop=True)
                        ins.then_inc(a_done.sem, 1)

                    @block.vector
                    def _(dve):
                        dve.tensor_scalar(laterM[:], const("later"), MASKED, None, ALU.mult).then_inc(copied.sem, 1)
                        dve.wait_ge(*copied(1))
                        dve.wait_ge(*a_done(1))
                        for A in range(4):
                            p = slice(32 * A, 32 * A + 32)
                            for h in range(2):
                                src = B[0][p, 0:8 * S].rearrange("p (k h) -> p h k", h=8)[:, 2 * A + h, :]
                                dve.scalar_tensor_tensor(out=bias[p, h, :], in0=src, scalar=64 ** 0.5, in1=laterM[p, :],
                                                         op0=ALU.mult, op1=ALU.add)
                qT, kT, vt = (sb2(n, [P, 2, 4, P]) for n in ("qT", "kT", "vt"))
                e, pt = sb2("e", [P, 2, 2, P]), sb2("pt", [P, 2, 2, P])
                o = sb2("o", [P, 2, 4, P])
                mx = sb2("mx", [P, 2, 8])
                qp, kp, vp = sig("proj_psum0", N), sig("proj_psum1", N), sig("proj_psum2", N)
                qd, kd, vd = sig("proj_done0", N), sig("proj_done1", N), sig("proj_done2", N)
                scores, centred, exp_ready, pT_ready = (sig(n, N) for n in ("scores", "centred", "exp_ready", "pT_ready"))
                s_summed = sig("s_summed", N)
                av_psum, o_ready, a_ready, y_psum, x_added = (sig(n, N) for n in ("av_psum", "o_ready", "a_ready", "y_psum", "x_added"))
                block = c2.enter_context(nc.Block())

                def run(eng, stages, depth, steps=None, per=0):
                    for t in range(2):
                        stages(t, t % 2, lambda x: 0 <= x < N)
                    with (steps.loop(1, N // 2, per) if steps else eng.Fori(1, N // 2)) as i:
                        for q in range(2):
                            stages(i * 2 + q, q, lambda x: True)
                    for t in range(N, N + depth):
                        stages(t, t % 2, lambda x: 0 <= x < N)

                @block.tensor
                def _(pe):
                    def stages(t, q, ok):
                        z = 1 - q
                        if ok(t):
                            tok = bass.ds(t * P, P)
                            pe.wait_ge(*vd(t))
                            for c in range(4):
                                ins = pe.matmul(B[0][:, c * P:(c + 1) * P], w(f"a1_q{c}"), XNT[:, tok], start=True, stop=True)
                            ins.then_inc(qp.sem, 1)
                            pe.wait_ge(*x_added(t - 1))
                            for c in range(4):
                                ins = pe.matmul(B[1][:, c * P:(c + 1) * P], w(f"a1_k{c}"), XNT[:, tok], start=True, stop=True)
                            ins.then_inc(kp.sem, 1)
                            pe.wait_ge(*qd(t + 1))
                            for c in range(4):
                                out_c = B[0][:].rearrange("p (b c s) -> p b c s", b=BPS, c=4)[:, :, c, :]
                                ins = pe.matmul(out_c, w(f"a1_v{c}"), XNT[:, tok], start=True, stop=True)
                            ins.then_inc(vp.sem, 1)
                        u = t - 1
                        if ok(u):
                            pe.wait_ge(*pT_ready(u + 1))
                            pe.wait_ge(*o_ready(u))
                            pe.wait_ge(*a_ready(u))
                            for b in range(BPS):
                                for A in range(4):
                                    p = slice(32 * A, 32 * A + 32)
                                    for h in range(2):
                                        ins = pe.matmul(B[4 + A][64 * h:64 * h + 64, b * S:(b + 1) * S],
                                                        vt[p, z].rearrange("p c s -> p (c s)")[:, b * P + 64 * h:b * P + 64 * h + 64],
                                                        pt[p, z, h, b * S:(b + 1) * S], start=True, stop=True,
                                                        tile_position=(32 * A, 64 * h))
                            ins.then_inc(av_psum.sem, 1)
                        if ok(t):
                            pe.wait_ge(*kd(t + 1))
                            pe.wait_ge(*s_summed(t))
                            pe.sem_inc(sig.sems["pe_passed"], 1)
                            for b in range(BPS):
                                for c in range(4):
                                    for h in range(2):
                                        r_ = slice(64 * h, 64 * h + 64)
                                        ins = pe.matmul(B[2 + h][32 * c:32 * c + 32, b * S:(b + 1) * S],
                                                        qT[r_, q, c, b * S:(b + 1) * S], kT[r_, q, c, b * S:(b + 1) * S],
                                                        start=True, stop=True, tile_position=(64 * h, 32 * c))
                            ins.then_inc(scores.sem, 1)
                        if ok(u):
                            pe.wait_ge(*o_ready(u + 1))
                            pe.wait_ge(*a_ready(u + 1))
                            if not ok(t):
                                pe.wait_ge(*kd(u + 1))
                            pe.matmul(B[1][:, 0:P], ones_row, r("a1_bo"), start=True, stop=False)
                            for c in range(4):
                                ins = pe.matmul(B[1][:, 0:P], o[:, z, c, :], w(f"a1_o{c}"), start=False, stop=(c == 3))
                            ins.then_inc(y_psum.sem, 1)
                    run(pe, stages, 1)

                @block.scalar
                def _(act):
                    def stages(t, q, ok):
                        z = 1 - q
                        if ok(t):
                            act.wait_ge(*qp(t + 1))
                            act.wait_ge(*scores(t - 1))
                            act.activation(qT[:, q], B[0][:].rearrange("p (c s) -> p c s", c=4), ACT.Copy, scale=64 ** -0.5).then_inc(qd.sem, 1)
                            act.wait_ge(*kp(t + 1))
                            act.copy(kT[:, q], B[1][:].rearrange("p (c s) -> p c s", c=4)).then_inc(kd.sem, 1)
                        u = t - 1
                        if ok(u):
                            act.wait_ge(*av_psum(u + 1))
                            act.wait_ge(*y_psum(u - 1))
                            act.copy(o[:, z, 0, :], B[4][:, 0:P])
                            act.copy(o[:, z, 1, :], B[5][:, 0:P]).then_inc(o_ready.sem, 1)
                        if ok(t):
                            act.wait_ge(*centred(t + 1))
                            act.activation(e[:, q], e[:, q], ACT.Exp).then_inc(exp_ready.sem, 1)
                    run(act, stages, 1)

                @block.vector
                def _(dve):
                    st_ = Steps(dve, sig, "dve_step")

                    def stages(t, q, ok):
                        z = 1 - q
                        if ok(t):
                            dve.wait_ge(*vp(t + 1))
                            dve.wait_ge(*av_psum(t - 1))
                            dve.transpose(vt[:, q].rearrange("p c s -> p (c s)"), B[0][:]).then_inc(vd.sem, 1)
                        u = t - 1
                        if ok(u):
                            dve.wait_ge(*av_psum(u + 1))
                            dve.wait_ge(*y_psum(u - 1))
                            dve.tensor_copy(o[:, z, 2, :], B[6][:, 0:P])
                            dve.tensor_copy(o[:, z, 3, :], B[7][:, 0:P]).then_inc(a_ready.sem, 1)
                        if ok(t):
                            dve.wait_ge(*scores(t + 1))
                            ev = e[:, q].rearrange("p h (b k) -> p h b k", k=S)
                            for h in range(2):
                                ins = dve.tensor_tensor(ev[:, h], B[2 + h][:, 0:P].rearrange("p (b k) -> p b k", k=S),
                                                        bias[:, h, :].unsqueeze(1).to_broadcast([P, BPS, S]), ALU.add)
                                if h == 0:
                                    st_.count(ins)
                            ins.then_inc(s_summed.sem, 1)
                            dve.wait_ge(*s_summed(t + 1))
                            eg = e[:, q].rearrange("p h (b k) -> p (h b) k", k=S)
                            m = mx[:, q, :]
                            st_.link(dve.tensor_reduce(m, eg, AX.X, ALU.max))
                            dve.tensor_tensor(eg, eg, m.unsqueeze(2).to_broadcast([P, 8, S]), ALU.subtract).then_inc(centred.sem, 1)
                            dve.wait_ge(*exp_ready(t + 1))
                            st_.link(dve.tensor_reduce(m, eg, AX.X, ALU.add))
                            st_.link(dve.reciprocal(m, m))
                            st_.link(dve.tensor_tensor(eg, eg, m.unsqueeze(2).to_broadcast([P, 8, S]), ALU.mult))
                            dve.transpose(pt[:, q].rearrange("p h s -> p (h s)"), e[:, q].rearrange("p h s -> p (h s)"))\
                                .then_inc(pT_ready.sem, 1)
                        if ok(u):
                            dve.wait_ge(*y_psum(u + 1))
                            xt_ = X[:, bass.ds(u, 1), :]
                            dve.tensor_tensor(xt_, xt_, B[1][:, 0:P].unsqueeze(1), ALU.add).then_inc(x_added.sem, 1)
                    run(dve, stages, 1, st_, 10)
                    st_.close()

        def key_rows():
            with ExitStack() as c2:
                fs, tk = hold(c2, "fs", [P, KEYS]), hold(c2, "tk", [P, 2, KEYS])
                ti = c2.enter_context(nc.sbuf_tensor("ti", [P, KEYS], I32))
                row_loaded, stored = sig("row_loaded", 2), sig("stored", 3)
                a_done, b_done, c_done, ln_done = (sig(n, 1) for n in ("a_done", "b_done", "c_done", "d_done"))
                block = c2.enter_context(nc.Block())

                @block.sync
                def _(sp):
                    sp.dma_start(fs[:], T["key_weights"]).then_inc(row_loaded.sem, 16)
                    sp.dma_start(ti[:], T["key_tokens"]).then_inc(row_loaded.sem, 16)
                    sp.wait_ge(*b_done(1))
                    sp.dma_start(T["rows_x2"], fs[:]).then_inc(stored.sem, 16)
                    sp.wait_ge(*c_done(1))
                    sp.dma_start(T["rows_x3"], tk[:, 0, :]).then_inc(stored.sem, 16)
                    sp.dma_start(T["rows_keep"], tk[:, 1, :]).then_inc(stored.sem, 16)
                    sp.wait_ge(*stored(3))

                @block.scalar
                def _(act):
                    act.wait_ge(*a_done(1))
                    act.activation(fs[:], fs[:], ACT.Ln).then_inc(ln_done.sem, 1)

                @block.vector
                def _(dve):
                    st_ = Steps(dve, sig, "dve_step")
                    dve.wait_ge(*row_loaded(2))
                    st_.link(dve.tensor_scalar(fs[:], fs[:], 1e-20, None, ALU.add))
                    dve.tensor_scalar(fs[:], fs[:], 2.0 ** 40, None, ALU.mult).then_inc(a_done.sem, 1)
                    st_.link(dve.tensor_scalar(tk[:, 0, :], ti[:], 0, None, ALU.is_equal))
                    st_.link(dve.tensor_scalar(tk[:, 1, :], tk[:, 0, :], -1.0, 1.0, ALU.mult, ALU.add))
                    dve.tensor_scalar(tk[:, 0, :], tk[:, 0, :], -1.0e9 / 8 ** 0.5, None, ALU.mult).then_inc(c_done.sem, 1)
                    dve.wait_ge(*ln_done(1))
                    dve.tensor_scalar(fs[:], fs[:], -40 * 0.6931471805599453, None, ALU.add).then_inc(b_done.sem, 1)
                    st_.close()

        def xattn(name):
            bias = name != "x3"
            with ExitStack() as c2:
                def sb2(n, shape):
                    return hold(c2, n, shape)
                QT = sb2("QT", [P, TILES * P])
                project([(QT, w(name + "_q"), XNT, v(name + "_bq" if bias else "zero"), 8 ** -0.5)])
                ct = [sb2("ct", [P, KEYS]) for _ in range(4)]
                rows = [sb2("rows", [P, KEYS]) for _ in range(4)] if name != "x1" else None
                keep = [sb2("keep", [P, KEYS]) for _ in range(4)] if name == "x3" else None
                qb = sb2("qb", [P, 2, 4, S])
                kT = sb2("kT", [P, 2, KEYS])
                vs = sb2("vs", [P, 4, 2 * P])
                vl = sb2("vl", [4, 4, P])
                sx = sb2("sx", [P, 2, 4, KEYS])
                nm, sm, rs = sb2("nm", [P, 2, 4]), sb2("sm", [P, 4, 4]), sb2("rs", [P, 4])
                pt, pl = sb2("pt", [P, 2, 2, 4 * P]), sb2("pl", [4, 2, P])
                a = sb2("a", [P, 2, P])
                oT = sb2("oT", [P, P])
                maskq = sb2("maskq", [P, KEYS])
                N = NB
                per_load = 1 + (rows is not None) + (keep is not None)
                loads = [sig(f"ct_loaded{j}", per_load * N // 4) for j in range(4)]
                q_built, k_psum, kv_psum, k_ready, v_ready = (sig(n, N) for n in ("q_built", "k_psum", "kv_psum", "k_ready", "v_ready"))
                scores, s_summed, exp_done = sig("scores", 4 * N), sig("s_summed", 4 * N), sig("exp_done", N)
                pT_psum, pT_ready, av_psum, a_ready, o_ready = (
                    sig(n, N) for n in ("pT_psum", "pT_ready", "av_psum", "a_ready", "o_ready"))
                p_ready, pT2_psum, pT2_ready = (sig(n, N) for n in ("probs_ready", "pT2_psum", "pT2_ready"))
                pl_psum, pl_ready = sig("pl_psum", N), sig("pl_ready", N)
                y_psum, x_added = sig("y_psum", TILES), sig("x_added", TILES)
                row_loaded = sig("row_loaded", 4 if name == "x1" else 0)
                vs_copied = sig("v_built", N if keep is not None else 0)
                DEPTH = 4
                block = c2.enter_context(nc.Block())

                def run(eng, stages, steps=None, per=0):
                    for x in range(8):
                        stages(x, x % 4, x // 4, lambda b: 0 <= b < N)
                    with (steps.loop(2, N // 4, per) if steps else eng.Fori(2, N // 4)) as i:
                        for r_ in range(4):
                            stages(i * 4 + r_, r_, i, lambda b: True)
                    for x in range(N, N + DEPTH):
                        stages(x, x % 4, x // 4, lambda b: 0 <= b < N)

                @block.sync
                def _(sp):
                    if name == "x1":
                        for A in range(4):
                            sp.dma_start(maskq[32 * A:32 * A + 32, :], T["mask"]).then_inc(row_loaded.sem, 16)

                    def load(b, j):
                        sp.wait_ge(*kv_psum(b - 3))
                        sp.dma_start(ct[j][:], T["ctxT"].rearrange("p (b k) -> p b k", k=KEYS)[:, bass.ds(b, 1), :]
                                     .rearrange("p b k -> p (b k)")).then_inc(loads[j].sem, 16)
                        if rows is not None:
                            sp.wait_ge(*s_summed(4 * (b - 3)))
                            sp.dma_start(rows[j][:], T["rows_" + name][bass.ds(b, 1), :].to_broadcast([P, KEYS]))\
                                .then_inc(loads[j].sem, 16)
                        if keep is not None:
                            sp.wait_ge(*k_ready(b - 3))
                            sp.dma_start(keep[j][:], T["rows_keep"][bass.ds(b, 1), :].to_broadcast([P, KEYS]))\
                                .then_inc(loads[j].sem, 16)
                    with sp.Fori(0, N // 4) as i:
                        for j in range(4):
                            load(i * 4 + j, j)

                @block.gpsimd
                def _(pool):
                    def build(b, q):
                        pool.wait_ge(*scores(4 * (b - 1)))
                        pool.tensor_tensor(qb[:, q], QT[:, bass.ds(b * S, S)].unsqueeze(1).to_broadcast([P, 4, S]),
                                           const("head").unsqueeze(2).to_broadcast([P, 4, S]), ALU.mult)\
                            .then_inc(q_built.sem, 1)
                    with pool.Fori(0, N // 2) as i:
                        for q in range(2):
                            build(i * 2 + q, q)

                @block.tensor
                def _(pe):
                    def read_scores(x, n):
                        k = 4 * (x - 1) + n
                        return s_summed(max(0, min(k, 4 * N)) if isinstance(k, int) else k)

                    def stages(x, r_, i, ok):
                        b, j = x, r_
                        if ok(b):
                            pe.wait_ge(*loads[j](per_load * (i + 1)))
                            pe.wait_ge(*k_ready(b))
                            pe.wait_ge(*v_ready(b))
                            pe.matmul(B[4][:, 0:KEYS], w(name + "_k"), ct[j][:], start=True, stop=True).then_inc(k_psum.sem, 1)
                            pe.matmul(B[5][0:4, 256:384], ct[j][:, 256:257].to_broadcast([P, 4]), w(name + "_v"),
                                      start=True, stop=True)
                            for c in range(2):
                                ins = pe.matmul(B[5][:, c * P:(c + 1) * P], ct[j][:, c * P:(c + 1) * P], w(name + "_v"),
                                                start=True, stop=True)
                            ins.then_inc(kv_psum.sem, 1)
                        b, q = x - 1, (r_ - 1) % 2
                        if ok(b):
                            pe.wait_ge(*k_ready(b + 1))
                            pe.wait_ge(*q_built(b + 1))
                            for h in range(4):
                                if h == 0:
                                    pe.wait_ge(*a_ready(b - 2))
                                elif h == 2 and r_ == 0:
                                    pe.wait_ge(*x_added(i - 1))
                                elif h == 3:
                                    pe.wait_ge(*pl_ready(b - 1))
                                pe.wait_ge(*s_summed(4 * (b - 1) + h + 1))
                                p = slice(32 * h, 32 * h + 32)
                                pe.matmul(B[h][:, 0:KEYS], qb[p, q].rearrange("p j s -> p (j s)"), kT[p, q, :],
                                          start=True, stop=True, tile_position=(32 * h, 0)).then_inc(scores.sem, 1)
                        b, q = x - 2, r_ % 2
                        if ok(b):
                            pe.wait_ge(*p_ready(b + 1))
                            pe.wait_ge(*pT_ready(b))
                            pe.wait_ge(*pT2_ready(b))
                            for c in range(2):
                                for h in range(4):
                                    ins = pe.transpose(B[6 + c][:, h * P:(h + 1) * P], sx[:, q, h, c * P:(c + 1) * P], ident)
                                ins.then_inc((pT_psum if c == 0 else pT2_psum).sem, 1)
                            pe.wait_ge(*pl_ready(b))
                            pe.wait_ge(*read_scores(x, 4))
                            pe.transpose(B[3][0:4, 384:512], sx[:, q, :, 256], ident).then_inc(pl_psum.sem, 1)
                        if r_ == 3 and ok(x - 4):
                            pe.wait_ge(*o_ready(x - 3))
                            pe.wait_ge(*read_scores(x, 3))
                            pe.matmul(B[2][:, 384:512], ones_row, r(name + "_bo"), start=True, stop=False)
                            pe.matmul(B[2][:, 384:512], oT[:], w(name + "_o"), start=False, stop=True).then_inc(y_psum.sem, 1)
                        b, q = x - 3, (r_ - 3) % 2
                        if ok(b):
                            pe.wait_ge(*pT_ready(b + 1))
                            pe.wait_ge(*pT2_ready(b + 1))
                            pe.wait_ge(*pl_ready(b + 1))
                            pe.wait_ge(*a_ready(b))
                            pe.wait_ge(*read_scores(x, 1))
                            for h in range(4):
                                vj = (r_ - 3) % 4
                                out_h = B[0][32 * h:32 * h + 32, 384:512]
                                for c in range(2):
                                    pe.matmul(out_h, vs[:, vj, c * P + 32 * h:c * P + 32 * h + 32],
                                              pt[:, q, c, h * P:(h + 1) * P], start=(c == 0), stop=False,
                                              tile_position=(0, 32 * h))
                                ins = pe.matmul(out_h, vl[:, vj, 32 * h:32 * h + 32], pl[:, q, :], start=False, stop=True,
                                                tile_position=(0, 32 * h))
                            ins.then_inc(av_psum.sem, 1)
                    run(pe, stages)

                @block.scalar
                def _(act):
                    def stages(x, r_, i, ok):
                        b, q, j = x, r_ % 2, r_
                        if ok(b):
                            if keep is None:
                                act.wait_ge(*k_psum(b + 1))
                                act.wait_ge(*scores(4 * (b - 1)))
                                act.activation(kT[:, q, :], B[4][:, 0:KEYS], ACT.Identity, bias=v(name + "_bk")).then_inc(k_ready.sem, 1)
                            else:
                                act.wait_ge(*kv_psum(b + 1))
                                act.wait_ge(*av_psum(b - 3))
                                act.copy(vs[:, j, :], B[5][:, 0:2 * P]).then_inc(vs_copied.sem, 1)
                        b, q = x - 1, (r_ - 1) % 2
                        if ok(b):
                            for h in range(4):
                                act.wait_ge(*s_summed(4 * b + h + 1))
                                ins = act.activation(sx[:, q, h, :], sx[:, q, h, :], ACT.Exp, bias=nm[:, q, h:h + 1], scale=-1.0,
                                                     accum_out=sm[:, (r_ - 1) % 4, h:h + 1])
                            ins.then_inc(exp_done.sem, 1)
                        b, q = x - 2, r_ % 2
                        if ok(b):
                            act.wait_ge(*pT2_psum(b + 1))
                            act.wait_ge(*av_psum(b - 1))
                            act.copy(pt[:, q, 1, :], B[7][:]).then_inc(pT2_ready.sem, 1)
                    run(act, stages)

                @block.vector
                def _(dve):
                    st_ = Steps(dve, sig, "dve_step")
                    if name == "x1":
                        dve.wait_ge(*row_loaded(4))
                        st_.link(dve.tensor_scalar(maskq[:], maskq[:], -1.0e9, None, ALU.mult))

                    def stages(x, r_, i, ok):
                        b, q, j = x - 2, r_ % 2, (r_ - 2) % 4
                        if ok(b):
                            dve.wait_ge(*exp_done(b + 1))
                            st_.link(dve.reciprocal(rs[:], sm[:, j, :]))
                            for h in range(4):
                                ins = dve.tensor_scalar(sx[:, q, h, :], sx[:, q, h, :], rs[:, h:h + 1], None, ALU.mult)
                            ins.then_inc(p_ready.sem, 1)
                        b, q, j = x, r_ % 2, r_
                        if ok(b):
                            if keep is not None:
                                dve.wait_ge(*k_psum(b + 1))
                                dve.wait_ge(*scores(4 * (b - 1)))
                                dve.tensor_tensor(kT[:, q, :], B[4][:, 0:KEYS], keep[j][:], ALU.mult).then_inc(k_ready.sem, 1)
                            dve.wait_ge(*kv_psum(b + 1))
                            dve.wait_ge(*av_psum(b - 3))
                            if keep is None:
                                st_.count(dve.tensor_copy(vs[:, j, :], B[5][:, 0:2 * P]))
                                st_.wait()
                            else:
                                dve.wait_ge(*vs_copied(b + 1))
                            dve.tensor_tensor(vl[:, j, :], B[5][0:4, 256:384], const("mask4")[0:4, :], ALU.mult)\
                                .then_inc(v_ready.sem, 1)
                        b, q, j = x - 1, (r_ - 1) % 2, (r_ - 1) % 4
                        if ok(b):
                            dve.wait_ge(*pl_psum(b - 1))
                            add = maskq[:] if rows is None else rows[j][:]
                            for h in range(4):
                                dve.wait_ge(*scores(4 * b + h + 1))
                                dve.sem_inc(sig.sems["dve_passed"], 1)
                                dve.tensor_tensor_reduce(sx[:, q, h, :], B[h][:, 0:KEYS], add, -1.0, 3.0e38, ALU.add, ALU.min,
                                                         nm[:, q, h:h + 1]).then_inc(s_summed.sem, 1)
                        b, q = x - 3, (r_ - 3) % 2
                        if ok(b):
                            dve.wait_ge(*av_psum(b + 1))
                            dve.scalar_tensor_tensor(out=a[:, q].rearrange("p (j s) -> p j s", j=4),
                                                     in0=B[0][:, 384:512].rearrange("p (j s) -> p j s", j=4),
                                                     scalar=v(name + "_bv" if bias else "zero"),
                                                     in1=const("head").unsqueeze(2).to_broadcast([P, 4, S]),
                                                     op0=ALU.add, op1=ALU.mult).then_inc(a_ready.sem, 1)
                            dve.wait_ge(*a_ready(b + 1))
                            if r_ == 3:
                                dve.wait_ge(*y_psum(i))
                            dve.tensor_reduce(oT[:, ((r_ - 3) % 4) * S:((r_ - 3) % 4) * S + S],
                                              a[:, q].rearrange("p (j s) -> p s j", j=4), AX.X, ALU.add)\
                                .then_inc(o_ready.sem, 1)
                        b, q = x - 2, r_ % 2
                        if ok(b):
                            dve.wait_ge(*pl_psum(b + 1))
                            dve.wait_ge(*av_psum(b - 1))
                            dve.tensor_copy(pl[:, q, :], B[3][0:4, 384:512]).then_inc(pl_ready.sem, 1)
                            dve.wait_ge(*pT_psum(b + 1))
                            dve.tensor_copy(pt[:, q, 0, :], B[6][:]).then_inc(pT_ready.sem, 1)
                        if r_ == 3 and ok(x - 4):
                            dve.wait_ge(*y_psum(i))
                            xt_ = X[:, bass.ds(i - 1, 1), :]
                            dve.tensor_tensor(xt_, xt_, B[2][:, 384:512].unsqueeze(1), ALU.add).then_inc(x_added.sem, 1)
                    run(dve, stages, st_, 4 * (2 if keep is None else 1))
                    st_.close()

        def butterfly_ffn():
            H2 = 512
            with ExitStack() as c2:
                def sb2(n, shape):
                    return hold(c2, n, shape)
                W1, W2, B1 = sb2("W1", [P, 1, H2]), sb2("W2", [P, 1, 4, P]), sb2("B1", [P, 1, 4])
                with ExitStack() as c3:
                    wu, wd = (hold(c3, n, [P, 9, 2 * H2]) for n in ("wu", "wd"))
                    U = hold(c3, "U", [P, 2, H2])
                    D = hold(c3, "D", [P, H2])
                    tu = [hold(c3, "tu", [P, 2, H2 // 2]) for _ in range(4)]
                    td_ = [hold(c3, "td", [P, H2 // 2]) for _ in range(4)]
                    both = hold(c3, "both", [P, P])
                    w_loaded = sig("w_loaded", 5)
                    a_done, b_done, c_done, d_done = (sig(n, 1) for n in ("a_done", "b_done", "c_done", "d_done"))
                    copied = sig("copied", 1)
                    block = c3.enter_context(nc.Block())

                    @block.sync
                    def _(sp):
                        sp.wait_ge(*copied(1))
                        sp.dma_start(U[:, 0, :], T["W_exp"]).then_inc(w_loaded.sem, 16)
                        sp.dma_start(U[0:1, 1, :], T["b_exp"]).then_inc(w_loaded.sem, 16)
                        sp.dma_start(D[:], T["W_conT"]).then_inc(w_loaded.sem, 16)
                        sp.dma_start(wu[:], T["up_w"].rearrange("s n -> (s n)").unsqueeze(0).to_broadcast([P, 9 * 2 * H2])
                                     .rearrange("p (s n) -> p s n", s=9)).then_inc(w_loaded.sem, 16)
                        sp.dma_start(wd[:], T["down_w"].rearrange("s n -> (s n)").unsqueeze(0).to_broadcast([P, 9 * 2 * H2])
                                     .rearrange("p (s n) -> p s n", s=9)).then_inc(w_loaded.sem, 16)

                    def weights_of(wt, s, st):
                        return wt[:, s, :].rearrange("p (n t i j) -> p n t i j", t=st, i=2, j=2)

                    @block.vector
                    def _(dve):
                        st_ = Steps(dve, sig, "dve_step")
                        dve.memset(U[:, 1, :], 0.0).then_inc(copied.sem, 1)
                        dve.wait_ge(*w_loaded(5))
                        for s in range(9):
                            st = 1 << s
                            n = H2 // (2 * st)
                            u = U[:].rearrange("p c (n i t) -> p c n i t", i=2, t=st)
                            ww = weights_of(wu, s, st)
                            for k in range(4):
                                o, i = k // 2, k % 2
                                for c in range(2):
                                    st_.count(dve.tensor_tensor(
                                        tu[k][:, c, :].rearrange("p (n t) -> p n t", t=st), u[:, c, :, i, :], ww[:, :, :, o, i], ALU.mult))
                            st_.wait()
                            for o in range(2):
                                for c in range(2):
                                    st_.count(dve.tensor_tensor(
                                        u[:, c, :, o, :], tu[2 * o][:, c, :].rearrange("p (n t) -> p n t", t=st),
                                        tu[2 * o + 1][:, c, :].rearrange("p (n t) -> p n t", t=st), ALU.add))
                            st_.wait()
                        dve.tensor_copy(W1[:, 0, :], U[:, 0, :]).then_inc(a_done.sem, 1)
                        dve.wait_ge(*b_done(1))
                        st_.count(dve.tensor_tensor(B1[:, 0, :], B[1][:, 0:4], V[:, VAT["up_b0"]:VAT["up_b0"] + 4], ALU.add))
                        st_.link(dve.tensor_copy(both[:], B[2][:, 0:P]))
                        st_.count(dve.tensor_tensor(X[:], X[:], both[:].unsqueeze(1).to_broadcast([P, TILES, P]), ALU.add))
                        dve.wait_ge(*d_done(1))
                        st_.count(dve.tensor_copy(W2[:, 0].rearrange("p c n -> p (c n)"), B[0][:]))
                        st_.wait()
                        st_.close()

                    @block.gpsimd
                    def _(pool):
                        st_ = Steps(pool, sig, "pool_step")
                        pool.wait_ge(*w_loaded(5))
                        for s in reversed(range(9)):
                            st = 1 << s
                            d = D[:].rearrange("p (n i t) -> p n i t", i=2, t=st)
                            ww = weights_of(wd, s, st)
                            for k in range(4):
                                o, i = k // 2, k % 2
                                st_.count(pool.tensor_tensor(td_[k][:].rearrange("p (n t) -> p n t", t=st), d[:, :, i, :],
                                                             ww[:, :, :, i, o], ALU.mult))
                            st_.wait()
                            for o in range(2):
                                st_.count(pool.tensor_tensor(d[:, :, o, :], td_[2 * o][:].rearrange("p (n t) -> p n t", t=st),
                                                             td_[2 * o + 1][:].rearrange("p (n t) -> p n t", t=st), ALU.add))
                            st_.wait()
                        st_.close()
                        pool.sem_inc(c_done.sem, 1)

                    @block.tensor
                    def _(pe):
                        pe.matmul(B[2][:, 0:P], ones_row, r("b_con"), start=True, stop=False)
                        pe.matmul(B[2][:, 0:P], ones_row, r("down_bias"), start=False, stop=True)
                        pe.wait_ge(*a_done(1))
                        for c in range(4):
                            ins = pe.matmul(B[1][:, c:c + 1], U[0:1, 1, c * P:(c + 1) * P], ones_row[:, 0:1], start=True, stop=True)
                        ins.then_inc(b_done.sem, 1)
                        pe.wait_ge(*c_done(1))
                        for c in range(4):
                            ins = pe.transpose(B[0][:, c * P:(c + 1) * P], D[:, c * P:(c + 1) * P], ident)
                        ins.then_inc(d_done.sem, 1)
                experts(1, 4, X, None, None, None, None, ready=(W1, W2, B1))

        def norm_affine_add(Y):
            with ExitStack() as c2:
                def sb2(n, shape):
                    return hold(c2, n, shape)
                st, var, dif = sb2("stats", [P, TILES, 6]), sb2("var", [P, TILES]), sb2("dif", [P, TILES])
                gb = sb2("gb", [P, 2, P])
                yn = sb2("yn", [P, 2, GT, P])
                var_ready, rstd_ready, a_done = sig("var_ready", 1), sig("rstd_ready", 1), sig("a_done", 1)
                x_added, stored = sig("x_added", 8), sig("stored", 8)
                block = c2.enter_context(nc.Block())

                @block.tensor
                def _(pe):
                    pe.matmul(B[0][:, 0:P], ones_row, r("gamma"), start=True, stop=True)
                    pe.matmul(B[0][:, P:2 * P], ones_row, r("beta"), start=True, stop=True).then_inc(a_done.sem, 1)

                @block.scalar
                def _(act):
                    st_ = Steps(act, sig, "act_step")
                    act.wait_ge(*var_ready(1))
                    st_.link(act.activation(var[:], var[:], ACT.Ln))
                    act.activation(rstd[:], var[:], ACT.Exp, scale=-0.5).then_inc(rstd_ready.sem, 1)
                    st_.close()

                @block.vector
                def _(dve):
                    st_ = Steps(dve, sig, "dve_step")
                    with st_.loop(0, GROUPS, GT) as g:
                        for j in range(GT):
                            st_.count(dve.bn_stats(st[:, bass.ds(g * GT + j, 1), :], Y[:, bass.ds(g * GT + j, 1), :]))
                    dve.wait_ge(*a_done(1))
                    st_.count(dve.tensor_copy(gb[:].rearrange("p a b -> p (a b)"), B[0][:, 0:2 * P]))
                    st_.wait()
                    st_.count(dve.tensor_tensor(mean[:], st[:, :, 1], st[:, :, 4], ALU.add))
                    st_.count(dve.tensor_tensor(dif[:], st[:, :, 1], st[:, :, 4], ALU.subtract))
                    st_.link(dve.tensor_tensor(var[:], st[:, :, 2], st[:, :, 5], ALU.add))
                    st_.count(dve.tensor_scalar(mean[:], mean[:], 0.5, None, ALU.mult))
                    st_.count(dve.tensor_scalar(var[:], var[:], 1.0 / P, EPS, ALU.mult, ALU.add))
                    st_.link(dve.tensor_tensor(dif[:], dif[:], dif[:], ALU.mult))
                    dve.scalar_tensor_tensor(out=var[:], in0=dif[:], scalar=0.25, in1=var[:],
                                             op0=ALU.mult, op1=ALU.add).then_inc(var_ready.sem, 1)
                    dve.wait_ge(*rstd_ready(1))
                    with st_.loop(0, GROUPS // 2, 12) as i:
                        for q in range(2):
                            g = i * 2 + q
                            for j in range(GT):
                                t = g * GT + j
                                st_.count(dve.tensor_scalar(yn[:, q, j, :], Y[:, bass.ds(t, 1), :], mean[:, bass.ds(t, 1)],
                                                            rstd[:, bass.ds(t, 1)], ALU.subtract, ALU.mult))
                            st_.wait()
                            st_.link(dve.tensor_tensor(yn[:, q], yn[:, q], gb[:, 0, :].unsqueeze(1).to_broadcast([P, GT, P]), ALU.mult))
                            st_.link(dve.tensor_tensor(yn[:, q], yn[:, q], gb[:, 1, :].unsqueeze(1).to_broadcast([P, GT, P]), ALU.add))
                            xg = X[:, bass.ds(g * GT, GT), :]
                            dve.tensor_tensor(xg, xg, yn[:, q], ALU.add).then_inc(x_added.sem, 1)
                    st_.close()

                @block.sync
                def _(sp):
                    with sp.Fori(0, GROUPS) as g:
                        sp.wait_ge(*x_added(g + 1))
                        sp.dma_start(ot[:, bass.ds(g * GT, GT), :], X[:, bass.ds(g * GT, GT), :]).then_inc(stored.sem, 16)
                    sp.wait_ge(*stored(8))

        with ExitStack() as c0:
            ctx0 = hold(c0, "ctx0", [P, TILES * P])
            ctx_loaded = sig("ctx_loaded", 1)
            with nc.Block() as block:
                @block.sync
                def _(sp):
                    sp.dma_start(ctx0[:], T["ctx_causal"]).then_inc(ctx_loaded.sem, 16)
                    sp.wait_ge(*ctx_loaded(1))
            norm()
            attn16("x0", ctx0, "x0_bv", "x0_bo", True)
        norm()
        rwkv()
        norm(add_back=True)
        with ExitStack() as c0:
            Cmb = hold(c0, "Cmb", [P, TILES, 24])
            route("pairs", Cmb, 24, GW0[:], GB[:])
            expert_bias(Cmb, 24, T["L0_b2"])
            experts(24, 4, X, Cmb, T["L0_w1"], T["L0_b1"], T["L0_w2"])

        key_rows()
        norm()
        xattn("x1")
        norm()
        attn8()
        norm()
        butterfly_ffn()
        norm()
        xattn("x2")
        norm()
        rglru()
        norm()
        with ExitStack() as c0:
            Cmb = hold(c0, "Cmb", [P, TILES, 9])
            route("capacity", Cmb, 8, GW2[:])
            expert_bias(Cmb, 9, T["L2_b2"])
            experts(9, 4, X, Cmb, T["L2_w1"], T["L2_b1"], T["L2_w2"])
        norm()
        xattn("x3")
        norm()
        attn16("a3", XNT, "a3_bv", "a3_bo", False)
        norm()
        with ExitStack() as c0:
            Cmb, Y = hold(c0, "Cmb", [P, TILES, 8]), hold(c0, "Y", [P, TILES, P])
            with nc.Block() as block:
                @block.vector
                def _(dve):
                    dve.memset(Y[:], 0.0)
            route("first", Cmb, 8, GW3[:])
            experts(8, 2, Y, Cmb, T["L3_w1"], T["L3_b1"], T["L3_w2"])
            norm_affine_add(Y)


def layout(inputs):
    import numpy as np
    a = {k: np.asarray(x) for k, x in inputs.items()}
    f = np.float32
    out = {"x": a["x"]}
    ctxT = np.ascontiguousarray(np.transpose(a["ctx_1024"], (2, 0, 1)))
    out["ctxT"] = ctxT.reshape(P, NB * KEYS)
    out["ctx_causal"] = np.ascontiguousarray(ctxT[:, :, :S]).reshape(P, NB * S)
    ws = {}
    for n in "qkvo":
        ws["x0_" + n] = a["L0_xattn_W" + n].T
        ws["x2_" + n] = a["L2_xattn_w" + n]
        ws["x3_" + n] = a["L3_xattn_W" + n]
    ws["a0_v"], ws["a0_r"], ws["a0_o"] = a["L0_attn_value_w"].T, a["L0_attn_recep_w"].T, a["L0_attn_out_w"].T
    for n in "qkv":
        ws["x1_" + n] = a[f"L1_xattn_w{n}_w"].T
    ws["x1_o"] = a["L1_xattn_dense_w"].T
    for i, n in enumerate("qkv"):
        ws["a3_" + n] = a["L3_attn_in_proj_w"][i * P:(i + 1) * P].T
    ws["a3_o"] = a["L3_attn_out_proj_w"].T
    for n, k in (("a2_i", "L2_attn_ig_w"), ("a2_a", "L2_attn_ag_w")):
        bd = np.zeros((P, P), f)
        for h in range(8):
            bd[16 * h:16 * h + 16, 16 * h:16 * h + 16] = a[k][h]
        ws[n] = bd
    for c in range(4):
        ws[f"a1_q{c}"] = a["L1_attn_Wq"][:, c * P:(c + 1) * P]
        ws[f"a1_k{c}"] = a["L1_attn_Wkv"][:, c * P:(c + 1) * P]
        ws[f"a1_v{c}"] = a["L1_attn_Wkv"][:, 512:].reshape(P, 4, 4, 32)[:, :, c, :].reshape(P, P)
        ws[f"a1_o{c}"] = a["L1_attn_Wo"][c * P:(c + 1) * P, :]
    out["weights"] = np.ascontiguousarray(np.stack([ws[n] for n in SLOTS], axis=1))
    z = np.zeros(P, f)
    vs = {"x0_bq": a["L0_xattn_bq"], "x0_bk": a["L0_xattn_bk"], "x0_bv": a["L0_xattn_bv"],
          "x1_bq": a["L1_xattn_wq_b"], "x1_bk": a["L1_xattn_wk_b"], "x1_bv": a["L1_xattn_wv_b"],
          "x2_bq": a["L2_xattn_bq"], "x2_bk": a["L2_xattn_bk"], "x2_bv": a["L2_xattn_bv"],
          "a3_bq": a["L3_attn_in_proj_b"][:P], "a3_bk": a["L3_attn_in_proj_b"][P:2 * P],
          "a3_bv": a["L3_attn_in_proj_b"][2 * P:], "zero": z, "time_decay": a["L0_attn_time_decay"],
          "time_first": a["L0_attn_time_first"], "a_param": a["L2_attn_a_param"],
          "ig_b": a["L2_attn_ig_b"].reshape(P), "ag_b": a["L2_attn_ag_b"].reshape(P)}
    for c in range(4):
        vs[f"up_b{c}"] = a["L1_ffn_up_bias"][c * P:(c + 1) * P]
    out["vecs"] = np.ascontiguousarray(np.stack([vs[n] for n in VECS], axis=1))
    rs = {"x0_bo": a["L0_xattn_bo"], "x1_bo": a["L1_xattn_dense_b"], "a1_bo": a["L1_attn_bo"],
          "x2_bo": a["L2_xattn_bo"], "x3_bo": a["L3_xattn_bo"], "a3_bo": a["L3_attn_out_proj_b"],
          "b_con": a["L1_ffn_b_con"], "down_bias": a["L1_ffn_down_bias"], "gamma": a["L3_ffn_ln_gamma"],
          "beta": a["L3_ffn_ln_beta"], "zero": z}
    out["rows"] = np.ascontiguousarray(np.stack([rs[n] for n in ROWS], axis=0))[None]
    p = np.arange(P)
    cs = {"ident": np.eye(P), "group": p[:, None] // 32 == np.arange(4), "head": p[:, None] % 32 // 8 == np.arange(4),
          "quarter": p[:, None] // 32 == np.arange(4),
          "sel": p[:, None] % 32 == np.arange(32), "later": np.arange(32)[None] > p[:, None] % 32,
          "rev": np.tile(24 - np.arange(24), (P, 1)), "upto": p[:, None] <= p[None], "ones": np.ones((P, P)),
          "mask4": p[:, None] == p[None] // 32,
          "diag512": np.repeat(p[:, None] % 32 // 8 == np.arange(4), P, axis=1)}
    out["consts"] = np.concatenate([cs[n].astype(f) for n in CONSTS], axis=1)
    out["gate0"], out["gate0_b"] = a["L0_ffn_gate_w"], a["L0_ffn_gate_b"][None]
    out["gate2"], out["gate3"] = a["L2_ffn_Wr"], np.ascontiguousarray(a["L3_ffn_gate_w"].T)
    out["L0_w1"], out["L0_w2"], out["L0_b2"] = a["L0_ffn_w1"], a["L0_ffn_w2"], a["L0_ffn_b2"]
    out["L0_b1"] = np.ascontiguousarray(a["L0_ffn_b1"].reshape(24, 4, P).transpose(0, 2, 1))
    out["L2_w1"] = np.concatenate([a["L2_ffn_W1"], a["L2_ffn_fw1"][None]])
    out["L2_w2"] = np.concatenate([a["L2_ffn_W2"], a["L2_ffn_fw2"][None]])
    out["L2_b2"] = np.concatenate([a["L2_ffn_b2"], a["L2_ffn_fb2"][None]])
    out["L2_b1"] = np.ascontiguousarray(np.concatenate([a["L2_ffn_b1"], a["L2_ffn_fb1"][None]]).reshape(9, 4, P).transpose(0, 2, 1))
    out["L3_w1"], out["L3_w2"] = a["L3_ffn_expert_w1"], a["L3_ffn_expert_w2"]
    out["key_weights"] = a["fside_BxS2_0"]
    out["key_tokens"] = a["itok_BxS2_0_99"]
    out["mask"] = a["mask_1x1xSxS2_fk1"].reshape(S, KEYS)
    out["rel_emb"] = a["L1_attn_rel_emb"]
    n = np.maximum(np.arange(S)[None, :] - np.arange(S)[:, None], 0)
    large = 16 + (np.log(np.maximum(n, 1) / 16) / np.log(128 / 16) * 16).astype(int)
    bucket = np.where(n < 16, n, np.minimum(large, 31))
    hot = (np.arange(32)[:, None, None] == bucket[None]).astype(f)
    out["buckets"] = np.tile(hot[:, :, None, :], (1, 1, 4, 1)).reshape(32, S * P)
    out["W_exp"], out["b_exp"] = a["L1_ffn_W_exp"], a["L1_ffn_b_exp"][None]
    out["W_conT"] = np.ascontiguousarray(a["L1_ffn_W_con"].T)
    out["up_w"], out["down_w"] = a["L1_ffn_up_weights"].reshape(9, 1024), a["L1_ffn_down_weights"].reshape(9, 1024)
    out["L3_b1"] = np.zeros((8, P, 2), f)
    return out


def kernel(**inputs):
    import numpy as np
    import concourse.bacc as bacc
    from concourse.bass_utils import run_bass_kernel_spmd

    nc = bacc.Bacc("TRN2", target_bir_lowering=False, num_devices=1)
    arrays = layout(inputs)
    T = {}
    feed = {}
    for name, a in arrays.items():
        a = np.ascontiguousarray(a)
        feed[f"in_{name}"] = a
        T[name] = nc.dram_tensor(f"in_{name}", a.shape, mybir.dt.from_np(a.dtype), kind="ExternalInput").ap()
    for name in ("rows_x2", "rows_x3", "rows_keep"):
        T[name] = nc.dram_tensor(name, (NB, KEYS), F32).ap()
    out = nc.dram_tensor("out_0", (NB, S, P), F32, kind="ExternalOutput").ap()
    program(nc, T, out)
    r = run_bass_kernel_spmd(nc, [feed], core_ids=[0])
    return r.results[0]["out_0"]
```

```python
from contextlib import ExitStack

import concourse.bass as bass
from concourse import mybir

F32 = mybir.dt.float32
I32 = mybir.dt.int32
ACT = mybir.ActivationFunctionType
ALU = mybir.AluOpType
AX = mybir.AxisListType

P = 128
NB = 128
S = 32
KEYS = 257
TILES = NB * S // P
BPT = P // S
GT = 4
GW = GT * P
GROUPS = TILES // GT
HEADS = 16
EPS = 1e-5
MAX_BLOCKS = 2 * TILES + 24 - 1
CAP = 320
MASKED = -1.0e30

SLOTS = ["x0_q", "x0_k", "x0_v", "x0_o", "a0_v", "a0_r", "a0_o", "x1_q", "x1_k", "x1_v", "x1_o",
         "x2_q", "x2_k", "x2_v", "x2_o", "a2_i", "a2_a", "x3_q", "x3_k", "x3_v", "x3_o",
         "a3_q", "a3_k", "a3_v", "a3_o"] + [f"a1_{n}{c}" for n in "qkvo" for c in range(4)]
WAT = {n: i for i, n in enumerate(SLOTS)}
VECS = ["x0_bq", "x0_bk", "x0_bv", "x1_bq", "x1_bk", "x1_bv", "x2_bq", "x2_bk", "x2_bv",
        "a3_bq", "a3_bk", "a3_bv", "zero", "time_decay", "time_first", "a_param", "ig_b", "ag_b",
        "up_b0", "up_b1", "up_b2", "up_b3"]
VAT = {n: i for i, n in enumerate(VECS)}
ROWS = ["x0_bo", "x1_bo", "a1_bo", "x2_bo", "x3_bo", "a3_bo", "b_con", "down_bias", "gamma", "beta", "zero"]
RAT = {n: i for i, n in enumerate(ROWS)}
CONSTS = {"ident": 128, "group": 4, "head": 4, "later": 32, "rev": 24, "upto": 128,
          "ones": 128, "mask4": 128, "diag512": 512, "multiples": 32, "spare": 32, "block_no": MAX_BLOCKS}
CAT = {}
_at = 0
for _n, _w in CONSTS.items():
    CAT[_n] = (_at, _at + _w)
    _at += _w
NCONST = _at

DMA_SIGNALS = ["loaded", "ctx_loaded", "row_loaded", "w_loaded", "w_loaded0", "w_loaded1", "ct_loaded0", "ct_loaded1", "ct_loaded2",
               "ct_loaded3", "stored", "stored0", "stored1", "stored2", "stored3"]
POOL_DMA_SIGNALS = ["cleared", "rows_sent", "rows_back0", "rows_back1"]
SIGNALS = ["dve_passed", "pe_passed", "act_passed", "dve_step", "act_step", "pool_step",
           "var_ready", "rstd_ready", "xn_ready", "xnT_psum", "xnT_ready",
           "proj_psum0", "proj_psum1", "proj_psum2", "proj_done0", "proj_done1", "proj_done2",
           "q_built", "v_turned", "v_built", "scores", "centred", "exp_ready", "sums_ready", "probs_ready", "pT_ready",
           "av_psum", "heads_ready", "y_psum", "x_added",
           "kv_psum", "k_psum", "k_ready", "v_ready", "s_summed", "exp_done", "pT_psum", "a_ready",
           "o_ready", "pl_psum", "pl_ready", "pT2_psum", "pT2_ready",
           "up_psum", "gelu_ready", "down_psum", "copied", "logits", "stage_ready",
           "c_turned", "c_ready", "x_turned", "xT_ready", "u_psum", "u_ready", "uT_psum", "h_ready", "yb_psum", "yb_ready", "scan_ready", "a_done", "b_done", "c_done", "d_done", "e_done"]


class Signal:

    def __init__(self, sem, base, unit):
        self.sem, self.base, self.unit = sem, base, unit

    def __call__(self, k):
        return self.sem, self.base + k * self.unit


class Signals:

    CREDIT = 16

    def __init__(self, ctx, nc):
        self.sems = {n: ctx.enter_context(nc.semaphore(n)) for n in SIGNALS + DMA_SIGNALS + POOL_DMA_SIGNALS}
        self.unit = {n: 1 if n in SIGNALS else 16 for n in self.sems}
        self.credit = {n: 0 if n in POOL_DMA_SIGNALS else self.CREDIT * self.unit[n] for n in self.sems}
        self.total = dict(self.credit)

    def __call__(self, name, times):
        s = Signal(self.sems[name], self.total[name], self.unit[name])
        self.total[name] += times * self.unit[name]
        return s


class Steps:

    def __init__(self, eng, signals, name):
        self.eng, self.signals, self.name = eng, signals, name
        self.base, self.k = signals.total[name], 0

    def link(self, ins):
        self.k += 1
        ins.then_inc(self.signals.sems[self.name], 1)
        self.eng.wait_ge(self.signals.sems[self.name], self.base + self.k)

    def count(self, ins):
        self.k += 1
        ins.then_inc(self.signals.sems[self.name], 1)

    def wait(self):
        self.eng.wait_ge(self.signals.sems[self.name], self.base + self.k)

    def loop(self, start, stop, per):
        return _StepLoop(self, start, stop, per)

    def close(self):
        self.signals.total[self.name] = self.base + self.k


class _StepLoop:
    def __init__(self, steps, start, stop, per):
        self.s, self.start, self.stop, self.per = steps, start, stop, per

    def __enter__(self):
        self.fori = self.s.eng.Fori(self.start, self.stop)
        i = self.fori.__enter__()
        self.b0, self.k0 = self.s.base, self.s.k
        self.s.base, self.s.k = (i - self.start) * self.per + (self.b0 + self.k0), 0
        return i

    def __exit__(self, *a):
        r = self.fori.__exit__(*a)
        assert a[0] is not None or self.s.k == self.per, f"the body links {self.s.k}, not {self.per}"
        self.s.base, self.s.k = self.b0, self.k0 + (self.stop - self.start) * self.per
        return r


def program(nc, T, out):
    with ExitStack() as ctx:
        def sb(name, shape, dt=F32):
            return ctx.enter_context(nc.sbuf_tensor(name, shape, dt))

        sig = Signals(ctx, nc)
        B = [ctx.enter_context(nc.psum_tensor(f"bank{i}", [P, 512], F32)) for i in range(8)]
        X = sb("X", [P, TILES, P])
        XNT = sb("XNT", [P, TILES * P])
        W = sb("W", [P, len(SLOTS), P])
        V = sb("V", [P, len(VECS)])
        R = sb("R", [1, len(ROWS), P])
        C = sb("C", [P, NCONST])
        GW0, GW2, GW3 = sb("GW0", [P, 24]), sb("GW2", [P, 8]), sb("GW3", [P, 8])
        GB = sb("GB", [1, 24])
        mean = sb("mean", [P, TILES])
        rstd = sb("rstd", [P, TILES])

        names = {}

        def hold(scope, name, shape):
            names[name] = names.get(name, 0) + 1
            return scope.enter_context(nc.sbuf_tensor(f"{name}_{names[name]}", shape, F32))

        def const(name):
            return C[:, CAT[name][0]:CAT[name][1]]

        def w(name):
            return W[:, WAT[name], :]

        def v(name):
            return V[:, VAT[name]:VAT[name] + 1]

        def r(name):
            return R[0:1, RAT[name], :]

        ident = const("ident")
        ones_row = C[0:1, CAT["ones"][0]:CAT["ones"][0] + P]
        xt = T["x"].rearrange("(t b) s d -> (b s) t d", b=BPT)
        ot = out.rearrange("(t b) s d -> (b s) t d", b=BPT)

        loaded, rest_loaded, cleared = sig("loaded", 2), sig("w_loaded1", 7), sig("cleared", 1)
        zeros = sb("zeros", [P, P])
        with nc.Block() as block:
            @block.sync
            def _(sp):
                for dst, src in ((X, xt), (C, T["consts"])):
                    sp.dma_start(dst[:], src).then_inc(loaded.sem, 16)
                for dst, src in ((W, T["weights"]), (V, T["vecs"]), (R, T["rows"]), (GW0, T["gate0"]), (GB, T["gate0_b"]),
                                 (GW2, T["gate2"]), (GW3, T["gate3"])):
                    sp.dma_start(dst[:], src).then_inc(rest_loaded.sem, 16)
                for n, s in sig.sems.items():
                    if sig.credit[n] and n != "loaded":
                        sp.sem_inc(s, sig.credit[n])
                sp.sem_inc(sig.sems["loaded"], sig.credit["loaded"])
                sp.wait_ge(*loaded(2))

            @block.gpsimd
            def _(pool):
                st_ = Steps(pool, sig, "pool_step")
                pool.wait_ge(*loaded(2))
                st_.link(pool.memset(zeros[:], 0.0))
                pool.dma_start(T["pair_rows"].rearrange("(j p) d -> p j d", p=P)[:, 0:MAX_BLOCKS, :],
                               zeros[:].unsqueeze(1).to_broadcast([P, MAX_BLOCKS, P])).then_inc(cleared.sem, 16)
                st_.close()

        def norm(add_back=False, XN=None, fetch=None):
            with ExitStack() as c2:
                st = hold(c2, "stats", [P, TILES, 6])
                var = hold(c2, "var", [P, TILES])
                dif = hold(c2, "dif", [P, TILES])
                xn = hold(c2, "xn", [P, 2, GT, P])
                var_ready, rstd_ready = sig("var_ready", 1), sig("rstd_ready", 1)
                xn_ready, xnT_psum, xnT_ready = sig("xn_ready", 8), sig("xnT_psum", 8), sig("xnT_ready", 8)
                kept = sig("copied", 8 if XN is not None else 0)
                block = c2.enter_context(nc.Block())

                if fetch:
                    @block.sync
                    def _(sp):
                        fetch(sp)

                if XN is not None:
                    @block.gpsimd
                    def _(pool):
                        with pool.Fori(0, GROUPS // 2) as i:
                            for q in range(2):
                                g = i * 2 + q
                                pool.wait_ge(*xn_ready(g + 1))
                                pool.tensor_copy(XN[:, bass.ds(g * GT, GT), :], xn[:, q]).then_inc(kept.sem, 1)

                @block.vector
                def _(dve):
                    st_ = Steps(dve, sig, "dve_step")
                    with st_.loop(0, 2, TILES // 2) as i:
                        for j in range(TILES // 2):
                            t = i * (TILES // 2) + j
                            st_.count(dve.bn_stats(st[:, bass.ds(t, 1), :], X[:, bass.ds(t, 1), :]))
                    st_.wait()
                    st_.count(dve.tensor_tensor(mean[:], st[:, :, 1], st[:, :, 4], ALU.add))
                    st_.count(dve.tensor_tensor(dif[:], st[:, :, 1], st[:, :, 4], ALU.subtract))
                    st_.link(dve.tensor_tensor(var[:], st[:, :, 2], st[:, :, 5], ALU.add))
                    st_.count(dve.tensor_scalar(mean[:], mean[:], 0.5, None, ALU.mult))
                    st_.count(dve.tensor_scalar(var[:], var[:], 1.0 / P, EPS, ALU.mult, ALU.add))
                    st_.link(dve.tensor_tensor(dif[:], dif[:], dif[:], ALU.mult))
                    st_.close()
                    dve.scalar_tensor_tensor(out=var[:], in0=dif[:], scalar=0.25, in1=var[:],
                                             op0=ALU.mult, op1=ALU.add).then_inc(var_ready.sem, 1)
                    dve.wait_ge(*rstd_ready(1))
                    with st_.loop(0, GROUPS // 2, 8 if add_back else 0) as i:
                        for q in range(2):
                            g = i * 2 + q
                            dve.wait_ge(*xnT_psum(g - 1))
                            if XN is not None:
                                dve.wait_ge(*kept(g - 1))
                            for j in range(GT):
                                t = g * GT + j
                                ins = dve.tensor_scalar(xn[:, q, j, :], X[:, bass.ds(t, 1), :], mean[:, bass.ds(t, 1)],
                                                        rstd[:, bass.ds(t, 1)], ALU.subtract, ALU.mult)
                                if j == GT - 1:
                                    ins.then_inc(xn_ready.sem, 1)
                                if add_back and j < GT - 1:
                                    st_.count(ins)
                            if add_back:
                                dve.wait_ge(*xn_ready(g + 1))
                                xg = X[:, bass.ds(g * GT, GT), :]
                                st_.count(dve.tensor_tensor(xg, xg, xn[:, q], ALU.add))
                    st_.close()

                @block.scalar
                def _(act):
                    st_ = Steps(act, sig, "act_step")
                    act.wait_ge(*var_ready(1))
                    st_.link(act.activation(var[:], var[:], ACT.Ln))
                    act.activation(rstd[:], var[:], ACT.Exp, scale=-0.5).then_inc(rstd_ready.sem, 1)
                    st_.close()
                    with act.Fori(0, GROUPS // 2) as i:
                        for q in range(2):
                            g = i * 2 + q
                            act.wait_ge(*xnT_psum(g + 1))
                            act.copy(XNT[:, bass.ds(g * GW, GW)], B[q][:]).then_inc(xnT_ready.sem, 1)

                @block.tensor
                def _(pe):
                    with pe.Fori(0, GROUPS // 2) as i:
                        for q in range(2):
                            g = i * 2 + q
                            pe.wait_ge(*xn_ready(g + 1))
                            pe.wait_ge(*xnT_ready(g - 1))
                            for j in range(GT):
                                ins = pe.transpose(B[q][:, j * P:(j + 1) * P], xn[:, q, j, :], ident)
                            ins.then_inc(xnT_psum.sem, 1)

        def project(jobs):
            psum = [sig(f"proj_psum{j}", 8) for j in range(len(jobs))]
            done = [sig(f"proj_done{j}", 8) for j in range(len(jobs))]
            with nc.Block() as block:
                @block.tensor
                def _(pe):
                    with pe.Fori(0, GROUPS // 2) as i:
                        for q in range(2):
                            g = i * 2 + q
                            for j, (dst, wt, src, bias, scale) in enumerate(jobs):
                                pe.wait_ge(*done[j](g - 1))
                                pe.matmul(B[2 * j + q][:], wt, src[:, bass.ds(g * GW, GW)],
                                          start=True, stop=True).then_inc(psum[j].sem, 1)

                @block.vector
                def _(dve):
                    with dve.Fori(0, GROUPS // 2) as i:
                        for q in range(2):
                            g = i * 2 + q
                            for j in (0, 2):
                                if j < len(jobs):
                                    dst, wt, src, bias, scale = jobs[j]
                                    dve.wait_ge(*psum[j](g + 1))
                                    dve.tensor_scalar(dst[:, bass.ds(g * GW, GW)], B[2 * j + q][:], bias, scale,
                                                      ALU.add, ALU.mult).then_inc(done[j].sem, 1)

                if len(jobs) > 1:
                    assert jobs[1][4] == 1.0

                    @block.scalar
                    def _(act):
                        with act.Fori(0, GROUPS // 2) as i:
                            for q in range(2):
                                g = i * 2 + q
                                act.wait_ge(*psum[1](g + 1))
                                act.activation(jobs[1][0][:, bass.ds(g * GW, GW)], B[2 + q][:], ACT.Identity,
                                               bias=jobs[1][3]).then_inc(done[1].sem, 1)

        def attn16(name, src, bv, bo, causal):
            with ExitStack() as c2:
                def sb2(n, shape):
                    return hold(c2, n, shape)
                QT, KT, VT = sb2("QT", [P, TILES * P]), sb2("KT", [P, TILES * P]), sb2("VT", [P, TILES * P])
                project([(QT, w(name + "_q"), XNT, v(name + "_bq"), 8 ** -0.5),
                         (KT, w(name + "_k"), src, v(name + "_bk"), 1.0),
                         (VT, w(name + "_v"), src, v("zero"), 1.0)])
                mask4x = sb2("mask4x", [P, BPT, 4, S])
                qb, kb, vb = (sb2(n, [P, 2, BPT, 4, S]) for n in ("qb", "kb", "vb"))
                vt = sb2("vt", [P, 2, P])
                e = sb2("e", [P, 2, GW])
                pt = sb2("pt", [P, 2, GW])
                m = sb2("m", [P, 2, 4, P])
                mx, sm = sb2("mx", [P, 2, 16]), sb2("sm", [P, 2, 16])
                q_built, v_turned, v_built = sig("q_built", 32), sig("v_turned", 32), sig("v_built", 32)
                scores, centred, exp_ready = sig("scores", 32), sig("centred", 32), sig("exp_ready", 32)
                pT_ready, av_psum = sig("pT_ready", 32), sig("av_psum", 32)
                heads_ready, y_psum, x_added = sig("heads_ready", 32), sig("y_psum", 32), sig("x_added", 32)
                copied = sig("copied", 1)
                N = TILES

                def masked(eng, dst, srcap, mask):
                    return eng.tensor_tensor(dst, srcap.unsqueeze(2).to_broadcast([P, BPT, 4, S]),
                                             mask.unsqueeze(1).unsqueeze(3).to_broadcast([P, BPT, 4, S]), ALU.mult)

                block = c2.enter_context(nc.Block())

                def run(eng, stages, depth, steps=None, per=0):
                    for t in range(2):
                        stages(t, t % 2, lambda x: 0 <= x < N)
                    lp = steps.loop(1, N // 2, per) if steps else eng.Fori(1, N // 2)
                    with lp as i:
                        for q in range(2):
                            stages(i * 2 + q, q, lambda x: True)
                    for t in range(N, N + depth):
                        stages(t, t % 2, lambda x: 0 <= x < N)

                @block.gpsimd
                def _(pool):
                    def stages(t, q, ok):
                        pool.wait_ge(*scores(t - 1))
                        tok = bass.ds(t * P, P)
                        masked(pool, qb[:, q], QT[:, tok].rearrange("p (b s) -> p b s", b=BPT), const("group"))
                        masked(pool, kb[:, q], KT[:, tok].rearrange("p (b s) -> p b s", b=BPT), const("head"))\
                            .then_inc(q_built.sem, 1)
                        pool.wait_ge(*v_turned(t + 1))
                        pool.wait_ge(*av_psum(t - 1))
                        masked(pool, vb[:, q], vt[:, q, :].rearrange("p (b s) -> p b s", b=BPT), const("group"))\
                            .then_inc(v_built.sem, 1)
                    run(pool, stages, 0)

                @block.tensor
                def _(pe):
                    def stages(t, q, ok):
                        if ok(t):
                            pe.wait_ge(*q_built(t + 1))
                            pe.wait_ge(*centred(t - 1))
                            if isinstance(t, int) and t == 0:
                                pe.wait_ge(*copied(1))
                            if causal:
                                pe.matmul(B[q][:], ident, mask4x[:].rearrange("p b j k -> p (b j k)"), start=True,
                                          stop=False, skip_group_check=True)
                            for b in range(BPT):
                                ins = pe.matmul(B[q][:, b * P:(b + 1) * P], qb[:, q, b].rearrange("p j s -> p (j s)"),
                                                kb[:, q, b].rearrange("p j s -> p (j s)"), start=not causal, stop=True,
                                                skip_group_check=True)
                            ins.then_inc(scores.sem, 1)
                        u, z = t - 1, 1 - q
                        if ok(u):
                            pe.wait_ge(*pT_ready(u + 1))
                            pe.wait_ge(*v_built(u + 1))
                            pe.wait_ge(*heads_ready(u - 1))
                            for b in range(BPT):
                                out_b = B[2 + z][:].rearrange("p (j b s) -> p j b s", j=4, b=BPT)[:, :, b, :]
                                ins = pe.matmul(out_b, vb[:, z, b].rearrange("p j s -> p (j s)"),
                                                pt[:, z, b * P:(b + 1) * P], start=True, stop=True)
                            ins.then_inc(av_psum.sem, 1)
                        u, z = t - 2, q
                        if ok(u):
                            pe.wait_ge(*heads_ready(u + 1))
                            pe.wait_ge(*x_added(u - 1))
                            pe.matmul(B[4 + z][:, 0:P], ones_row, r(bo), start=True, stop=False)
                            for j in range(4):
                                ins = pe.matmul(B[4 + z][:, 0:P], m[:, z, j, :], w(name + "_o"),
                                                start=False, stop=(j == 3))
                            ins.then_inc(y_psum.sem, 1)
                    run(pe, stages, 2)

                @block.scalar
                def _(act):
                    def stages(t, q, ok):
                        act.wait_ge(*centred(t + 1))
                        act.activation(e[:, q, :], e[:, q, :], ACT.Exp).then_inc(exp_ready.sem, 1)
                    run(act, stages, 0)

                @block.vector
                def _(dve):
                    st_ = Steps(dve, sig, "dve_step")
                    for b in range(BPT):
                        for j in range(4):
                            ins = dve.tensor_scalar(mask4x[:, b, j, :], const("later"),
                                                    MASKED, None, ALU.mult)
                    ins.then_inc(copied.sem, 1)

                    def stages(t, q, ok):
                        if ok(t):
                            dve.wait_ge(*v_built(t - 1))
                            tok = bass.ds(t * P, P)
                            st_.link(dve.tensor_copy(vt[:, q, :], VT[:, tok]))
                            dve.transpose(vt[:, q, :], vt[:, q, :]).then_inc(v_turned.sem, 1)
                            dve.wait_ge(*scores(t + 1))
                            st_.link(dve.tensor_reduce(mx[:, q, :], B[q][:].rearrange("p (g k) -> p g k", k=S), AX.X, ALU.max))
                            dve.tensor_tensor(e[:, q, :].rearrange("p (g k) -> p g k", k=S),
                                              B[q][:].rearrange("p (g k) -> p g k", k=S),
                                              mx[:, q, :].unsqueeze(2).to_broadcast([P, 16, S]),
                                              ALU.subtract).then_inc(centred.sem, 1)
                        u, z = t - 1, 1 - q
                        if ok(u):
                            dve.wait_ge(*av_psum(u + 1))
                            dve.wait_ge(*y_psum(u - 1))
                            dve.scalar_tensor_tensor(out=m[:, z].rearrange("p j t -> p (j t)"), in0=B[2 + z][:],
                                                     scalar=v(bv), in1=const("diag512"), op0=ALU.add,
                                                     op1=ALU.mult).then_inc(heads_ready.sem, 1)
                        if ok(t):
                            dve.wait_ge(*exp_ready(t + 1))
                            ev = e[:, q, :].rearrange("p (g k) -> p g k", k=S)
                            st_.link(dve.tensor_reduce(sm[:, q, :], ev, AX.X, ALU.add))
                            st_.link(dve.reciprocal(sm[:, q, :], sm[:, q, :]))
                            st_.link(dve.tensor_tensor(ev, ev, sm[:, q, :].unsqueeze(2).to_broadcast([P, 16, S]), ALU.mult))
                            dve.wait_ge(*av_psum(t - 1))
                            dve.transpose(pt[:, q, :], e[:, q, :]).then_inc(pT_ready.sem, 1)
                        u, z = t - 2, q
                        if ok(u):
                            dve.wait_ge(*y_psum(u + 1))
                            xt_ = X[:, bass.ds(u, 1), :]
                            dve.tensor_tensor(xt_, xt_, B[4 + z][:, 0:P].unsqueeze(1), ALU.add).then_inc(x_added.sem, 1)
                    run(dve, stages, 2, st_, 10)
                    st_.close()

        def rwkv():
            with ExitStack() as c2:
                def sb2(n, shape):
                    return hold(c2, n, shape)
                VT, RT = sb2("VT", [P, TILES * P]), sb2("RT", [P, TILES * P])
                project([(VT, w("a0_v"), XNT, v("zero"), 1.0), (RT, w("a0_r"), XNT, v("zero"), 1.0)])
                pp = sb2("pp", [P, S + 1])
                relu_td = sb2("relu_td", [P, S])
                low = sb2("low", [P, S])
                ex = sb2("ex", [P, 4, S])
                bb = sb2("bb", [P, S + 1])
                den = sb2("den", [P, S])
                decay = sb2("decay", [P, 16, S])
                ub = sb2("ub", [P, 16, S])
                aa = sb2("aa", [P, 16, S])
                y = sb2("y", [P, 2, 16, S])
                a_done, b_done = sig("a_done", 1), sig("b_done", 1)
                exp_ready, scan_ready = sig("exp_ready", 8), sig("scan_ready", 8)
                y_psum, x_added = sig("y_psum", 8), sig("x_added", 8)
                block = c2.enter_context(nc.Block())
                td, tf = v("time_decay"), v("time_first")

                @block.vector
                def _(dve):
                    st_ = Steps(dve, sig, "dve_step")
                    p0 = pp[:, 0:S]
                    st_.count(dve.memset(pp[:, 0:1], -10000.0))
                    st_.count(dve.memset(low[:], -3.0e38))
                    st_.count(dve.memset(bb[:, 0:1], 0.0))
                    st_.count(dve.memset(ub[:], 0.0))
                    st_.count(dve.memset(decay[:], 0.0))
                    st_.count(dve.memset(relu_td[:], 0.0))
                    st_.wait()
                    st_.link(dve.tensor_scalar(relu_td[:], relu_td[:], td, None, ALU.max))
                    st_.link(dve.tensor_tensor_scan(pp[:, 1:S + 1], relu_td[:], low[:], pp[:, 0:1], ALU.add, ALU.max))
                    for k, x in ((0, tf), (2, td)):
                        st_.link(dve.tensor_scalar(ex[:, k + 1, :], p0, x, None, ALU.add))
                        st_.link(dve.tensor_tensor(den[:], p0, ex[:, k + 1, :], ALU.max))
                        st_.count(dve.tensor_tensor(ex[:, k, :], p0, den[:], ALU.subtract))
                        ins = dve.tensor_tensor(ex[:, k + 1, :], ex[:, k + 1, :], den[:], ALU.subtract)
                        st_.link(ins) if k == 0 else ins.then_inc(a_done.sem, 1)
                    dve.wait_ge(*b_done(1))
                    st_.link(dve.tensor_tensor_scan(bb[:, 1:S + 1], ex[:, 2, :], ex[:, 3, :], bb[:, 0:1], ALU.mult, ALU.add))
                    st_.link(dve.tensor_tensor(den[:], ex[:, 0, :], bb[:, 0:S], ALU.mult))
                    st_.link(dve.tensor_tensor(den[:], den[:], ex[:, 1, :], ALU.add))
                    st_.link(dve.tensor_scalar(den[:], den[:], 1e-6, None, ALU.add))
                    st_.link(dve.reciprocal(den[:], den[:]))
                    st_.count(dve.tensor_tensor(ex[:, 0, :], ex[:, 0, :], den[:], ALU.mult))
                    st_.count(dve.tensor_tensor(ex[:, 1, :], ex[:, 1, :], den[:], ALU.mult))
                    st_.link(dve.tensor_copy(decay[:, :, 1:S], ex[:, 2, 0:S - 1].unsqueeze(1).to_broadcast([P, 16, S - 1])))

                    def add(g, q):
                        dve.wait_ge(*y_psum(g + 1))
                        xg = X[:, bass.ds(g * GT, GT), :]
                        dve.tensor_tensor(xg, xg, B[q][:].rearrange("p (t d) -> p t d", t=GT), ALU.add)\
                            .then_inc(x_added.sem, 1)

                    def body(g, q):
                        vg = VT[:, bass.ds(g * GW, GW)].rearrange("p (b s) -> p b s", s=S)
                        st_.link(dve.tensor_tensor(ub[:, :, 1:S], vg[:, :, 0:S - 1],
                                                   ex[:, 3, 0:S - 1].unsqueeze(1).to_broadcast([P, 16, S - 1]), ALU.mult))
                        st_.link(dve.tensor_tensor_scan(aa[:].rearrange("p b s -> p (b s)"), decay[:].rearrange("p b s -> p (b s)"),
                                                        ub[:].rearrange("p b s -> p (b s)"), 0.0, ALU.mult, ALU.add))
                        st_.link(dve.tensor_tensor(aa[:], aa[:], ex[:, 0, :].unsqueeze(1).to_broadcast([P, 16, S]), ALU.mult))
                        dve.wait_ge(*y_psum(g - 1))
                        st_.link(dve.tensor_tensor(y[:, q], vg, ex[:, 1, :].unsqueeze(1).to_broadcast([P, 16, S]), ALU.mult))
                        st_.link(dve.tensor_tensor(y[:, q], y[:, q], aa[:], ALU.add))
                        dve.wait_ge(*exp_ready(g + 1))
                        dve.tensor_tensor(y[:, q], y[:, q], RT[:, bass.ds(g * GW, GW)].rearrange("p (b s) -> p b s", s=S), ALU.mult)\
                            .then_inc(scan_ready.sem, 1)
                    with st_.loop(0, GROUPS // 2, 10) as i:
                        for q in range(2):
                            body(i * 2 + q, q)
                            add(i * 2 + q, q)
                    st_.close()

                @block.scalar
                def _(act):
                    act.wait_ge(*a_done(1))
                    act.activation(ex[:], ex[:], ACT.Exp).then_inc(b_done.sem, 1)
                    with act.Fori(0, GROUPS) as g:
                        rg = RT[:, bass.ds(g * GW, GW)]
                        act.activation(rg, rg, ACT.Sigmoid).then_inc(exp_ready.sem, 1)

                @block.tensor
                def _(pe):
                    with pe.Fori(0, GROUPS // 2) as i:
                        for q in range(2):
                            g = i * 2 + q
                            pe.wait_ge(*scan_ready(g + 1))
                            pe.wait_ge(*x_added(g - 1))
                            for j in range(GT):
                                ins = pe.matmul(B[q][:, j * P:(j + 1) * P],
                                                y[:, q].rearrange("p b s -> p (b s)")[:, j * P:(j + 1) * P],
                                                w("a0_o"), start=True, stop=True)
                            ins.then_inc(y_psum.sem, 1)

        def rglru():
            with ExitStack() as c2:
                def sb2(n, shape):
                    return hold(c2, n, shape)
                GX, GA = sb2("GX", [P, TILES * P]), sb2("GA", [P, TILES * P])
                project([(GX, w("a2_i"), XNT, v("ig_b"), 1.0), (GA, w("a2_a"), XNT, v("ag_b"), 1.0)])
                cp = sb2("cp", [P, 4])
                inner, first = sb2("inner", [P, 16, S]), sb2("first", [P, 16, S])
                a2, ash, p, u = (sb2(n, [P, 2, 16, S]) for n in ("a2", "ash", "p", "u"))
                gx = sb2("gx", [P, 2, 16, S])
                a_done, b_done = sig("a_done", 1), sig("b_done", 1)
                exp_ready, d_done, e_done = sig("exp_ready", 8), sig("d_done", 8), sig("e_done", 8)
                copied, y_done = sig("copied", 8), sig("sums_ready", 8)
                scan_ready, y_psum, x_added = sig("scan_ready", 8), sig("y_psum", 8), sig("x_added", 8)
                block = c2.enter_context(nc.Block())
                flat = "p b s -> p (b s)"

                @block.scalar
                def _(act):
                    st_ = Steps(act, sig, "act_step")
                    st_.link(act.activation(cp[:, 0:1], v("a_param"), ACT.Abs))
                    st_.link(act.activation(cp[:, 0:1], cp[:, 0:1], ACT.Exp, scale=-1.0))
                    act.activation(cp[:, 0:1], cp[:, 0:1], ACT.Ln, bias=1.0).then_inc(a_done.sem, 1)
                    st_.close()
                    with act.Fori(0, GROUPS) as g:
                        tok = bass.ds(g * GW, GW)
                        act.activation(GX[:, tok], GX[:, tok], ACT.Sigmoid)
                        act.activation(GA[:, tok], GA[:, tok], ACT.Sigmoid).then_inc(exp_ready.sem, 1)
                    act.wait_ge(*b_done(1))
                    with st_.loop(0, GROUPS // 2, 2) as i:
                        for q in range(2):
                            g = i * 2 + q
                            ga = GA[:, bass.ds(g * GW, GW)].rearrange("p (b s) -> p b s", s=S)
                            act.wait_ge(*exp_ready(g + 1))
                            act.wait_ge(*scan_ready(g - 1))
                            act.sem_inc(sig.sems["act_passed"], 1)
                            act.activation(a2[:, q], ga, ACT.Exp, scale=cp[:, 2:3]).then_inc(d_done.sem, 1)
                            act.activation(ash[:, q], ga, ACT.Exp, scale=cp[:, 1:2]).then_inc(copied.sem, 1)
                            act.wait_ge(*e_done(g + 1))
                            st_.link(act.activation(a2[:, q], a2[:, q], ACT.Ln))
                            act.activation(a2[:, q], a2[:, q], ACT.Exp, scale=0.5).then_inc(y_done.sem, 1)
                    st_.close()

                @block.vector
                def _(dve):
                    st_ = Steps(dve, sig, "dve_step")
                    st_.count(dve.memset(inner[:], 1.0))
                    st_.count(dve.memset(first[:], 0.0))
                    st_.wait()
                    st_.count(dve.memset(inner[:, :, 0:1], 0.0))
                    st_.count(dve.memset(first[:, :, 0:1], 1.0))
                    st_.link(dve.memset(cp[:, 3:4], 0.0))
                    dve.wait_ge(*a_done(1))
                    st_.link(dve.tensor_scalar(cp[:, 3:4], cp[:, 3:4], v("a_param"), None, ALU.max))
                    st_.link(dve.tensor_tensor(cp[:, 3:4], cp[:, 3:4], cp[:, 0:1], ALU.add))
                    st_.count(dve.tensor_scalar(cp[:, 1:2], cp[:, 3:4], -8.0, None, ALU.mult))
                    dve.tensor_scalar(cp[:, 2:3], cp[:, 3:4], -16.0, None, ALU.mult).then_inc(b_done.sem, 1)
                    with st_.loop(0, GROUPS // 2, 20) as i:
                        for q in range(2):
                            g = i * 2 + q
                            tok = bass.ds(g * GW, GW)
                            dve.wait_ge(*exp_ready(g + 1))
                            st_.link(dve.tensor_tensor(gx[:, q].rearrange(flat), GX[:, tok], XNT[:, tok], ALU.mult))
                            dve.wait_ge(*d_done(g + 1))
                            st_.link(dve.tensor_scalar(a2[:, q], a2[:, q], -1.0, 1.0, ALU.mult, ALU.add))
                            dve.tensor_scalar(a2[:, q], a2[:, q], 1e-7, None, ALU.max).then_inc(e_done.sem, 1)
                            dve.wait_ge(*copied(g + 1))
                            st_.count(dve.tensor_copy(u[:, q, :, 1:S], ash[:, q, :, 0:S - 1]))
                            st_.link(dve.memset(u[:, q, :, 0:1], 0.0))
                            st_.link(dve.tensor_tensor_scan(p[:, q].rearrange(flat), u[:, q].rearrange(flat),
                                                            first[:].rearrange(flat), 0.0, ALU.mult, ALU.add))
                            st_.link(dve.tensor_scalar(p[:, q], p[:, q], 1e-7, None, ALU.max))
                            st_.link(dve.reciprocal(u[:, q], p[:, q]))
                            dve.wait_ge(*y_done(g + 1))
                            st_.link(dve.tensor_tensor(gx[:, q], gx[:, q], a2[:, q], ALU.mult))
                            st_.link(dve.tensor_tensor(u[:, q], u[:, q], gx[:, q], ALU.mult))
                            dve.wait_ge(*y_psum(g - 1))
                            st_.link(dve.tensor_tensor_scan(gx[:, q].rearrange(flat), inner[:].rearrange(flat),
                                                            u[:, q].rearrange(flat), 0.0, ALU.mult, ALU.add))
                            dve.tensor_tensor(p[:, q], p[:, q], gx[:, q], ALU.mult).then_inc(scan_ready.sem, 1)
                            dve.wait_ge(*y_psum(g + 1))
                            xg = X[:, bass.ds(g * GT, GT), :]
                            dve.tensor_tensor(xg, xg, B[q][:].rearrange("p (t d) -> p t d", t=GT), ALU.add)\
                                .then_inc(x_added.sem, 1)
                    st_.close()

                @block.tensor
                def _(pe):
                    with pe.Fori(0, GROUPS // 2) as i:
                        for q in range(2):
                            g = i * 2 + q
                            pe.wait_ge(*scan_ready(g + 1))
                            pe.wait_ge(*x_added(g - 1))
                            for j in range(GT):
                                ins = pe.transpose(B[q][:, j * P:(j + 1) * P],
                                                   p[:, q].rearrange(flat)[:, j * P:(j + 1) * P], ident)
                            ins.then_inc(y_psum.sem, 1)

        def gate_logits(G, E, gw, bias_row):
            with ExitStack() as c2:
                stage = hold(c2, "stage", [P, 2, GW])
                stage_ready, logits, copied = sig("stage_ready", 8), sig("logits", 8), sig("copied", 8)
                block = c2.enter_context(nc.Block())

                @block.scalar
                def _(act):
                    with act.Fori(0, GROUPS // 2) as i:
                        for q in range(2):
                            g = i * 2 + q
                            act.wait_ge(*logits(g - 1))
                            act.copy(stage[:, q, :], XNT[:, bass.ds(g * GW, GW)]).then_inc(stage_ready.sem, 1)

                @block.tensor
                def _(pe):
                    with pe.Fori(0, GROUPS // 2) as i:
                        for q in range(2):
                            g = i * 2 + q
                            pe.wait_ge(*stage_ready(g + 1))
                            pe.wait_ge(*copied(g - 1))
                            for j in range(GT):
                                o = B[q][:, j * E:(j + 1) * E]
                                if bias_row is not None:
                                    pe.matmul(o, ones_row, bias_row, start=True, stop=False)
                                ins = pe.matmul(o, stage[:, q, j * P:(j + 1) * P], gw, start=bias_row is None, stop=True)
                            ins.then_inc(logits.sem, 1)

                @block.vector
                def _(dve):
                    with dve.Fori(0, GROUPS // 2) as i:
                        for q in range(2):
                            g = i * 2 + q
                            dve.wait_ge(*logits(g + 1))
                            dve.tensor_copy(G[:, bass.ds(g * GT, GT), 0:E],
                                            B[q][:, 0:GT * E].rearrange("p (t e) -> p t e", t=GT)).then_inc(copied.sem, 1)

        def bc(ap, E):
            return ap.unsqueeze(2).to_broadcast([P, TILES, E])

        def pick(st_, dve, G, m, hot, E, tmp):
            rev = const("rev")[:, 0:E].unsqueeze(1).to_broadcast([P, TILES, E])
            st_.link(dve.tensor_reduce(m[:], G, AX.X, ALU.max))
            st_.link(dve.tensor_tensor(hot, G, bc(m[:], E), ALU.is_equal))
            st_.link(dve.tensor_tensor(hot, hot, rev, ALU.mult))
            st_.link(dve.tensor_reduce(tmp[:], hot, AX.X, ALU.max))
            st_.link(dve.tensor_tensor(hot, hot, bc(tmp[:], E), ALU.is_equal))

        def route(kind, Cmb, E, gw, bias_row=None, chosen=None):
            with ExitStack() as c2:
                def sb2(n, shape):
                    return hold(c2, n, shape)
                G, h1, h2 = (sb2(n, [P, TILES, E]) for n in ("G", "h1", "h2"))
                if chosen:
                    M1, M2, g1, g2 = chosen
                m1, m2, tmp, tot, fb = (sb2(n, [P, TILES]) for n in ("m1", "m2", "tmp", "tot", "fb"))
                elig, keep, one = (sb2(n, [P, TILES]) for n in ("elig", "keep", "one"))
                gate_logits(G, E, gw, bias_row)
                a_done, b_done = sig("a_done", 1), sig("b_done", 1)
                c_done, d_done = (sig(n, E if kind == "capacity" else 0) for n in ("c_done", "d_done"))
                block = c2.enter_context(nc.Block())

                @block.scalar
                def _(act):
                    act.wait_ge(*a_done(1))
                    if kind == "pairs":
                        act.activation(m2[:], m2[:], ACT.Exp).then_inc(b_done.sem, 1)
                    else:
                        act.activation(G[:], G[:], ACT.Exp).then_inc(b_done.sem, 1)

                if kind == "capacity":
                    @block.tensor
                    def _(pe):
                        for e in range(E):
                            pe.wait_ge(*c_done(e + 1))
                            pe.matmul(B[0][:, 0:TILES], const("upto"), elig[:], start=True, stop=True)
                            pe.matmul(B[1][:, 0:TILES], const("ones"), elig[:], start=True, stop=True)\
                                .then_inc(d_done.sem, 1)

                @block.vector
                def _(dve):
                    st_ = Steps(dve, sig, "dve_step")
                    if kind == "pairs":
                        pick(st_, dve, G[:], m1, h1[:], E, tmp)
                        st_.link(dve.scalar_tensor_tensor(out=G[:], in0=h1[:], scalar=-3.0e38, in1=G[:],
                                                          op0=ALU.mult, op1=ALU.add))
                        pick(st_, dve, G[:], m2, h2[:], E, tmp)
                        dve.tensor_tensor(m2[:], m2[:], m1[:], ALU.subtract).then_inc(a_done.sem, 1)
                        dve.wait_ge(*b_done(1))
                        st_.link(dve.tensor_scalar(m1[:], m2[:], 1.0, None, ALU.add))
                        st_.link(dve.reciprocal(m1[:], m1[:]))
                        st_.link(dve.tensor_tensor(m2[:], m2[:], m1[:], ALU.mult))
                        for to, frm in ((M1, h1), (M2, h2), (g1, m1), (g2, m2)):
                            st_.count(dve.tensor_copy(to[:], frm[:]))
                        st_.wait()
                        st_.link(dve.tensor_tensor(h1[:], h1[:], bc(m1[:], E), ALU.mult))
                        st_.link(dve.tensor_tensor(h2[:], h2[:], bc(m2[:], E), ALU.mult))
                        st_.link(dve.tensor_tensor(Cmb[:], h1[:], h2[:], ALU.add))
                    else:
                        st_.link(dve.tensor_reduce(m1[:], G[:], AX.X, ALU.max))
                        dve.tensor_tensor(G[:], G[:], bc(m1[:], E), ALU.subtract).then_inc(a_done.sem, 1)
                        dve.wait_ge(*b_done(1))
                        st_.link(dve.tensor_reduce(m1[:], G[:], AX.X, ALU.add))
                        st_.link(dve.reciprocal(m1[:], m1[:]))
                        st_.link(dve.tensor_tensor(G[:], G[:], bc(m1[:], E), ALU.mult))
                        pick(st_, dve, G[:], m1, h1[:], E, tmp)
                    if kind == "first":
                        st_.link(dve.tensor_scalar(tmp[:], m1[:], 1e-8, None, ALU.add))
                        st_.link(dve.reciprocal(tmp[:], tmp[:]))
                        st_.link(dve.tensor_tensor(m1[:], m1[:], tmp[:], ALU.mult))
                        st_.link(dve.tensor_tensor(Cmb[:], h1[:], bc(m1[:], E), ALU.mult))
                    if kind == "capacity":
                        st_.link(dve.scalar_tensor_tensor(out=G[:], in0=h1[:], scalar=-3.0e38, in1=G[:],
                                                          op0=ALU.mult, op1=ALU.add))
                        pick(st_, dve, G[:], m2, h2[:], E, tmp)
                        st_.link(dve.tensor_tensor(tmp[:], m1[:], m2[:], ALU.add))
                        st_.link(dve.tensor_scalar(tmp[:], tmp[:], 1e-9, None, ALU.max))
                        st_.link(dve.reciprocal(tmp[:], tmp[:]))
                        st_.count(dve.tensor_tensor(m1[:], m1[:], tmp[:], ALU.mult))
                        st_.count(dve.tensor_tensor(m2[:], m2[:], tmp[:], ALU.mult))
                        st_.link(dve.tensor_tensor(G[:], h1[:], h2[:], ALU.add))
                        st_.count(dve.memset(one[:], 1.0))
                        st_.link(dve.memset(fb[:], 0.0))
                        for e in range(E):
                            st_.link(dve.tensor_tensor(keep[:], G[:, :, e], fb[:], ALU.mult))
                            dve.tensor_tensor(elig[:], G[:, :, e], keep[:], ALU.subtract).then_inc(c_done.sem, 1)
                            dve.wait_ge(*d_done(e + 1))
                            st_.link(dve.tensor_tensor_scan(tot[:], one[:], B[1][:, 0:TILES], 0.0, ALU.mult, ALU.add))
                            st_.link(dve.tensor_tensor(tot[:], tot[:], B[1][:, 0:TILES], ALU.subtract))
                            st_.link(dve.tensor_tensor(tot[:], tot[:], B[0][:, 0:TILES], ALU.add))
                            st_.link(dve.scalar_tensor_tensor(out=keep[:], in0=tot[:], scalar=float(CAP), in1=elig[:],
                                                              op0=ALU.is_le, op1=ALU.mult))
                            st_.link(dve.tensor_tensor(elig[:], elig[:], keep[:], ALU.subtract))
                            st_.count(dve.tensor_tensor(fb[:], fb[:], elig[:], ALU.add))
                            st_.link(dve.tensor_copy(Cmb[:, :, e], keep[:]))
                        st_.count(dve.tensor_copy(M1[:, :, E], fb[:]))
                        st_.count(dve.memset(M2[:, :, E], 0.0))
                        st_.link(dve.tensor_scalar(keep[:], fb[:], -1.0, 1.0, ALU.mult, ALU.add))
                        st_.count(dve.tensor_tensor(Cmb[:, :, 0:E], Cmb[:, :, 0:E], bc(keep[:], E), ALU.mult))
                        st_.link(dve.tensor_tensor(m1[:], m1[:], keep[:], ALU.mult))
                        st_.count(dve.tensor_tensor(M1[:, :, 0:E], h1[:], Cmb[:, :, 0:E], ALU.mult))
                        st_.count(dve.tensor_tensor(M2[:, :, 0:E], h2[:], Cmb[:, :, 0:E], ALU.mult))
                        st_.count(dve.tensor_tensor(g1[:], m1[:], fb[:], ALU.add))
                        st_.link(dve.tensor_copy(g2[:], m2[:]))
                        st_.count(dve.tensor_tensor(h2[:], M2[:, :, 0:E], bc(g2[:], E), ALU.mult))
                        st_.link(dve.tensor_tensor(Cmb[:], M1[:], bc(g1[:], E + 1), ALU.mult))
                        st_.link(dve.tensor_tensor(Cmb[:, :, 0:E], Cmb[:, :, 0:E], h2[:], ALU.add))
                        st_.link(dve.tensor_reduce(g2[:], h2[:], AX.X, ALU.add))
                    st_.close()

        def expert_bias(Cmb, E, b2, send_rows):
            with ExitStack() as c2:
                def sb2(n, shape):
                    return hold(c2, n, shape)
                b2s = sb2("b2s", [E, P])
                cst, ct = sb2("cst", [P, 2, GT, E]), sb2("ct", [E, 2, GW])
                w_loaded = sig("w_loaded", 1)
                stage_ready, c_turned, c_ready = sig("stage_ready", 8), sig("c_turned", 8), sig("c_ready", 8)
                y_psum, x_added = sig("y_psum", 8), sig("x_added", 8)
                block = c2.enter_context(nc.Block())

                @block.gpsimd
                def _(pool):
                    send_rows(pool)

                @block.sync
                def _(sp):
                    sp.dma_start(b2s[:], b2).then_inc(w_loaded.sem, 16)

                @block.vector
                def _(dve):
                    with dve.Fori(0, GROUPS // 2) as i:
                        for q in range(2):
                            g = i * 2 + q
                            dve.wait_ge(*c_turned(g - 1))
                            dve.tensor_copy(cst[:, q], Cmb[:, bass.ds(g * GT, GT), :]).then_inc(stage_ready.sem, 1)
                            dve.wait_ge(*y_psum(g + 1))
                            xg = X[:, bass.ds(g * GT, GT), :]
                            dve.tensor_tensor(xg, xg, B[2 + q][:].rearrange("p (t d) -> p t d", t=GT), ALU.add)\
                                .then_inc(x_added.sem, 1)

                @block.scalar
                def _(act):
                    with act.Fori(0, GROUPS // 2) as i:
                        for q in range(2):
                            g = i * 2 + q
                            act.wait_ge(*c_turned(g + 1))
                            act.wait_ge(*y_psum(g - 1))
                            act.copy(ct[:, q, :], B[q][0:E, :]).then_inc(c_ready.sem, 1)

                @block.tensor
                def _(pe):
                    pe.wait_ge(*w_loaded(1))
                    with pe.Fori(0, GROUPS // 2) as i:
                        for q in range(2):
                            g = i * 2 + q
                            pe.wait_ge(*stage_ready(g + 1))
                            pe.wait_ge(*c_ready(g - 1))
                            for j in range(GT):
                                ins = pe.transpose(B[q][0:E, j * P:(j + 1) * P], cst[:, q, j, :], ident)
                            ins.then_inc(c_turned.sem, 1)
                            pe.wait_ge(*c_ready(g + 1))
                            pe.wait_ge(*x_added(g - 1))
                            for j in range(GT):
                                ins = pe.matmul(B[2 + q][:, j * P:(j + 1) * P], ct[:, q, j * P:(j + 1) * P], b2s[:],
                                                start=True, stop=True)
                            ins.then_inc(y_psum.sem, 1)

        def experts(E, FC, Y, Cmb, w1, b1, w2, ready=None):
            with ExitStack() as c2:
                def sb2(n, shape):
                    return hold(c2, n, shape)
                F = FC * P
                if ready is None:
                    W1, W2, B1 = sb2("W1", [P, 2, F]), sb2("W2", [P, 2, FC, P]), sb2("B1", [P, 2, FC])
                else:
                    W1, W2, B1 = ready
                H = sb2("H", [P, 2, FC, GW])
                steps = E * GROUPS
                loads = [0, 0] if ready else [(E + 1) // 2, E // 2]
                w_loaded = [sig(f"w_loaded{s}", 3 * loads[s]) for s in range(2)]
                up_psum, gelu_ready = sig("up_psum", steps * FC), sig("gelu_ready", steps * FC)
                down_psum, x_added = sig("down_psum", steps), sig("x_added", steps)
                block = c2.enter_context(nc.Block())
                pairs = (E - 1) // 2

                def over_experts(eng, body):
                    if pairs:
                        with eng.Fori(0, pairs) as i:
                            for s in range(2):
                                body(i * 2 + s, i, s, False)
                    for e in range(2 * pairs, E):
                        body(e, e // 2, e % 2, e == E - 1)

                def over_groups(eng, e, fn, last=4):
                    with eng.Fori(0, last) as j:
                        for q in range(2):
                            fn(e, j * 2 + q, q)

                @block.sync
                def _(sp):
                    def body(e, h, s, last):
                        sp.wait_ge(*down_psum(8 * (e - 1)))
                        sp.dma_start(W1[:, s, :], w1[bass.ds(e, 1)].rearrange("e p f -> p (e f)")).then_inc(w_loaded[s].sem, 16)
                        sp.dma_start(B1[:, s, :], b1[bass.ds(e, 1)].rearrange("e p c -> p (e c)")).then_inc(w_loaded[s].sem, 16)
                        sp.dma_start(W2[:, s], w2[bass.ds(e, 1)].rearrange("e (c p) n -> p (e c) n", p=P)).then_inc(w_loaded[s].sem, 16)
                    if ready is None:
                        over_experts(sp, body)

                @block.tensor
                def _(pe):
                    def up(e, g, q, s):
                        for c in range(FC):
                            n = (e * GROUPS + g) * FC + c
                            bank = B[c if FC == 4 else 2 * q + c]
                            pe.wait_ge(*gelu_ready(n - 3))
                            pe.matmul(bank[:], W1[:, s, c * P:(c + 1) * P], XNT[:, bass.ds(g * GW, GW)],
                                      start=True, stop=True).then_inc(up_psum.sem, 1)

                    def down(e, g, q, s):
                        n = e * GROUPS + g
                        pe.wait_ge(*gelu_ready((n + 1) * FC))
                        pe.wait_ge(*x_added(n - 1))
                        for j in range(GT):
                            for c in range(FC):
                                ins = pe.matmul(B[4 + q][:, j * P:(j + 1) * P], H[:, q, c, j * P:(j + 1) * P],
                                                W2[:, s, c, :], start=(c == 0), stop=(c == FC - 1))
                        ins.then_inc(down_psum.sem, 1)

                    def body(e, h, s, last):
                        def fn(e, g, q):
                            up(e, g + 1, 1 - q, s)
                            down(e, g, q, s)
                        over_groups(pe, e, fn, 3)
                        up(e, 7, 1, s)
                        down(e, 6, 0, s)
                        if not last:
                            pe.wait_ge(*w_loaded[1 - s](3 * (h + s + 1)))
                            up(e + 1, 0, 0, 1 - s)
                        down(e, 7, 1, s)
                    if ready is None:
                        pe.wait_ge(*w_loaded[0](3))
                    up(0, 0, 0, 0)
                    over_experts(pe, body)

                @block.scalar
                def _(act):
                    def body(e, h, s, last):
                        if ready is None:
                            act.wait_ge(*w_loaded[s](3 * (h + 1)))

                        def fn(e, g, q):
                            n = e * GROUPS + g
                            act.wait_ge(*down_psum(n - 1))
                            for c in range(FC):
                                act.wait_ge(*up_psum(n * FC + c + 1))
                                bank = B[c if FC == 4 else 2 * q + c]
                                act.activation(H[:, q, c, :], bank[:], ACT.Gelu, bias=B1[:, s, c:c + 1])\
                                    .then_inc(gelu_ready.sem, 1)
                        over_groups(act, e, fn)
                    over_experts(act, body)

                @block.vector
                def _(dve):
                    def body(e, h, s, last):
                        def fn(e, g, q):
                            n = e * GROUPS + g
                            dve.wait_ge(*down_psum(n + 1))
                            dve.wait_ge(*x_added(n - 7))
                            for j in range(GT):
                                t = g * GT + j
                                yt = Y[:, bass.ds(t, 1), :]
                                bj = B[4 + q][:, j * P:(j + 1) * P]
                                if Cmb is None:
                                    ins = dve.tensor_tensor(yt, bj.unsqueeze(1), yt, ALU.add)
                                else:
                                    ins = dve.scalar_tensor_tensor(
                                        out=yt, in0=bj.unsqueeze(1), scalar=Cmb[:, bass.ds(t, 1), bass.ds(e, 1)].rearrange("p a b -> p (a b)"),
                                        in1=yt, op0=ALU.mult, op1=ALU.add)
                            ins.then_inc(x_added.sem, 1)
                        over_groups(dve, e, fn)
                    over_experts(dve, body)

        def attn8():
            with ExitStack() as c2:
                def sb2(n, shape):
                    return hold(c2, n, shape)
                BPS, N = BPT, TILES
                hot = sb2("hot", [32, S * P])
                emb = sb2("emb", [32, 8])
                bias = sb2("bias", [P, 2, S])
                laterM = sb2("laterM", [P, S])
                row_loaded = sig("row_loaded", 2)

                def fetch(sp):
                    sp.dma_start(hot[:], T["buckets"]).then_inc(row_loaded.sem, 16)
                    sp.dma_start(emb[:], T["rel_emb"]).then_inc(row_loaded.sem, 16)
                norm(fetch=fetch)
                copied, a_done = sig("copied", 1), sig("a_done", 1)
                with nc.Block() as block:
                    @block.tensor
                    def _(pe):
                        pe.wait_ge(*row_loaded(2))
                        for k in range(S):
                            ins = pe.matmul(B[0][:, 8 * k:8 * k + 8], hot[:, k * P:(k + 1) * P], emb[:], start=True, stop=True)
                        ins.then_inc(a_done.sem, 1)

                    @block.vector
                    def _(dve):
                        dve.tensor_scalar(laterM[:], const("later"), MASKED, None, ALU.mult).then_inc(copied.sem, 1)
                        dve.wait_ge(*copied(1))
                        dve.wait_ge(*a_done(1))
                        for A in range(4):
                            p = slice(32 * A, 32 * A + 32)
                            for h in range(2):
                                src = B[0][p, 0:8 * S].rearrange("p (k h) -> p h k", h=8)[:, 2 * A + h, :]
                                dve.scalar_tensor_tensor(out=bias[p, h, :], in0=src, scalar=64 ** 0.5, in1=laterM[p, :],
                                                         op0=ALU.mult, op1=ALU.add)
                qT, kT, vt = (sb2(n, [P, 2, 4, P]) for n in ("qT", "kT", "vt"))
                e, pt = sb2("e", [P, 2, 2, P]), sb2("pt", [P, 2, 2, P])
                o = sb2("o", [P, 2, 4, P])
                mx = sb2("mx", [P, 2, 8])
                qp, kp, vp = sig("proj_psum0", N), sig("proj_psum1", N), sig("proj_psum2", N)
                qd, kd, vd = sig("proj_done0", N), sig("proj_done1", N), sig("proj_done2", N)
                scores, centred, exp_ready, pT_ready = (sig(n, N) for n in ("scores", "centred", "exp_ready", "pT_ready"))
                s_summed = sig("s_summed", N)
                av_psum, o_ready, a_ready, y_psum, x_added = (sig(n, N) for n in ("av_psum", "o_ready", "a_ready", "y_psum", "x_added"))
                block = c2.enter_context(nc.Block())

                def run(eng, stages, depth, steps=None, per=0):
                    for t in range(2):
                        stages(t, t % 2, lambda x: 0 <= x < N)
                    with (steps.loop(1, N // 2, per) if steps else eng.Fori(1, N // 2)) as i:
                        for q in range(2):
                            stages(i * 2 + q, q, lambda x: True)
                    for t in range(N, N + depth):
                        stages(t, t % 2, lambda x: 0 <= x < N)

                @block.tensor
                def _(pe):
                    def stages(t, q, ok):
                        z = 1 - q
                        if ok(t):
                            tok = bass.ds(t * P, P)
                            pe.wait_ge(*vd(t))
                            for c in range(4):
                                ins = pe.matmul(B[0][:, c * P:(c + 1) * P], w(f"a1_q{c}"), XNT[:, tok], start=True, stop=True)
                            ins.then_inc(qp.sem, 1)
                            pe.wait_ge(*x_added(t - 1))
                            for c in range(4):
                                ins = pe.matmul(B[1][:, c * P:(c + 1) * P], w(f"a1_k{c}"), XNT[:, tok], start=True, stop=True)
                            ins.then_inc(kp.sem, 1)
                            pe.wait_ge(*qd(t + 1))
                            for c in range(4):
                                out_c = B[0][:].rearrange("p (b c s) -> p b c s", b=BPS, c=4)[:, :, c, :]
                                ins = pe.matmul(out_c, w(f"a1_v{c}"), XNT[:, tok], start=True, stop=True)
                            ins.then_inc(vp.sem, 1)
                        u = t - 1
                        if ok(u):
                            pe.wait_ge(*pT_ready(u + 1))
                            pe.wait_ge(*o_ready(u))
                            pe.wait_ge(*a_ready(u))
                            for b in range(BPS):
                                for A in range(4):
                                    p = slice(32 * A, 32 * A + 32)
                                    for h in range(2):
                                        ins = pe.matmul(B[4 + A][64 * h:64 * h + 64, b * S:(b + 1) * S],
                                                        vt[p, z].rearrange("p c s -> p (c s)")[:, b * P + 64 * h:b * P + 64 * h + 64],
                                                        pt[p, z, h, b * S:(b + 1) * S], start=True, stop=True,
                                                        tile_position=(32 * A, 64 * h))
                            ins.then_inc(av_psum.sem, 1)
                        if ok(t):
                            pe.wait_ge(*kd(t + 1))
                            pe.wait_ge(*s_summed(t))
                            pe.sem_inc(sig.sems["pe_passed"], 1)
                            for b in range(BPS):
                                for c in range(4):
                                    for h in range(2):
                                        r_ = slice(64 * h, 64 * h + 64)
                                        ins = pe.matmul(B[2 + h][32 * c:32 * c + 32, b * S:(b + 1) * S],
                                                        qT[r_, q, c, b * S:(b + 1) * S], kT[r_, q, c, b * S:(b + 1) * S],
                                                        start=True, stop=True, tile_position=(64 * h, 32 * c))
                            ins.then_inc(scores.sem, 1)
                        if ok(u):
                            pe.wait_ge(*o_ready(u + 1))
                            pe.wait_ge(*a_ready(u + 1))
                            if not ok(t):
                                pe.wait_ge(*kd(u + 1))
                            pe.matmul(B[1][:, 0:P], ones_row, r("a1_bo"), start=True, stop=False)
                            for c in range(4):
                                ins = pe.matmul(B[1][:, 0:P], o[:, z, c, :], w(f"a1_o{c}"), start=False, stop=(c == 3))
                            ins.then_inc(y_psum.sem, 1)
                    run(pe, stages, 1)

                @block.scalar
                def _(act):
                    def stages(t, q, ok):
                        z = 1 - q
                        if ok(t):
                            act.wait_ge(*qp(t + 1))
                            act.wait_ge(*scores(t - 1))
                            act.activation(qT[:, q], B[0][:].rearrange("p (c s) -> p c s", c=4), ACT.Copy, scale=64 ** -0.5).then_inc(qd.sem, 1)
                            act.wait_ge(*kp(t + 1))
                            act.copy(kT[:, q], B[1][:].rearrange("p (c s) -> p c s", c=4)).then_inc(kd.sem, 1)
                        u = t - 1
                        if ok(u):
                            act.wait_ge(*av_psum(u + 1))
                            act.wait_ge(*y_psum(u - 1))
                            act.copy(o[:, z, 0, :], B[4][:, 0:P])
                            act.copy(o[:, z, 1, :], B[5][:, 0:P]).then_inc(o_ready.sem, 1)
                        if ok(t):
                            act.wait_ge(*centred(t + 1))
                            act.activation(e[:, q], e[:, q], ACT.Exp).then_inc(exp_ready.sem, 1)
                    run(act, stages, 1)

                @block.vector
                def _(dve):
                    st_ = Steps(dve, sig, "dve_step")

                    def stages(t, q, ok):
                        z = 1 - q
                        if ok(t):
                            dve.wait_ge(*vp(t + 1))
                            dve.wait_ge(*av_psum(t - 1))
                            dve.transpose(vt[:, q].rearrange("p c s -> p (c s)"), B[0][:]).then_inc(vd.sem, 1)
                        u = t - 1
                        if ok(u):
                            dve.wait_ge(*av_psum(u + 1))
                            dve.wait_ge(*y_psum(u - 1))
                            dve.tensor_copy(o[:, z, 2, :], B[6][:, 0:P])
                            dve.tensor_copy(o[:, z, 3, :], B[7][:, 0:P]).then_inc(a_ready.sem, 1)
                        if ok(t):
                            dve.wait_ge(*scores(t + 1))
                            ev = e[:, q].rearrange("p h (b k) -> p h b k", k=S)
                            for h in range(2):
                                ins = dve.tensor_tensor(ev[:, h], B[2 + h][:, 0:P].rearrange("p (b k) -> p b k", k=S),
                                                        bias[:, h, :].unsqueeze(1).to_broadcast([P, BPS, S]), ALU.add)
                                if h == 0:
                                    st_.count(ins)
                            ins.then_inc(s_summed.sem, 1)
                            dve.wait_ge(*s_summed(t + 1))
                            eg = e[:, q].rearrange("p h (b k) -> p (h b) k", k=S)
                            m = mx[:, q, :]
                            st_.link(dve.tensor_reduce(m, eg, AX.X, ALU.max))
                            dve.tensor_tensor(eg, eg, m.unsqueeze(2).to_broadcast([P, 8, S]), ALU.subtract).then_inc(centred.sem, 1)
                            dve.wait_ge(*exp_ready(t + 1))
                            st_.link(dve.tensor_reduce(m, eg, AX.X, ALU.add))
                            st_.link(dve.reciprocal(m, m))
                            st_.link(dve.tensor_tensor(eg, eg, m.unsqueeze(2).to_broadcast([P, 8, S]), ALU.mult))
                            dve.transpose(pt[:, q].rearrange("p h s -> p (h s)"), e[:, q].rearrange("p h s -> p (h s)"))\
                                .then_inc(pT_ready.sem, 1)
                        if ok(u):
                            dve.wait_ge(*y_psum(u + 1))
                            xt_ = X[:, bass.ds(u, 1), :]
                            dve.tensor_tensor(xt_, xt_, B[1][:, 0:P].unsqueeze(1), ALU.add).then_inc(x_added.sem, 1)
                    run(dve, stages, 1, st_, 10)
                    st_.close()

        def dispatch(E, XN, M1, M2, send, back, expert_of, blocks):
            with ExitStack() as c2:
                def sb2(n, shape):
                    return hold(c2, n, shape)
                HT_ = TILES // 2
                A, pos = sb2("A", [P, TILES, E]), sb2("pos", [P, TILES, E])
                tot, cum, carry = (sb2(n, [P, E, TILES]) for n in ("tot", "cum", "carry"))
                above = sb2("above", [P, E, TILES])
                nb, end = sb2("nb", [P, E]), sb2("end", [P, E])
                ended, at = sb2("ended", [1, blocks, E]), sb2("at", [1, blocks])
                p1, p2, has = (sb2(n, [P, TILES]) for n in ("p1", "p2", "has"))
                a_done, b_done = sig("a_done", 1), sig("b_done", 1)
                block = c2.enter_context(nc.Block())

                @block.tensor
                def _(pe):
                    pe.wait_ge(*a_done(1))
                    for h in range(2):
                        ah = A[:, h * HT_:(h + 1) * HT_, :].rearrange("p t e -> p (t e)")
                        pe.matmul(B[h][:, 0:HT_ * E], const("upto"), ah, start=True, stop=True)
                        ins = pe.matmul(B[2 + h][:, 0:HT_ * E], const("ones"), ah, start=True, stop=True)
                    ins.then_inc(b_done.sem, 1)

                @block.vector
                def _(dve):
                    st_ = Steps(dve, sig, "dve_step")
                    dve.tensor_tensor(A[:], M1[:], M2[:], ALU.add).then_inc(a_done.sem, 1)
                    st_.link(dve.memset(carry[:], 1.0))
                    st_.count(dve.memset(carry[:, :, 0], 0.0))
                    dve.wait_ge(*b_done(1))
                    for h in range(2):
                        st_.count(dve.tensor_copy(tot[:, :, h * HT_:(h + 1) * HT_],
                                                  B[2 + h][:, 0:HT_ * E].rearrange("p (t e) -> p e t", e=E)))
                    st_.wait()
                    st_.link(dve.tensor_tensor_scan(cum[:].rearrange("p e t -> p (e t)"), carry[:].rearrange("p e t -> p (e t)"),
                                                    tot[:].rearrange("p e t -> p (e t)"), 0.0, ALU.mult, ALU.add))
                    st_.link(dve.tensor_tensor(above[:], cum[:, :, TILES - 1:TILES].to_broadcast([P, E, 32]),
                                                const("multiples").unsqueeze(1).to_broadcast([P, E, 32]), ALU.is_gt))
                    st_.link(dve.tensor_tensor(cum[:], cum[:], tot[:], ALU.subtract))
                    st_.link(dve.tensor_reduce(nb[:], above[:], AX.X, ALU.add))
                    st_.link(dve.tensor_tensor_scan(end[:], const("ones")[:, 0:E], nb[:], 0.0, ALU.mult, ALU.add))
                    st_.link(dve.tensor_tensor(ended[:], end[0:1, :].unsqueeze(1).to_broadcast([1, blocks, E]),
                                                const("block_no")[0:1, 0:blocks].unsqueeze(2).to_broadcast([1, blocks, E]), ALU.is_le))
                    st_.link(dve.tensor_tensor(nb[:], end[:], nb[:], ALU.subtract))
                    st_.link(dve.tensor_reduce(at[:], ended[:], AX.X, ALU.add))
                    st_.link(dve.tensor_scalar(nb[:], nb[:], float(P), -1.0, ALU.mult, ALU.add))
                    st_.link(dve.tensor_scalar(at[:], at[:], float(E - 1), None, ALU.min))
                    st_.link(dve.tensor_tensor(cum[:], cum[:], nb[:].unsqueeze(2).to_broadcast([P, E, TILES]), ALU.add))
                    st_.count(dve.tensor_copy(expert_of[:], at[:]))
                    for h in range(2):
                        st_.count(dve.tensor_tensor(pos[:, h * HT_:(h + 1) * HT_, :],
                                                    B[h][:, 0:HT_ * E].rearrange("p (t e) -> p t e", e=E),
                                                    cum[:, :, h * HT_:(h + 1) * HT_].rearrange("p e t -> p t e"), ALU.add))
                    st_.wait()
                    st_.link(dve.tensor_tensor(A[:], M1[:], pos[:], ALU.mult))
                    st_.count(dve.tensor_tensor(pos[:], M2[:], pos[:], ALU.mult))
                    st_.count(dve.tensor_reduce(p1[:], A[:], AX.X, ALU.add))
                    st_.count(dve.tensor_reduce(has[:], M2[:], AX.X, ALU.add))
                    st_.wait()
                    st_.count(dve.tensor_reduce(p2[:], pos[:], AX.X, ALU.add))
                    st_.count(dve.tensor_scalar(has[:], has[:], -1.0, 1.0, ALU.mult, ALU.add))
                    st_.link(dve.tensor_copy(back[:, 0, :], p1[:]))
                    st_.link(dve.tensor_copy(send[:, 0, :], p1[:]))
                    st_.link(dve.tensor_copy(back[:, 1, :], p2[:]))
                    st_.link(dve.tensor_scalar(p1[:], const("spare"), float(blocks * P), None, ALU.add))
                    st_.link(dve.tensor_tensor(has[:], has[:], p1[:], ALU.mult))
                    st_.link(dve.tensor_tensor(p2[:], p2[:], has[:], ALU.add))
                    st_.link(dve.tensor_copy(send[:, 1, :], p2[:]))
                    st_.close()

            rows_sent = sig("rows_sent", 2 * TILES)

            def send_rows(pool):
                pool.wait_ge(*cleared(1))
                for k in range(2):
                    for t in range(TILES):
                        pool.indirect_dma_start(T["pair_rows"], bass.IndirectOffsetOnAxis(ap=send[:, k, t:t + 1], axis=0),
                                                XN[:, t, :], None).then_inc(rows_sent.sem, 16)
                pool.wait_ge(*rows_sent(2 * TILES))
            return send_rows

        def sparse_experts(E, W1, w_loaded, w2, b1, g, back, expert_of, blocks):
            with ExitStack() as c2:
                def sb2(n, shape):
                    return hold(c2, n, shape)
                F = 4 * P
                N = blocks
                W2, B1 = sb2("W2", [P, E, 4, P]), sb2("B1", [P, E, 4])
                with ExitStack() as c3:
                    def sb3(n, shape):
                        return hold(c3, n, shape)
                    xb, yb = sb3("xb", [P, 4, P]), sb3("yb", [P, 4, P])
                    xT, u, hT = sb3("xT", [P, 2, P]), sb3("u", [P, 2, F]), sb3("hT", [P, 2, F])
                    loads = [sig(f"ct_loaded{j}", len(range(j, N, 4))) for j in range(4)]
                    stores = [sig(f"stored{j}", len(range(j, N, 4))) for j in range(4)]
                    w2_loaded = sig("w_loaded0", 5)
                    x_turned, xT_ready, u_psum, u_ready = (sig(n, N) for n in ("x_turned", "xT_ready", "u_psum", "u_ready"))
                    uT_psum, h_ready, yb_psum, yb_ready = (sig(n, N) for n in ("uT_psum", "h_ready", "yb_psum", "yb_ready"))
                    block = c3.enter_context(nc.Block())
                    first, drain = 2, 6

                    def run(eng, stages):
                        for x in range(4 * first):
                            stages(x, x % 4, x // 4, lambda b: 0 <= b < N)
                        with eng.Fori(first, N // 4) as i:
                            for r_ in range(4):
                                stages(i * 4 + r_, r_, i, lambda b: True)
                        for x in range(N // 4 * 4, N + drain):
                            stages(x, x % 4, x // 4, lambda b: 0 <= b < N)

                    def expert(eng, b):
                        return eng.value_load(expert_of[0:1, bass.ds(b, 1)], min_val=0, max_val=E - 1)

                    rows = T["pair_rows"].rearrange("(j p) d -> j p d", p=P)
                    outs = T["pair_outs"].rearrange("(j p) d -> j p d", p=P)

                    @block.sync
                    def _(sp):
                        for c in range(4):
                            sp.dma_start(W2[:, :, c, :], w2[:, c * P:(c + 1) * P, :].rearrange("e p n -> p e n"))\
                                .then_inc(w2_loaded.sem, 16)
                        sp.dma_start(B1[:], b1.rearrange("e p c -> p e c")).then_inc(w2_loaded.sem, 16)

                        def stages(x, r_, i, ok):
                            if ok(x):
                                sp.wait_ge(*x_turned(x - 3))
                                sp.dma_start(xb[:, r_, :], rows[bass.ds(x, 1)].rearrange("j p d -> p (j d)"))\
                                    .then_inc(loads[r_].sem, 16)
                            b, j = x - 6, (r_ - 6) % 4
                            if ok(b):
                                sp.wait_ge(*yb_ready(b + 1))
                                sp.dma_start(outs[bass.ds(b, 1)].rearrange("j p d -> p (j d)"), yb[:, j, :])\
                                    .then_inc(stores[j].sem, 16)
                        run(sp, stages)
                        for j in range(4):
                            sp.wait_ge(*stores[j](len(range(j, N, 4))))

                    @block.tensor
                    def _(pe):
                        pe.wait_ge(*w_loaded(1))
                        pe.wait_ge(*w2_loaded(5))

                        first_of, second_of = {}, {}

                        def stages(x, r_, i, ok):
                            if r_ == 0:
                                if ok(x - 1):
                                    first_of[0] = expert(pe, x - 1)
                                if ok(x - 3):
                                    second_of[0] = expert(pe, x - 3)
                            b, q = x, r_ % 2
                            if ok(b):
                                pe.wait_ge(*loads[r_](i + 1))
                                pe.wait_ge(*xT_ready(b - 1))
                                pe.transpose(B[q][:, 0:P], xb[:, r_, :], ident).then_inc(x_turned.sem, 1)
                            b, q = x - 1, (r_ - 1) % 2
                            if ok(b):
                                e = first_of[r_]
                                if r_ < 2:
                                    second_of[r_ + 2] = e
                                pe.wait_ge(*xT_ready(b + 1))
                                pe.wait_ge(*u_ready(b - 1))
                                pe.matmul(B[2 + q][:], xT[:, q, :], W1[:, bass.ds(e, 1), :].rearrange("p e f -> p (e f)"),
                                          start=True, stop=True).then_inc(u_psum.sem, 1)
                            b, q = x - 2, r_ % 2
                            if ok(b):
                                pe.wait_ge(*u_ready(b + 1))
                                pe.wait_ge(*h_ready(b - 1))
                                for c in range(4):
                                    ins = pe.transpose(B[4 + q][:, c * P:(c + 1) * P], u[:, q, c * P:(c + 1) * P], ident)
                                ins.then_inc(uT_psum.sem, 1)
                            if r_ < 3 and ok(x):
                                first_of[r_ + 1] = expert(pe, x)
                            if r_ == 0 and ok(x - 2):
                                second_of[1] = expert(pe, x - 2)
                            b, q = x - 3, (r_ - 3) % 2
                            if ok(b):
                                e = second_of[r_]
                                pe.wait_ge(*h_ready(b + 1))
                                pe.wait_ge(*yb_ready(b - 1))
                                pe.sem_inc(sig.sems["pe_passed"], 1)
                                for c in range(4):
                                    ins = pe.matmul(B[6 + q][:, 0:P], hT[:, q, c * P:(c + 1) * P],
                                                    W2[:, bass.ds(e, 1), c, :].rearrange("p e n -> p (e n)"),
                                                    start=(c == 0), stop=(c == 3))
                                ins.then_inc(yb_psum.sem, 1)
                        run(pe, stages)

                    @block.scalar
                    def _(act):
                        act.wait_ge(*w2_loaded(5))

                        def stages(x, r_, i, ok):
                            b, q = x - 2, r_ % 2
                            if ok(b):
                                e = expert(act, b)
                                act.wait_ge(*uT_psum(b + 1))
                                act.wait_ge(*yb_psum(b - 1))
                                act.sem_inc(sig.sems["act_passed"], 1)
                                for c in range(4):
                                    ins = act.activation(hT[:, q, c * P:(c + 1) * P], B[4 + q][:, c * P:(c + 1) * P], ACT.Gelu,
                                                         bias=B1[:, bass.ds(e, 1), c])
                                ins.then_inc(h_ready.sem, 1)
                        run(act, stages)

                    @block.vector
                    def _(dve):
                        def stages(x, r_, i, ok):
                            b, q = x, r_ % 2
                            if ok(b):
                                dve.wait_ge(*x_turned(b + 1))
                                dve.wait_ge(*u_psum(b - 1))
                                dve.tensor_copy(xT[:, q, :], B[q][:, 0:P]).then_inc(xT_ready.sem, 1)
                            b, q = x - 1, (r_ - 1) % 2
                            if ok(b):
                                dve.wait_ge(*u_psum(b + 1))
                                dve.wait_ge(*uT_psum(b - 1))
                                dve.tensor_copy(u[:, q, :], B[2 + q][:]).then_inc(u_ready.sem, 1)
                            b, q, j = x - 3, (r_ - 3) % 2, (r_ - 3) % 4
                            if ok(b):
                                dve.wait_ge(*yb_psum(b + 1))
                                if not isinstance(b, int) or b >= 4:
                                    dve.wait_ge(*stores[j](i if r_ == 3 else i - 1))
                                dve.tensor_copy(yb[:, j, :], B[6 + q][:, 0:P]).then_inc(yb_ready.sem, 1)
                        run(dve, stages)

                yg = sb2("yg", [P, 4, P])
                rows_back = [sig(f"rows_back{k}", TILES) for k in range(2)]
                x_added = sig("x_added", 2 * TILES)
                block = c2.enter_context(nc.Block())

                @block.gpsimd
                def _(pool):
                    for t in range(TILES):
                        for k in range(2):
                            pool.wait_ge(*x_added(2 * t + k - 3))
                            pool.indirect_dma_start(yg[:, (t % 2) * 2 + k, :], None, T["pair_outs"][0:blocks * P, :],
                                                    bass.IndirectOffsetOnAxis(ap=back[:, k, t:t + 1], axis=0))\
                                .then_inc(rows_back[t % 2].sem, 16)

                @block.vector
                def _(dve):
                    for t in range(TILES):
                        dve.wait_ge(*rows_back[t % 2](2 * (t // 2 + 1)))
                        for k in range(2):
                            dve.wait_ge(*x_added(2 * t + k))
                            dve.scalar_tensor_tensor(out=X[:, t, :], in0=yg[:, (t % 2) * 2 + k, :], scalar=g[k][:, t:t + 1],
                                                     in1=X[:, t, :], op0=ALU.mult, op1=ALU.add).then_inc(x_added.sem, 1)

        def moe(kind, E, blocks, gw, bias_row, w1, b1, w2, b2, add_back):
            with ExitStack() as c0:
                def sb2(n, shape):
                    return hold(c0, n, shape)
                send, back = (c0.enter_context(nc.sbuf_tensor(f"{n}_{kind}", [P, 2, TILES], I32)) for n in ("send", "back"))
                expert_of = c0.enter_context(nc.sbuf_tensor(f"expert_of_{kind}", [1, blocks], I32))
                g1, g2 = sb2("g1", [P, TILES]), sb2("g2", [P, TILES])
                W1 = sb2("W1", [P, E, 4 * P])
                w1_loaded = sig("w_loaded1", 1)
                with ExitStack() as c1:
                    XN = hold(c1, "XN", [P, TILES, P])
                    Cmb, M1, M2 = (hold(c1, n, [P, TILES, E]) for n in ("Cmb", "M1", "M2"))
                    norm(add_back, XN, lambda sp: sp.dma_start(W1[:], w1.rearrange("e p f -> p e f")).then_inc(w1_loaded.sem, 16))
                    route(kind, Cmb, E - (kind == "capacity"), gw, bias_row, (M1, M2, g1, g2))
                    send_rows = dispatch(E, XN, M1, M2, send, back, expert_of, blocks)
                    expert_bias(Cmb, E, b2, send_rows)
                sparse_experts(E, W1, w1_loaded, w2, b1, (g1, g2), back, expert_of, blocks)

        def key_rows():
            with ExitStack() as c2:
                fs, tk = hold(c2, "fs", [P, KEYS]), hold(c2, "tk", [P, 2, KEYS])
                ti = c2.enter_context(nc.sbuf_tensor("ti", [P, KEYS], I32))
                row_loaded, stored = sig("row_loaded", 2), sig("stored", 3)
                a_done, b_done, c_done, ln_done = (sig(n, 1) for n in ("a_done", "b_done", "c_done", "d_done"))
                block = c2.enter_context(nc.Block())

                @block.sync
                def _(sp):
                    sp.dma_start(fs[:], T["key_weights"]).then_inc(row_loaded.sem, 16)
                    sp.dma_start(ti[:], T["key_tokens"]).then_inc(row_loaded.sem, 16)
                    sp.wait_ge(*b_done(1))
                    sp.dma_start(T["rows_x2"], fs[:]).then_inc(stored.sem, 16)
                    sp.wait_ge(*c_done(1))
                    sp.dma_start(T["rows_x3"], tk[:, 0, :]).then_inc(stored.sem, 16)
                    sp.dma_start(T["rows_keep"], tk[:, 1, :]).then_inc(stored.sem, 16)
                    sp.wait_ge(*stored(3))

                @block.scalar
                def _(act):
                    act.wait_ge(*a_done(1))
                    act.activation(fs[:], fs[:], ACT.Ln).then_inc(ln_done.sem, 1)

                @block.vector
                def _(dve):
                    st_ = Steps(dve, sig, "dve_step")
                    dve.wait_ge(*row_loaded(2))
                    st_.link(dve.tensor_scalar(fs[:], fs[:], 1e-20, None, ALU.add))
                    dve.tensor_scalar(fs[:], fs[:], 2.0 ** 40, None, ALU.mult).then_inc(a_done.sem, 1)
                    st_.link(dve.tensor_scalar(tk[:, 0, :], ti[:], 0, None, ALU.is_equal))
                    st_.link(dve.tensor_scalar(tk[:, 1, :], tk[:, 0, :], -1.0, 1.0, ALU.mult, ALU.add))
                    dve.tensor_scalar(tk[:, 0, :], tk[:, 0, :], -1.0e9 / 8 ** 0.5, None, ALU.mult).then_inc(c_done.sem, 1)
                    dve.wait_ge(*ln_done(1))
                    dve.tensor_scalar(fs[:], fs[:], -40 * 0.6931471805599453, None, ALU.add).then_inc(b_done.sem, 1)
                    st_.close()

        def xattn(name):
            bias = name != "x3"
            with ExitStack() as c2:
                def sb2(n, shape):
                    return hold(c2, n, shape)
                QT = sb2("QT", [P, TILES * P])
                project([(QT, w(name + "_q"), XNT, v(name + "_bq" if bias else "zero"), 8 ** -0.5)])
                ct = [sb2("ct", [P, KEYS]) for _ in range(4)]
                rows = [sb2("rows", [P, KEYS]) for _ in range(4)] if name != "x1" else None
                keep = [sb2("keep", [P, KEYS]) for _ in range(4)] if name == "x3" else None
                qb = sb2("qb", [P, 2, 4, S])
                kT = sb2("kT", [P, 2, KEYS])
                vs = sb2("vs", [P, 4, 2 * P])
                vl = sb2("vl", [4, 4, P])
                sx = sb2("sx", [P, 2, 4, KEYS])
                nm, sm, rs = sb2("nm", [P, 2, 4]), sb2("sm", [P, 4, 4]), sb2("rs", [P, 4])
                pt, pl = sb2("pt", [P, 2, 2, 4 * P]), sb2("pl", [4, 2, P])
                a = sb2("a", [P, 2, P])
                oT = sb2("oT", [P, P])
                maskq = sb2("maskq", [P, KEYS])
                N = NB
                per_load = 1 + (rows is not None) + (keep is not None)
                loads = [sig(f"ct_loaded{j}", per_load * N // 4) for j in range(4)]
                q_built, k_psum, kv_psum, k_ready, v_ready = (sig(n, N) for n in ("q_built", "k_psum", "kv_psum", "k_ready", "v_ready"))
                scores, s_summed, exp_done = sig("scores", 4 * N), sig("s_summed", 4 * N), sig("exp_done", N)
                pT_psum, pT_ready, av_psum, a_ready, o_ready = (
                    sig(n, N) for n in ("pT_psum", "pT_ready", "av_psum", "a_ready", "o_ready"))
                p_ready, pT2_psum, pT2_ready = (sig(n, N) for n in ("probs_ready", "pT2_psum", "pT2_ready"))
                pl_psum, pl_ready = sig("pl_psum", N), sig("pl_ready", N)
                y_psum, x_added = sig("y_psum", TILES), sig("x_added", TILES)
                row_loaded = sig("row_loaded", 4 if name == "x1" else 0)
                vs_copied = sig("v_built", N if keep is not None else 0)
                DEPTH = 4
                block = c2.enter_context(nc.Block())

                def run(eng, stages, steps=None, per=0):
                    for x in range(8):
                        stages(x, x % 4, x // 4, lambda b: 0 <= b < N)
                    with (steps.loop(2, N // 4, per) if steps else eng.Fori(2, N // 4)) as i:
                        for r_ in range(4):
                            stages(i * 4 + r_, r_, i, lambda b: True)
                    for x in range(N, N + DEPTH):
                        stages(x, x % 4, x // 4, lambda b: 0 <= b < N)

                @block.sync
                def _(sp):
                    if name == "x1":
                        for A in range(4):
                            sp.dma_start(maskq[32 * A:32 * A + 32, :], T["mask"]).then_inc(row_loaded.sem, 16)

                    def load(b, j):
                        sp.wait_ge(*kv_psum(b - 3))
                        sp.dma_start(ct[j][:], T["ctxT"].rearrange("p (b k) -> p b k", k=KEYS)[:, bass.ds(b, 1), :]
                                     .rearrange("p b k -> p (b k)")).then_inc(loads[j].sem, 16)
                        if rows is not None:
                            sp.wait_ge(*s_summed(4 * (b - 3)))
                            sp.dma_start(rows[j][:], T["rows_" + name][bass.ds(b, 1), :].to_broadcast([P, KEYS]))\
                                .then_inc(loads[j].sem, 16)
                        if keep is not None:
                            sp.wait_ge(*k_ready(b - 3))
                            sp.dma_start(keep[j][:], T["rows_keep"][bass.ds(b, 1), :].to_broadcast([P, KEYS]))\
                                .then_inc(loads[j].sem, 16)
                    with sp.Fori(0, N // 4) as i:
                        for j in range(4):
                            load(i * 4 + j, j)

                @block.gpsimd
                def _(pool):
                    def build(b, q):
                        pool.wait_ge(*scores(4 * (b - 1)))
                        pool.tensor_tensor(qb[:, q], QT[:, bass.ds(b * S, S)].unsqueeze(1).to_broadcast([P, 4, S]),
                                           const("head").unsqueeze(2).to_broadcast([P, 4, S]), ALU.mult)\
                            .then_inc(q_built.sem, 1)
                    with pool.Fori(0, N // 2) as i:
                        for q in range(2):
                            build(i * 2 + q, q)

                @block.tensor
                def _(pe):
                    def read_scores(x, n):
                        k = 4 * (x - 1) + n
                        return s_summed(max(0, min(k, 4 * N)) if isinstance(k, int) else k)

                    def stages(x, r_, i, ok):
                        b, j = x, r_
                        if ok(b):
                            pe.wait_ge(*loads[j](per_load * (i + 1)))
                            pe.wait_ge(*k_ready(b))
                            pe.wait_ge(*v_ready(b))
                            pe.matmul(B[4][:, 0:KEYS], w(name + "_k"), ct[j][:], start=True, stop=True).then_inc(k_psum.sem, 1)
                            pe.matmul(B[5][0:4, 256:384], ct[j][:, 256:257].to_broadcast([P, 4]), w(name + "_v"),
                                      start=True, stop=True)
                            for c in range(2):
                                ins = pe.matmul(B[5][:, c * P:(c + 1) * P], ct[j][:, c * P:(c + 1) * P], w(name + "_v"),
                                                start=True, stop=True)
                            ins.then_inc(kv_psum.sem, 1)
                        b, q = x - 1, (r_ - 1) % 2
                        if ok(b):
                            pe.wait_ge(*k_ready(b + 1))
                            pe.wait_ge(*q_built(b + 1))
                            for h in range(4):
                                if h == 0:
                                    pe.wait_ge(*a_ready(b - 2))
                                elif h == 2 and r_ == 0:
                                    pe.wait_ge(*x_added(i - 1))
                                elif h == 3:
                                    pe.wait_ge(*pl_ready(b - 1))
                                pe.wait_ge(*s_summed(4 * (b - 1) + h + 1))
                                p = slice(32 * h, 32 * h + 32)
                                pe.matmul(B[h][:, 0:KEYS], qb[p, q].rearrange("p j s -> p (j s)"), kT[p, q, :],
                                          start=True, stop=True, tile_position=(32 * h, 0)).then_inc(scores.sem, 1)
                        b, q = x - 2, r_ % 2
                        if ok(b):
                            pe.wait_ge(*p_ready(b + 1))
                            pe.wait_ge(*pT_ready(b))
                            pe.wait_ge(*pT2_ready(b))
                            for c in range(2):
                                for h in range(4):
                                    ins = pe.transpose(B[6 + c][:, h * P:(h + 1) * P], sx[:, q, h, c * P:(c + 1) * P], ident)
                                ins.then_inc((pT_psum if c == 0 else pT2_psum).sem, 1)
                        if r_ == 3 and ok(x - 4):
                            pe.wait_ge(*o_ready(x - 3))
                            pe.wait_ge(*read_scores(x, 3))
                            pe.matmul(B[2][:, 384:512], ones_row, r(name + "_bo"), start=True, stop=False)
                            pe.matmul(B[2][:, 384:512], oT[:], w(name + "_o"), start=False, stop=True).then_inc(y_psum.sem, 1)
                        b, q = x - 3, (r_ - 3) % 2
                        if ok(b):
                            pe.wait_ge(*pT_ready(b + 1))
                            pe.wait_ge(*pT2_ready(b + 1))
                            pe.wait_ge(*pl_ready(b + 1))
                            pe.wait_ge(*a_ready(b))
                            pe.wait_ge(*read_scores(x, 1))
                            for h in range(4):
                                vj = (r_ - 3) % 4
                                out_h = B[0][32 * h:32 * h + 32, 384:512]
                                for c in range(2):
                                    pe.matmul(out_h, vs[:, vj, c * P + 32 * h:c * P + 32 * h + 32],
                                              pt[:, q, c, h * P:(h + 1) * P], start=(c == 0), stop=False,
                                              tile_position=(0, 32 * h))
                                ins = pe.matmul(out_h, vl[:, vj, 32 * h:32 * h + 32], pl[:, q, :], start=False, stop=True,
                                                tile_position=(0, 32 * h))
                            ins.then_inc(av_psum.sem, 1)
                        b, q = x - 2, r_ % 2
                        if ok(b):
                            pe.wait_ge(*pl_ready(b))
                            pe.wait_ge(*read_scores(x, 4))
                            pe.transpose(B[3][0:4, 384:512], sx[:, q, :, 256], ident).then_inc(pl_psum.sem, 1)
                    run(pe, stages)

                @block.scalar
                def _(act):
                    def stages(x, r_, i, ok):
                        b, q, j = x, r_ % 2, r_
                        if ok(b):
                            if keep is None:
                                act.wait_ge(*k_psum(b + 1))
                                act.wait_ge(*scores(4 * (b - 1)))
                                act.activation(kT[:, q, :], B[4][:, 0:KEYS], ACT.Identity, bias=v(name + "_bk")).then_inc(k_ready.sem, 1)
                            else:
                                act.wait_ge(*kv_psum(b + 1))
                                act.wait_ge(*av_psum(b - 3))
                                act.copy(vs[:, j, :], B[5][:, 0:2 * P]).then_inc(vs_copied.sem, 1)
                        b, q = x - 1, (r_ - 1) % 2
                        if ok(b):
                            for h in range(4):
                                act.wait_ge(*s_summed(4 * b + h + 1))
                                ins = act.activation(sx[:, q, h, :], sx[:, q, h, :], ACT.Exp, bias=nm[:, q, h:h + 1], scale=-1.0,
                                                     accum_out=sm[:, (r_ - 1) % 4, h:h + 1])
                            ins.then_inc(exp_done.sem, 1)
                        b, q = x - 2, r_ % 2
                        if ok(b):
                            act.wait_ge(*pT2_psum(b + 1))
                            act.wait_ge(*av_psum(b - 1))
                            act.copy(pt[:, q, 1, :], B[7][:]).then_inc(pT2_ready.sem, 1)
                    run(act, stages)

                @block.vector
                def _(dve):
                    st_ = Steps(dve, sig, "dve_step")
                    if name == "x1":
                        dve.wait_ge(*row_loaded(4))
                        st_.link(dve.tensor_scalar(maskq[:], maskq[:], -1.0e9, None, ALU.mult))

                    def stages(x, r_, i, ok):
                        b, q, j = x - 2, r_ % 2, (r_ - 2) % 4
                        if ok(b):
                            dve.wait_ge(*exp_done(b + 1))
                            st_.link(dve.reciprocal(rs[:], sm[:, j, :]))
                            for h in range(4):
                                ins = dve.tensor_scalar(sx[:, q, h, :], sx[:, q, h, :], rs[:, h:h + 1], None, ALU.mult)
                            ins.then_inc(p_ready.sem, 1)
                        b, q, j = x - 1, (r_ - 1) % 2, (r_ - 1) % 4
                        if ok(b):
                            dve.wait_ge(*pl_psum(b - 1))
                            add = maskq[:] if rows is None else rows[j][:]
                            for h in range(4):
                                dve.wait_ge(*scores(4 * b + h + 1))
                                dve.sem_inc(sig.sems["dve_passed"], 1)
                                dve.tensor_tensor_reduce(sx[:, q, h, :], B[h][:, 0:KEYS], add, -1.0, 3.0e38, ALU.add, ALU.min,
                                                         nm[:, q, h:h + 1]).then_inc(s_summed.sem, 1)
                        b, q, j = x, r_ % 2, r_
                        if ok(b):
                            if keep is not None:
                                dve.wait_ge(*k_psum(b + 1))
                                dve.wait_ge(*scores(4 * (b - 1)))
                                dve.tensor_tensor(kT[:, q, :], B[4][:, 0:KEYS], keep[j][:], ALU.mult).then_inc(k_ready.sem, 1)
                            dve.wait_ge(*kv_psum(b + 1))
                            dve.wait_ge(*av_psum(b - 3))
                            if keep is None:
                                st_.count(dve.tensor_copy(vs[:, j, :], B[5][:, 0:2 * P]))
                                st_.wait()
                            else:
                                dve.wait_ge(*vs_copied(b + 1))
                            dve.tensor_tensor(vl[:, j, :], B[5][0:4, 256:384], const("mask4")[0:4, :], ALU.mult)\
                                .then_inc(v_ready.sem, 1)
                        b, q = x - 2, r_ % 2
                        if ok(b):
                            dve.wait_ge(*pT_psum(b + 1))
                            dve.wait_ge(*av_psum(b - 1))
                            dve.tensor_copy(pt[:, q, 0, :], B[6][:]).then_inc(pT_ready.sem, 1)
                        b, q = x - 3, (r_ - 3) % 2
                        if ok(b):
                            dve.wait_ge(*av_psum(b + 1))
                            dve.scalar_tensor_tensor(out=a[:, q].rearrange("p (j s) -> p j s", j=4),
                                                     in0=B[0][:, 384:512].rearrange("p (j s) -> p j s", j=4),
                                                     scalar=v(name + "_bv" if bias else "zero"),
                                                     in1=const("head").unsqueeze(2).to_broadcast([P, 4, S]),
                                                     op0=ALU.add, op1=ALU.mult).then_inc(a_ready.sem, 1)
                            dve.wait_ge(*a_ready(b + 1))
                            if r_ == 3:
                                dve.wait_ge(*y_psum(i))
                            dve.tensor_reduce(oT[:, ((r_ - 3) % 4) * S:((r_ - 3) % 4) * S + S],
                                              a[:, q].rearrange("p (j s) -> p s j", j=4), AX.X, ALU.add)\
                                .then_inc(o_ready.sem, 1)
                        b, q = x - 2, r_ % 2
                        if ok(b):
                            dve.wait_ge(*pl_psum(b + 1))
                            dve.wait_ge(*av_psum(b - 1))
                            dve.tensor_copy(pl[:, q, :], B[3][0:4, 384:512]).then_inc(pl_ready.sem, 1)
                        if r_ == 3 and ok(x - 4):
                            dve.wait_ge(*y_psum(i))
                            xt_ = X[:, bass.ds(i - 1, 1), :]
                            dve.tensor_tensor(xt_, xt_, B[2][:, 384:512].unsqueeze(1), ALU.add).then_inc(x_added.sem, 1)
                    run(dve, stages, st_, 4 * (2 if keep is None else 1))
                    st_.close()

        def butterfly_ffn():
            H2 = 512
            with ExitStack() as c2:
                def sb2(n, shape):
                    return hold(c2, n, shape)
                W1, W2, B1 = sb2("W1", [P, 1, H2]), sb2("W2", [P, 1, 4, P]), sb2("B1", [P, 1, 4])
                with ExitStack() as c3:
                    wu, wd = (hold(c3, n, [P, 9, 2 * H2]) for n in ("wu", "wd"))
                    U = hold(c3, "U", [P, 2, H2])
                    D = hold(c3, "D", [P, H2])
                    ready_early = sig("w_loaded0", 4)

                    def fetch(sp):
                        sp.dma_start(wu[:], T["up_w"].rearrange("s n -> (s n)").unsqueeze(0).to_broadcast([P, 9 * 2 * H2])
                                     .rearrange("p (s n) -> p s n", s=9)).then_inc(ready_early.sem, 16)
                        sp.dma_start(wd[:], T["down_w"].rearrange("s n -> (s n)").unsqueeze(0).to_broadcast([P, 9 * 2 * H2])
                                     .rearrange("p (s n) -> p s n", s=9)).then_inc(ready_early.sem, 16)
                        sp.dma_start(U[:, 0, :], T["W_exp"]).then_inc(ready_early.sem, 16)
                        sp.dma_start(D[:], T["W_conT"]).then_inc(ready_early.sem, 16)
                    norm(fetch=fetch)
                    tu = [hold(c3, "tu", [P, 2, H2 // 2]) for _ in range(4)]
                    td_ = [hold(c3, "td", [P, H2 // 2]) for _ in range(4)]
                    both = hold(c3, "both", [P, P])
                    w_loaded = sig("w_loaded", 1)
                    a_done, b_done, c_done, d_done = (sig(n, 1) for n in ("a_done", "b_done", "c_done", "d_done"))
                    copied = sig("copied", 1)
                    block = c3.enter_context(nc.Block())

                    @block.sync
                    def _(sp):
                        sp.wait_ge(*copied(1))
                        sp.dma_start(U[0:1, 1, :], T["b_exp"]).then_inc(w_loaded.sem, 16)

                    def weights_of(wt, s, st):
                        return wt[:, s, :].rearrange("p (n t i j) -> p n t i j", t=st, i=2, j=2)

                    @block.vector
                    def _(dve):
                        st_ = Steps(dve, sig, "dve_step")
                        dve.memset(U[:, 1, :], 0.0).then_inc(copied.sem, 1)
                        dve.wait_ge(*ready_early(4))
                        dve.wait_ge(*w_loaded(1))
                        for s in range(9):
                            st = 1 << s
                            n = H2 // (2 * st)
                            u = U[:].rearrange("p c (n i t) -> p c n i t", i=2, t=st)
                            ww = weights_of(wu, s, st)
                            for k in range(4):
                                o, i = k // 2, k % 2
                                for c in range(2):
                                    st_.count(dve.tensor_tensor(
                                        tu[k][:, c, :].rearrange("p (n t) -> p n t", t=st), u[:, c, :, i, :], ww[:, :, :, o, i], ALU.mult))
                            st_.wait()
                            for o in range(2):
                                for c in range(2):
                                    st_.count(dve.tensor_tensor(
                                        u[:, c, :, o, :], tu[2 * o][:, c, :].rearrange("p (n t) -> p n t", t=st),
                                        tu[2 * o + 1][:, c, :].rearrange("p (n t) -> p n t", t=st), ALU.add))
                            st_.wait()
                        dve.tensor_copy(W1[:, 0, :], U[:, 0, :]).then_inc(a_done.sem, 1)
                        dve.wait_ge(*b_done(1))
                        st_.count(dve.tensor_tensor(B1[:, 0, :], B[1][:, 0:4], V[:, VAT["up_b0"]:VAT["up_b0"] + 4], ALU.add))
                        st_.link(dve.tensor_copy(both[:], B[2][:, 0:P]))
                        st_.count(dve.tensor_tensor(X[:], X[:], both[:].unsqueeze(1).to_broadcast([P, TILES, P]), ALU.add))
                        dve.wait_ge(*d_done(1))
                        st_.count(dve.tensor_copy(W2[:, 0].rearrange("p c n -> p (c n)"), B[0][:]))
                        st_.wait()
                        st_.close()

                    @block.gpsimd
                    def _(pool):
                        st_ = Steps(pool, sig, "pool_step")
                        pool.wait_ge(*ready_early(4))
                        for s in reversed(range(9)):
                            st = 1 << s
                            d = D[:].rearrange("p (n i t) -> p n i t", i=2, t=st)
                            ww = weights_of(wd, s, st)
                            for k in range(4):
                                o, i = k // 2, k % 2
                                st_.count(pool.tensor_tensor(td_[k][:].rearrange("p (n t) -> p n t", t=st), d[:, :, i, :],
                                                             ww[:, :, :, i, o], ALU.mult))
                            st_.wait()
                            for o in range(2):
                                st_.count(pool.tensor_tensor(d[:, :, o, :], td_[2 * o][:].rearrange("p (n t) -> p n t", t=st),
                                                             td_[2 * o + 1][:].rearrange("p (n t) -> p n t", t=st), ALU.add))
                            st_.wait()
                        st_.close()
                        pool.sem_inc(c_done.sem, 1)

                    @block.tensor
                    def _(pe):
                        pe.matmul(B[2][:, 0:P], ones_row, r("b_con"), start=True, stop=False)
                        pe.matmul(B[2][:, 0:P], ones_row, r("down_bias"), start=False, stop=True)
                        pe.wait_ge(*a_done(1))
                        for c in range(4):
                            ins = pe.matmul(B[1][:, c:c + 1], U[0:1, 1, c * P:(c + 1) * P], ones_row[:, 0:1], start=True, stop=True)
                        ins.then_inc(b_done.sem, 1)
                        pe.wait_ge(*c_done(1))
                        for c in range(4):
                            ins = pe.transpose(B[0][:, c * P:(c + 1) * P], D[:, c * P:(c + 1) * P], ident)
                        ins.then_inc(d_done.sem, 1)
                experts(1, 4, X, None, None, None, None, ready=(W1, W2, B1))

        def norm_affine_add(Y):
            with ExitStack() as c2:
                def sb2(n, shape):
                    return hold(c2, n, shape)
                st, var, dif = sb2("stats", [P, TILES, 6]), sb2("var", [P, TILES]), sb2("dif", [P, TILES])
                gb = sb2("gb", [P, 2, P])
                yn = sb2("yn", [P, 2, GT, P])
                var_ready, rstd_ready, a_done = sig("var_ready", 1), sig("rstd_ready", 1), sig("a_done", 1)
                x_added, stored = sig("x_added", 8), sig("stored", 8)
                block = c2.enter_context(nc.Block())

                @block.tensor
                def _(pe):
                    pe.matmul(B[0][:, 0:P], ones_row, r("gamma"), start=True, stop=True)
                    pe.matmul(B[0][:, P:2 * P], ones_row, r("beta"), start=True, stop=True).then_inc(a_done.sem, 1)

                @block.scalar
                def _(act):
                    st_ = Steps(act, sig, "act_step")
                    act.wait_ge(*var_ready(1))
                    st_.link(act.activation(var[:], var[:], ACT.Ln))
                    act.activation(rstd[:], var[:], ACT.Exp, scale=-0.5).then_inc(rstd_ready.sem, 1)
                    st_.close()

                @block.vector
                def _(dve):
                    st_ = Steps(dve, sig, "dve_step")
                    with st_.loop(0, GROUPS, GT) as g:
                        for j in range(GT):
                            st_.count(dve.bn_stats(st[:, bass.ds(g * GT + j, 1), :], Y[:, bass.ds(g * GT + j, 1), :]))
                    dve.wait_ge(*a_done(1))
                    st_.count(dve.tensor_copy(gb[:].rearrange("p a b -> p (a b)"), B[0][:, 0:2 * P]))
                    st_.wait()
                    st_.count(dve.tensor_tensor(mean[:], st[:, :, 1], st[:, :, 4], ALU.add))
                    st_.count(dve.tensor_tensor(dif[:], st[:, :, 1], st[:, :, 4], ALU.subtract))
                    st_.link(dve.tensor_tensor(var[:], st[:, :, 2], st[:, :, 5], ALU.add))
                    st_.count(dve.tensor_scalar(mean[:], mean[:], 0.5, None, ALU.mult))
                    st_.count(dve.tensor_scalar(var[:], var[:], 1.0 / P, EPS, ALU.mult, ALU.add))
                    st_.link(dve.tensor_tensor(dif[:], dif[:], dif[:], ALU.mult))
                    dve.scalar_tensor_tensor(out=var[:], in0=dif[:], scalar=0.25, in1=var[:],
                                             op0=ALU.mult, op1=ALU.add).then_inc(var_ready.sem, 1)
                    dve.wait_ge(*rstd_ready(1))
                    with st_.loop(0, GROUPS // 2, 12) as i:
                        for q in range(2):
                            g = i * 2 + q
                            for j in range(GT):
                                t = g * GT + j
                                st_.count(dve.tensor_scalar(yn[:, q, j, :], Y[:, bass.ds(t, 1), :], mean[:, bass.ds(t, 1)],
                                                            rstd[:, bass.ds(t, 1)], ALU.subtract, ALU.mult))
                            st_.wait()
                            st_.link(dve.tensor_tensor(yn[:, q], yn[:, q], gb[:, 0, :].unsqueeze(1).to_broadcast([P, GT, P]), ALU.mult))
                            st_.link(dve.tensor_tensor(yn[:, q], yn[:, q], gb[:, 1, :].unsqueeze(1).to_broadcast([P, GT, P]), ALU.add))
                            xg = X[:, bass.ds(g * GT, GT), :]
                            dve.tensor_tensor(xg, xg, yn[:, q], ALU.add).then_inc(x_added.sem, 1)
                    st_.close()

                @block.sync
                def _(sp):
                    with sp.Fori(0, GROUPS) as g:
                        sp.wait_ge(*x_added(g + 1))
                        sp.dma_start(ot[:, bass.ds(g * GT, GT), :], X[:, bass.ds(g * GT, GT), :]).then_inc(stored.sem, 16)
                    sp.wait_ge(*stored(8))

        with ExitStack() as c0:
            ctx0 = hold(c0, "ctx0", [P, TILES * P])
            ctx_loaded = sig("ctx_loaded", 1)
            norm(fetch=lambda sp: sp.dma_start(ctx0[:], T["ctx_causal"]).then_inc(ctx_loaded.sem, 16))
            with nc.Block() as block:
                @block.sync
                def _(sp):
                    sp.wait_ge(*ctx_loaded(1))
                    sp.wait_ge(*rest_loaded(7))
            attn16("x0", ctx0, "x0_bv", "x0_bo", True)
        norm()
        rwkv()
        moe("pairs", 24, 2 * TILES + 24 - 1, GW0[:], GB[:], T["L0_w1"], T["L0_b1"], T["L0_w2"], T["L0_b2"], True)

        key_rows()
        norm()
        xattn("x1")
        attn8()
        butterfly_ffn()
        norm()
        xattn("x2")
        norm()
        rglru()
        moe("capacity", 9, 2 * TILES + 9 - 1, GW2[:], None, T["L2_w1"], T["L2_b1"], T["L2_w2"], T["L2_b2"], False)
        norm()
        xattn("x3")
        norm()
        attn16("a3", XNT, "a3_bv", "a3_bo", False)
        norm()
        with ExitStack() as c0:
            Cmb, Y = hold(c0, "Cmb", [P, TILES, 8]), hold(c0, "Y", [P, TILES, P])
            with nc.Block() as block:
                @block.vector
                def _(dve):
                    dve.memset(Y[:], 0.0)
            route("first", Cmb, 8, GW3[:])
            experts(8, 2, Y, Cmb, T["L3_w1"], T["L3_b1"], T["L3_w2"])
            norm_affine_add(Y)


def layout(inputs):
    import numpy as np
    a = {k: np.asarray(x) for k, x in inputs.items()}
    f = np.float32
    out = {"x": a["x"]}
    ctxT = np.ascontiguousarray(np.transpose(a["ctx_1024"], (2, 0, 1)))
    out["ctxT"] = ctxT.reshape(P, NB * KEYS)
    out["ctx_causal"] = np.ascontiguousarray(ctxT[:, :, :S]).reshape(P, NB * S)
    ws = {}
    for n in "qkvo":
        ws["x0_" + n] = a["L0_xattn_W" + n].T
        ws["x2_" + n] = a["L2_xattn_w" + n]
        ws["x3_" + n] = a["L3_xattn_W" + n]
    ws["a0_v"], ws["a0_r"], ws["a0_o"] = a["L0_attn_value_w"].T, a["L0_attn_recep_w"].T, a["L0_attn_out_w"].T
    for n in "qkv":
        ws["x1_" + n] = a[f"L1_xattn_w{n}_w"].T
    ws["x1_o"] = a["L1_xattn_dense_w"].T
    for i, n in enumerate("qkv"):
        ws["a3_" + n] = a["L3_attn_in_proj_w"][i * P:(i + 1) * P].T
    ws["a3_o"] = a["L3_attn_out_proj_w"].T
    for n, k in (("a2_i", "L2_attn_ig_w"), ("a2_a", "L2_attn_ag_w")):
        bd = np.zeros((P, P), f)
        for h in range(8):
            bd[16 * h:16 * h + 16, 16 * h:16 * h + 16] = a[k][h]
        ws[n] = bd
    for c in range(4):
        ws[f"a1_q{c}"] = a["L1_attn_Wq"][:, c * P:(c + 1) * P]
        ws[f"a1_k{c}"] = a["L1_attn_Wkv"][:, c * P:(c + 1) * P]
        ws[f"a1_v{c}"] = a["L1_attn_Wkv"][:, 512:].reshape(P, 4, 4, 32)[:, :, c, :].reshape(P, P)
        ws[f"a1_o{c}"] = a["L1_attn_Wo"][c * P:(c + 1) * P, :]
    out["weights"] = np.ascontiguousarray(np.stack([ws[n] for n in SLOTS], axis=1))
    z = np.zeros(P, f)
    vs = {"x0_bq": a["L0_xattn_bq"], "x0_bk": a["L0_xattn_bk"], "x0_bv": a["L0_xattn_bv"],
          "x1_bq": a["L1_xattn_wq_b"], "x1_bk": a["L1_xattn_wk_b"], "x1_bv": a["L1_xattn_wv_b"],
          "x2_bq": a["L2_xattn_bq"], "x2_bk": a["L2_xattn_bk"], "x2_bv": a["L2_xattn_bv"],
          "a3_bq": a["L3_attn_in_proj_b"][:P], "a3_bk": a["L3_attn_in_proj_b"][P:2 * P],
          "a3_bv": a["L3_attn_in_proj_b"][2 * P:], "zero": z, "time_decay": a["L0_attn_time_decay"],
          "time_first": a["L0_attn_time_first"], "a_param": a["L2_attn_a_param"],
          "ig_b": a["L2_attn_ig_b"].reshape(P), "ag_b": a["L2_attn_ag_b"].reshape(P)}
    for c in range(4):
        vs[f"up_b{c}"] = a["L1_ffn_up_bias"][c * P:(c + 1) * P]
    out["vecs"] = np.ascontiguousarray(np.stack([vs[n] for n in VECS], axis=1))
    rs = {"x0_bo": a["L0_xattn_bo"], "x1_bo": a["L1_xattn_dense_b"], "a1_bo": a["L1_attn_bo"],
          "x2_bo": a["L2_xattn_bo"], "x3_bo": a["L3_xattn_bo"], "a3_bo": a["L3_attn_out_proj_b"],
          "b_con": a["L1_ffn_b_con"], "down_bias": a["L1_ffn_down_bias"], "gamma": a["L3_ffn_ln_gamma"],
          "beta": a["L3_ffn_ln_beta"], "zero": z}
    out["rows"] = np.ascontiguousarray(np.stack([rs[n] for n in ROWS], axis=0))[None]
    p = np.arange(P)
    cs = {"ident": np.eye(P), "group": p[:, None] // 32 == np.arange(4), "head": p[:, None] % 32 // 8 == np.arange(4),
          "later": np.arange(32)[None] > p[:, None] % 32,
          "rev": np.tile(24 - np.arange(24), (P, 1)), "upto": p[:, None] <= p[None], "ones": np.ones((P, P)),
          "mask4": p[:, None] == p[None] // 32,
          "multiples": np.tile(P * np.arange(32), (P, 1)), "spare": p[:, None] + P * np.arange(TILES),
          "block_no": np.tile(np.arange(MAX_BLOCKS), (P, 1)),
          "diag512": np.repeat(p[:, None] % 32 // 8 == np.arange(4), P, axis=1)}
    out["consts"] = np.concatenate([cs[n].astype(f) for n in CONSTS], axis=1)
    out["gate0"], out["gate0_b"] = a["L0_ffn_gate_w"], a["L0_ffn_gate_b"][None]
    out["gate2"], out["gate3"] = a["L2_ffn_Wr"], np.ascontiguousarray(a["L3_ffn_gate_w"].T)
    out["L0_w1"], out["L0_w2"], out["L0_b2"] = a["L0_ffn_w1"], a["L0_ffn_w2"], a["L0_ffn_b2"]
    out["L0_b1"] = np.ascontiguousarray(a["L0_ffn_b1"].reshape(24, 4, P).transpose(0, 2, 1))
    out["L2_w1"] = np.concatenate([a["L2_ffn_W1"], a["L2_ffn_fw1"][None]])
    out["L2_w2"] = np.concatenate([a["L2_ffn_W2"], a["L2_ffn_fw2"][None]])
    out["L2_b2"] = np.concatenate([a["L2_ffn_b2"], a["L2_ffn_fb2"][None]])
    out["L2_b1"] = np.ascontiguousarray(np.concatenate([a["L2_ffn_b1"], a["L2_ffn_fb1"][None]]).reshape(9, 4, P).transpose(0, 2, 1))
    out["L3_w1"], out["L3_w2"] = a["L3_ffn_expert_w1"], a["L3_ffn_expert_w2"]
    out["key_weights"] = a["fside_BxS2_0"]
    out["key_tokens"] = a["itok_BxS2_0_99"]
    out["mask"] = a["mask_1x1xSxS2_fk1"].reshape(S, KEYS)
    out["rel_emb"] = a["L1_attn_rel_emb"]
    n = np.maximum(np.arange(S)[None, :] - np.arange(S)[:, None], 0)
    large = 16 + (np.log(np.maximum(n, 1) / 16) / np.log(128 / 16) * 16).astype(int)
    bucket = np.where(n < 16, n, np.minimum(large, 31))
    hot = (np.arange(32)[:, None, None] == bucket[None]).astype(f)
    out["buckets"] = np.tile(hot[:, :, None, :], (1, 1, 4, 1)).reshape(32, S * P)
    out["W_exp"], out["b_exp"] = a["L1_ffn_W_exp"], a["L1_ffn_b_exp"][None]
    out["W_conT"] = np.ascontiguousarray(a["L1_ffn_W_con"].T)
    out["up_w"], out["down_w"] = a["L1_ffn_up_weights"].reshape(9, 1024), a["L1_ffn_down_weights"].reshape(9, 1024)
    out["L3_b1"] = np.zeros((8, P, 2), f)
    return out


def kernel(**inputs):
    import numpy as np
    import concourse.bacc as bacc
    from concourse.bass_utils import run_bass_kernel_spmd

    nc = bacc.Bacc("TRN2", target_bir_lowering=False, num_devices=1)
    arrays = layout(inputs)
    T = {}
    feed = {}
    for name, a in arrays.items():
        a = np.ascontiguousarray(a)
        feed[f"in_{name}"] = a
        T[name] = nc.dram_tensor(f"in_{name}", a.shape, mybir.dt.from_np(a.dtype), kind="ExternalInput").ap()
    for name in ("rows_x2", "rows_x3", "rows_keep"):
        T[name] = nc.dram_tensor(name, (NB, KEYS), F32).ap()
    T["pair_rows"] = nc.dram_tensor("pair_rows", ((MAX_BLOCKS + TILES) * P, P), F32).ap()
    T["pair_outs"] = nc.dram_tensor("pair_outs", (MAX_BLOCKS * P, P), F32).ap()
    out = nc.dram_tensor("out_0", (NB, S, P), F32, kind="ExternalOutput").ap()
    program(nc, T, out)
    r = run_bass_kernel_spmd(nc, [feed], core_ids=[0])
    return r.results[0]["out_0"]
```
